# Optimizing a Trainium2 kernel written in Bass

```python
import numpy as np
import jax
import jax.numpy as jnp

def _softmax(x, axis=-1):
    return jax.nn.softmax(x, axis=axis)

def _gelu(x):
    return jax.nn.gelu(x, approximate=True)

def _silu(x):
    return jax.nn.silu(x)

def _sigmoid(x):
    return jax.nn.sigmoid(x)

def _layernorm(x, axis=-1, eps=1e-05):
    m = jnp.mean(x, axis=axis, keepdims=True)
    v = jnp.var(x, axis=axis, keepdims=True)
    return (x - m) / jnp.sqrt(v + eps)

def _scatter_add(tgt, idx, src, axis=0):
    return tgt.at[idx].add(src)

def _segment_sum(src, seg, n):
    return jax.ops.segment_sum(src, seg, n)
kernel_name = 'mk_gnn_resnorm_d4_gnn_r32_3bca52'

def setup_inputs(seed: int=0):
    np.random.seed(seed)
    _w = jnp.asarray

    def _rec_inputs():
        import jax
        import jax.numpy as jnp
        _gk = jax.random.key(seed)
        x = -0.0003713 + 1 * jax.random.normal(jax.random.fold_in(_gk, 1), (3125, 128), jnp.float32)
        src = jax.random.randint(jax.random.fold_in(_gk, 2), (100000,), 0, 3125, jnp.int32)
        dst = jnp.minimum((3125 * jax.random.uniform(jax.random.fold_in(_gk, 3), (100000,)) ** 2.0).astype(jnp.int32), 99999)
        _o = jnp.argsort(dst, stable=True)
        src = src[_o]
        dst = dst[_o]
        edge_attr_16 = -1.02531e-05 + 0.999808 * jax.random.normal(jax.random.fold_in(_gk, 13), (100000, 16), jnp.float32)
        edge_attr_32 = -5.3897e-05 + 0.999841 * jax.random.normal(jax.random.fold_in(_gk, 14), (100000, 32), jnp.float32)
        edge_type_9 = jax.random.randint(jax.random.fold_in(_gk, 16), (100000,), 0, 9, jnp.int32)
        return (x, src, dst, edge_attr_16, edge_attr_32, edge_type_9)
    x, src, dst, edge_attr_16, edge_attr_32, edge_type_9 = _rec_inputs()

    def _L0_gnn_setup():
        import jax, jax.numpy as jnp
        import numpy as np
        N = 3125
        E = 50000
        D = 128

        def _sage_layer(x, src, dst, Wl, bl, Wr, num_nodes):
            msg = x[src]
            ssum = jax.ops.segment_sum(msg, dst, num_segments=num_nodes)
            deg = jax.ops.segment_sum(jnp.ones((src.shape[0], 1), x.dtype), dst, num_segments=num_nodes)
            agg = ssum / jnp.maximum(deg, 1.0)
            return agg @ Wl + bl + x @ Wr
        key = jax.random.key(seed)
        ks = jax.random.split(key, 8)
        s = 1.0 / np.sqrt(D)
        x = jax.random.normal(ks[0], (N, D), dtype=jnp.float32)
        Wl1 = jax.random.uniform(ks[1], (D, D), jnp.float32, -s, s)
        bl1 = jnp.zeros((D,), jnp.float32)
        Wr1 = jax.random.uniform(ks[2], (D, D), jnp.float32, -s, s)
        Wl2 = jax.random.uniform(ks[3], (D, D), jnp.float32, -s, s)
        bl2 = jnp.zeros((D,), jnp.float32)
        Wr2 = jax.random.uniform(ks[4], (D, D), jnp.float32, -s, s)
        edge_index = jax.random.randint(ks[5], (2, E), 0, N, dtype=jnp.int64)
        return {'x': x, 'Wl1': Wl1, 'bl1': bl1, 'Wr1': Wr1, 'Wl2': Wl2, 'bl2': bl2, 'Wr2': Wr2, 'edge_index': edge_index}
    _L0_gnn_all = _L0_gnn_setup()
    _L0_gnn_in = {k: v for k, v in _L0_gnn_all.items() if k in ('Wl1', 'bl1', 'Wr1', 'Wl2', 'bl2', 'Wr2')}
    del _L0_gnn_all

    def _L1_gnn_setup():
        import jax, jax.numpy as jnp
        import numpy as np
        NUM_EDGE_TYPES = 8
        HIDDEN = 128
        N_NODES = 50000
        N_EDGES = 18750

        def _gru_cell(x, h, W_ih, W_hh, b_ih, b_hh):
            H = h.shape[-1]
            gi = x @ W_ih.T + b_ih
            gh = h @ W_hh.T + b_hh
            i_r, i_z, i_n = (gi[:, :H], gi[:, H:2 * H], gi[:, 2 * H:])
            h_r, h_z, h_n = (gh[:, :H], gh[:, H:2 * H], gh[:, 2 * H:])
            r = jax.nn.sigmoid(i_r + h_r)
            z = jax.nn.sigmoid(i_z + h_z)
            n = jnp.tanh(i_n + r * h_n)
            return (1.0 - z) * n + z * h
        key = jax.random.key(seed)
        ks = jax.random.split(key, 10)
        H = HIDDEN
        h = jax.random.normal(ks[0], (N_NODES, H), dtype=jnp.float32)
        edge_index = jax.random.randint(ks[1], (2, N_EDGES), 0, N_NODES, dtype=jnp.int32)
        edge_type = jax.random.randint(ks[2], (N_EDGES,), 0, NUM_EDGE_TYPES + 1, dtype=jnp.int32)
        s = 1.0 / np.sqrt(H)
        W_msg = jax.random.uniform(ks[3], (H, H), jnp.float32, -s, s)
        b_msg = jax.random.uniform(ks[4], (H,), jnp.float32, -s, s)
        edge_embed = jax.random.normal(ks[5], (NUM_EDGE_TYPES + 1, H), dtype=jnp.float32)
        W_ih = jax.random.uniform(ks[6], (3 * H, H), jnp.float32, -s, s)
        W_hh = jax.random.uniform(ks[7], (3 * H, H), jnp.float32, -s, s)
        b_ih = jax.random.uniform(ks[8], (3 * H,), jnp.float32, -s, s)
        b_hh = jax.random.uniform(ks[9], (3 * H,), jnp.float32, -s, s)
        return {'h': h, 'edge_index': edge_index, 'edge_type': edge_type, 'num_nodes': N_NODES, 'W_msg': W_msg, 'b_msg': b_msg, 'edge_embed': edge_embed, 'W_ih': W_ih, 'W_hh': W_hh, 'b_ih': b_ih, 'b_hh': b_hh}
    _L1_gnn_all = _L1_gnn_setup()
    _L1_gnn_in = {k: v for k, v in _L1_gnn_all.items() if k in ('W_msg', 'b_msg', 'edge_embed', 'W_ih', 'W_hh', 'b_ih', 'b_hh')}
    del _L1_gnn_all

    def _L2_gnn_setup():
        import jax, jax.numpy as jnp
        import numpy as np
        NUM_LAYER = 3
        NUM_GRAPHS = 512
        EMB = 128
        EDGE_DIM = 16
        BN_EPS = 1e-05

        def _forward(input_feature, edge_attr, vn_emb, conv_edge_w, conv_edge_b, conv_w1, conv_b1, conv_w2, conv_b2, bn_gamma, bn_beta, vn_w1, vn_b1, vn_g1, vn_be1, vn_w2, vn_b2, vn_g2, vn_be2, edge_index, batch):
            N = input_feature.shape[0]
            src, dst = (edge_index[0], edge_index[1])
            inv = 1.0 / jnp.sqrt(jnp.asarray(1.0 + BN_EPS, input_feature.dtype))
            vn = jnp.broadcast_to(vn_emb, (NUM_GRAPHS, EMB))
            h = input_feature
            for l in range(NUM_LAYER):
                h_in = h + vn[batch]
                edge_emb = edge_attr @ conv_edge_w[l] + conv_edge_b[l]
                msg = jax.nn.relu(h_in[src] + edge_emb)
                agg = jax.ops.segment_sum(msg, dst, num_segments=N)
                z = h_in + agg
                z = jax.nn.relu(z @ conv_w1[l] + conv_b1[l]) @ conv_w2[l] + conv_b2[l]
                z = z * (bn_gamma[l] * inv) + bn_beta[l]
                if l < NUM_LAYER - 1:
                    z = jax.nn.relu(z)
                z = z + h_in
                if l < NUM_LAYER - 1:
                    vt = jax.ops.segment_sum(h_in, batch, num_segments=NUM_GRAPHS) + vn
                    m = jax.nn.relu((vt @ vn_w1[l] + vn_b1[l]) * (vn_g1[l] * inv) + vn_be1[l])
                    m = jax.nn.relu((m @ vn_w2[l] + vn_b2[l]) * (vn_g2[l] * inv) + vn_be2[l])
                    vn = vn + m
                h = z
            return h
        key = jax.random.key(seed)
        ks = jax.random.split(key, 24)
        N, E = (3125, 18750)
        s = 0.02
        inp = {'input_feature': jax.random.normal(ks[0], (N, EMB), jnp.float32), 'edge_attr': jax.random.normal(ks[1], (E, EDGE_DIM), jnp.float32), 'edge_index': jax.random.randint(ks[2], (2, E), 0, N, jnp.int64), 'batch': jnp.sort(jax.random.randint(ks[3], (N,), 0, NUM_GRAPHS, jnp.int64)), 'vn_emb': jnp.zeros((1, EMB), jnp.float32), 'conv_edge_w': s * jax.random.normal(ks[4], (NUM_LAYER, EDGE_DIM, EMB), jnp.float32), 'conv_edge_b': jnp.zeros((NUM_LAYER, EMB), jnp.float32), 'conv_w1': s * jax.random.normal(ks[5], (NUM_LAYER, EMB, 2 * EMB), jnp.float32), 'conv_b1': jnp.zeros((NUM_LAYER, 2 * EMB), jnp.float32), 'conv_w2': s * jax.random.normal(ks[6], (NUM_LAYER, 2 * EMB, EMB), jnp.float32), 'conv_b2': jnp.zeros((NUM_LAYER, EMB), jnp.float32), 'bn_gamma': 1.0 + s * jax.random.normal(ks[7], (NUM_LAYER, EMB), jnp.float32), 'bn_beta': s * jax.random.normal(ks[8], (NUM_LAYER, EMB), jnp.float32), 'vn_w1': s * jax.random.normal(ks[9], (NUM_LAYER - 1, EMB, 2 * EMB), jnp.float32), 'vn_b1': jnp.zeros((NUM_LAYER - 1, 2 * EMB), jnp.float32), 'vn_g1': jnp.ones((NUM_LAYER - 1, 2 * EMB), jnp.float32), 'vn_be1': jnp.zeros((NUM_LAYER - 1, 2 * EMB), jnp.float32), 'vn_w2': s * jax.random.normal(ks[10], (NUM_LAYER - 1, 2 * EMB, EMB), jnp.float32), 'vn_b2': jnp.zeros((NUM_LAYER - 1, EMB), jnp.float32), 'vn_g2': jnp.ones((NUM_LAYER - 1, EMB), jnp.float32), 'vn_be2': jnp.zeros((NUM_LAYER - 1, EMB), jnp.float32)}
        return inp
    _L2_gnn_all = _L2_gnn_setup()
    _L2_gnn_in = {k: v for k, v in _L2_gnn_all.items() if k in ('vn_emb', 'conv_edge_w', 'conv_edge_b', 'conv_w1', 'conv_b1', 'conv_w2', 'conv_b2', 'bn_gamma', 'bn_beta', 'vn_w1', 'vn_b1', 'vn_g1', 'vn_be1', 'vn_w2', 'vn_b2', 'vn_g2', 'vn_be2')}
    del _L2_gnn_all

    def _L3_gnn_setup():
        import jax, jax.numpy as jnp
        import numpy as np
        N, E = (50000, 25000)
        IN, HID, H, ED = (128, 128, 4, 32)

        def _gatv2(x, src, dst, ea, Wl, bl, Wr, br, We, att, b, concat):
            n = x.shape[0]
            h, c = att.shape
            xl = (x @ Wl + bl).reshape(n, h, c)
            xr = (x @ Wr + br).reshape(n, h, c)
            e = (ea @ We).reshape(-1, h, c)
            m = xl[src] + xr[dst] + e
            m = jnp.where(m > 0, m, 0.2 * m)
            s = jnp.einsum('ehc,hc->eh', m, att)
            smax = jax.ops.segment_max(s, dst, num_segments=n)
            ex = jnp.exp(s - smax[dst])
            den = jax.ops.segment_sum(ex, dst, num_segments=n)
            alpha = ex / den[dst]
            out = jax.ops.segment_sum(xl[src] * alpha[:, :, None], dst, num_segments=n)
            out = out.reshape(n, h * c) if concat else out.mean(axis=1)
            return out + b

        def _ln(x, g, b):
            mu = x.mean(-1, keepdims=True)
            v = ((x - mu) ** 2).mean(-1, keepdims=True)
            return (x - mu) / jnp.sqrt(v + 1e-05) * g + b
        key = jax.random.key(seed)
        ks = jax.random.split(key, 24)
        p = lambda i, shape: jax.random.normal(ks[i], shape, dtype=jnp.float32) * 0.1
        inp = {'x': jax.random.normal(ks[0], (N, IN), dtype=jnp.float32), 'edge_attr': jax.random.normal(ks[1], (E, ED), dtype=jnp.float32), 'src': jax.random.randint(ks[2], (E,), 0, N), 'dst': jax.random.randint(ks[3], (E,), 0, N)}
        k = 4
        dims = [(IN, H, HID // H), (HID, H, HID // H), (HID, 1, HID)]
        for l, (din, h, c) in enumerate(dims):
            inp[f'Wl{l}'] = p(k, (din, h * c))
            k += 1
            inp[f'bl{l}'] = jnp.zeros((h * c,), jnp.float32)
            inp[f'Wr{l}'] = p(k, (din, h * c))
            k += 1
            inp[f'br{l}'] = jnp.zeros((h * c,), jnp.float32)
            inp[f'We{l}'] = p(k, (ED, h * c))
            k += 1
            inp[f'att{l}'] = p(k, (h, c))
            k += 1
            inp[f'b{l}'] = jnp.zeros((HID,), jnp.float32)
            inp[f'g{l}'] = jnp.ones((HID,), jnp.float32)
            inp[f'be{l}'] = jnp.zeros((HID,), jnp.float32)
        return inp
    _L3_gnn_all = _L3_gnn_setup()
    _L3_gnn_in = {k: v for k, v in _L3_gnn_all.items() if k in ('Wl0', 'bl0', 'Wr0', 'br0', 'We0', 'att0', 'b0', 'g0', 'be0', 'Wl1', 'bl1', 'Wr1', 'br1', 'We1', 'att1', 'b1', 'g1', 'be1', 'Wl2', 'bl2', 'Wr2', 'br2', 'We2', 'att2', 'b2', 'g2', 'be2')}
    del _L3_gnn_all
    return {'x': x, 'src': src, 'dst': dst, 'edge_attr_16': edge_attr_16, 'edge_attr_32': edge_attr_32, 'edge_type_9': edge_type_9, 'L0_gnn_Wl1': _L0_gnn_in['Wl1'], 'L0_gnn_bl1': _L0_gnn_in['bl1'], 'L0_gnn_Wr1': _L0_gnn_in['Wr1'], 'L0_gnn_Wl2': _L0_gnn_in['Wl2'], 'L0_gnn_bl2': _L0_gnn_in['bl2'], 'L0_gnn_Wr2': _L0_gnn_in['Wr2'], 'L1_gnn_W_msg': _L1_gnn_in['W_msg'], 'L1_gnn_b_msg': _L1_gnn_in['b_msg'], 'L1_gnn_edge_embed': _L1_gnn_in['edge_embed'], 'L1_gnn_W_ih': _L1_gnn_in['W_ih'], 'L1_gnn_W_hh': _L1_gnn_in['W_hh'], 'L1_gnn_b_ih': _L1_gnn_in['b_ih'], 'L1_gnn_b_hh': _L1_gnn_in['b_hh'], 'L2_gnn_vn_emb': _L2_gnn_in['vn_emb'], 'L2_gnn_conv_edge_w': _L2_gnn_in['conv_edge_w'], 'L2_gnn_conv_edge_b': _L2_gnn_in['conv_edge_b'], 'L2_gnn_conv_w1': _L2_gnn_in['conv_w1'], 'L2_gnn_conv_b1': _L2_gnn_in['conv_b1'], 'L2_gnn_conv_w2': _L2_gnn_in['conv_w2'], 'L2_gnn_conv_b2': _L2_gnn_in['conv_b2'], 'L2_gnn_bn_gamma': _L2_gnn_in['bn_gamma'], 'L2_gnn_bn_beta': _L2_gnn_in['bn_beta'], 'L2_gnn_vn_w1': _L2_gnn_in['vn_w1'], 'L2_gnn_vn_b1': _L2_gnn_in['vn_b1'], 'L2_gnn_vn_g1': _L2_gnn_in['vn_g1'], 'L2_gnn_vn_be1': _L2_gnn_in['vn_be1'], 'L2_gnn_vn_w2': _L2_gnn_in['vn_w2'], 'L2_gnn_vn_b2': _L2_gnn_in['vn_b2'], 'L2_gnn_vn_g2': _L2_gnn_in['vn_g2'], 'L2_gnn_vn_be2': _L2_gnn_in['vn_be2'], 'L3_gnn_Wl0': _L3_gnn_in['Wl0'], 'L3_gnn_bl0': _L3_gnn_in['bl0'], 'L3_gnn_Wr0': _L3_gnn_in['Wr0'], 'L3_gnn_br0': _L3_gnn_in['br0'], 'L3_gnn_We0': _L3_gnn_in['We0'], 'L3_gnn_att0': _L3_gnn_in['att0'], 'L3_gnn_b0': _L3_gnn_in['b0'], 'L3_gnn_g0': _L3_gnn_in['g0'], 'L3_gnn_be0': _L3_gnn_in['be0'], 'L3_gnn_Wl1': _L3_gnn_in['Wl1'], 'L3_gnn_bl1': _L3_gnn_in['bl1'], 'L3_gnn_Wr1': _L3_gnn_in['Wr1'], 'L3_gnn_br1': _L3_gnn_in['br1'], 'L3_gnn_We1': _L3_gnn_in['We1'], 'L3_gnn_att1': _L3_gnn_in['att1'], 'L3_gnn_b1': _L3_gnn_in['b1'], 'L3_gnn_g1': _L3_gnn_in['g1'], 'L3_gnn_be1': _L3_gnn_in['be1'], 'L3_gnn_Wl2': _L3_gnn_in['Wl2'], 'L3_gnn_bl2': _L3_gnn_in['bl2'], 'L3_gnn_Wr2': _L3_gnn_in['Wr2'], 'L3_gnn_br2': _L3_gnn_in['br2'], 'L3_gnn_We2': _L3_gnn_in['We2'], 'L3_gnn_att2': _L3_gnn_in['att2'], 'L3_gnn_b2': _L3_gnn_in['b2'], 'L3_gnn_g2': _L3_gnn_in['g2'], 'L3_gnn_be2': _L3_gnn_in['be2']}

def reference(x, src, dst, edge_attr_16, edge_attr_32, edge_type_9, L0_gnn_Wl1, L0_gnn_bl1, L0_gnn_Wr1, L0_gnn_Wl2, L0_gnn_bl2, L0_gnn_Wr2, L1_gnn_W_msg, L1_gnn_b_msg, L1_gnn_edge_embed, L1_gnn_W_ih, L1_gnn_W_hh, L1_gnn_b_ih, L1_gnn_b_hh, L2_gnn_vn_emb, L2_gnn_conv_edge_w, L2_gnn_conv_edge_b, L2_gnn_conv_w1, L2_gnn_conv_b1, L2_gnn_conv_w2, L2_gnn_conv_b2, L2_gnn_bn_gamma, L2_gnn_bn_beta, L2_gnn_vn_w1, L2_gnn_vn_b1, L2_gnn_vn_g1, L2_gnn_vn_be1, L2_gnn_vn_w2, L2_gnn_vn_b2, L2_gnn_vn_g2, L2_gnn_vn_be2, L3_gnn_Wl0, L3_gnn_bl0, L3_gnn_Wr0, L3_gnn_br0, L3_gnn_We0, L3_gnn_att0, L3_gnn_b0, L3_gnn_g0, L3_gnn_be0, L3_gnn_Wl1, L3_gnn_bl1, L3_gnn_Wr1, L3_gnn_br1, L3_gnn_We1, L3_gnn_att1, L3_gnn_b1, L3_gnn_g1, L3_gnn_be1, L3_gnn_Wl2, L3_gnn_bl2, L3_gnn_Wr2, L3_gnn_br2, L3_gnn_We2, L3_gnn_att2, L3_gnn_b2, L3_gnn_g2, L3_gnn_be2):
    import jax
    import jax.numpy as jnp

    def _L0_gnn_ref(x, Wl1, bl1, Wr1, Wl2, bl2, Wr2, edge_index):
        import jax, jax.numpy as jnp
        import numpy as np
        N = 3125
        E = 50000
        D = 128

        def _sage_layer(x, src, dst, Wl, bl, Wr, num_nodes):
            msg = x[src]
            ssum = jax.ops.segment_sum(msg, dst, num_segments=num_nodes)
            deg = jax.ops.segment_sum(jnp.ones((src.shape[0], 1), x.dtype), dst, num_segments=num_nodes)
            agg = ssum / jnp.maximum(deg, 1.0)
            return agg @ Wl + bl + x @ Wr
        src, dst = (edge_index[0], edge_index[1])
        n = x.shape[0]
        h = jax.nn.relu(_sage_layer(x, src, dst, Wl1, bl1, Wr1, n))
        h = jax.nn.relu(_sage_layer(h, src, dst, Wl2, bl2, Wr2, n))
        return h

    def _L1_gnn_ref(h, edge_index, edge_type, num_nodes, W_msg, b_msg, edge_embed, W_ih, W_hh, b_ih, b_hh):
        import jax, jax.numpy as jnp
        import numpy as np
        NUM_EDGE_TYPES = 8
        HIDDEN = 128
        N_NODES = 50000
        N_EDGES = 18750

        def _gru_cell(x, h, W_ih, W_hh, b_ih, b_hh):
            H = h.shape[-1]
            gi = x @ W_ih.T + b_ih
            gh = h @ W_hh.T + b_hh
            i_r, i_z, i_n = (gi[:, :H], gi[:, H:2 * H], gi[:, 2 * H:])
            h_r, h_z, h_n = (gh[:, :H], gh[:, H:2 * H], gh[:, 2 * H:])
            r = jax.nn.sigmoid(i_r + h_r)
            z = jax.nn.sigmoid(i_z + h_z)
            n = jnp.tanh(i_n + r * h_n)
            return (1.0 - z) * n + z * h
        src = edge_index[0]
        dst = edge_index[1]
        src_h = h[src] @ W_msg.T + b_msg
        emb = edge_embed[jnp.clip(edge_type, 0, NUM_EDGE_TYPES)]
        msg = src_h + emb
        messages = jax.ops.segment_sum(msg, dst, num_segments=num_nodes)
        h_new = _gru_cell(messages, h[:num_nodes], W_ih, W_hh, b_ih, b_hh)
        result = jnp.zeros_like(h).at[:num_nodes].set(h_new)
        return result

    def _L2_gnn_ref(input_feature, edge_index, edge_attr, batch, vn_emb, conv_edge_w, conv_edge_b, conv_w1, conv_b1, conv_w2, conv_b2, bn_gamma, bn_beta, vn_w1, vn_b1, vn_g1, vn_be1, vn_w2, vn_b2, vn_g2, vn_be2):
        import jax, jax.numpy as jnp
        import numpy as np
        NUM_LAYER = 3
        NUM_GRAPHS = 512
        EMB = 128
        EDGE_DIM = 16
        BN_EPS = 1e-05

        def _forward(input_feature, edge_attr, vn_emb, conv_edge_w, conv_edge_b, conv_w1, conv_b1, conv_w2, conv_b2, bn_gamma, bn_beta, vn_w1, vn_b1, vn_g1, vn_be1, vn_w2, vn_b2, vn_g2, vn_be2, edge_index, batch):
            N = input_feature.shape[0]
            src, dst = (edge_index[0], edge_index[1])
            inv = 1.0 / jnp.sqrt(jnp.asarray(1.0 + BN_EPS, input_feature.dtype))
            vn = jnp.broadcast_to(vn_emb, (NUM_GRAPHS, EMB))
            h = input_feature
            for l in range(NUM_LAYER):
                h_in = h + vn[batch]
                edge_emb = edge_attr @ conv_edge_w[l] + conv_edge_b[l]
                msg = jax.nn.relu(h_in[src] + edge_emb)
                agg = jax.ops.segment_sum(msg, dst, num_segments=N)
                z = h_in + agg
                z = jax.nn.relu(z @ conv_w1[l] + conv_b1[l]) @ conv_w2[l] + conv_b2[l]
                z = z * (bn_gamma[l] * inv) + bn_beta[l]
                if l < NUM_LAYER - 1:
                    z = jax.nn.relu(z)
                z = z + h_in
                if l < NUM_LAYER - 1:
                    vt = jax.ops.segment_sum(h_in, batch, num_segments=NUM_GRAPHS) + vn
                    m = jax.nn.relu((vt @ vn_w1[l] + vn_b1[l]) * (vn_g1[l] * inv) + vn_be1[l])
                    m = jax.nn.relu((m @ vn_w2[l] + vn_b2[l]) * (vn_g2[l] * inv) + vn_be2[l])
                    vn = vn + m
                h = z
            return h
        return _forward(input_feature, edge_attr, vn_emb, conv_edge_w, conv_edge_b, conv_w1, conv_b1, conv_w2, conv_b2, bn_gamma, bn_beta, vn_w1, vn_b1, vn_g1, vn_be1, vn_w2, vn_b2, vn_g2, vn_be2, edge_index, batch)

    def _L3_gnn_ref(x, edge_attr, src, dst, Wl0, bl0, Wr0, br0, We0, att0, b0, g0, be0, Wl1, bl1, Wr1, br1, We1, att1, b1, g1, be1, Wl2, bl2, Wr2, br2, We2, att2, b2, g2, be2):
        import jax, jax.numpy as jnp
        import numpy as np
        N, E = (50000, 25000)
        IN, HID, H, ED = (128, 128, 4, 32)

        def _gatv2(x, src, dst, ea, Wl, bl, Wr, br, We, att, b, concat):
            n = x.shape[0]
            h, c = att.shape
            xl = (x @ Wl + bl).reshape(n, h, c)
            xr = (x @ Wr + br).reshape(n, h, c)
            e = (ea @ We).reshape(-1, h, c)
            m = xl[src] + xr[dst] + e
            m = jnp.where(m > 0, m, 0.2 * m)
            s = jnp.einsum('ehc,hc->eh', m, att)
            smax = jax.ops.segment_max(s, dst, num_segments=n)
            ex = jnp.exp(s - smax[dst])
            den = jax.ops.segment_sum(ex, dst, num_segments=n)
            alpha = ex / den[dst]
            out = jax.ops.segment_sum(xl[src] * alpha[:, :, None], dst, num_segments=n)
            out = out.reshape(n, h * c) if concat else out.mean(axis=1)
            return out + b

        def _ln(x, g, b):
            mu = x.mean(-1, keepdims=True)
            v = ((x - mu) ** 2).mean(-1, keepdims=True)
            return (x - mu) / jnp.sqrt(v + 1e-05) * g + b
        h = _gatv2(x, src, dst, edge_attr, Wl0, bl0, Wr0, br0, We0, att0, b0, True)
        h = jax.nn.relu(_ln(h, g0, be0))
        h = _gatv2(h, src, dst, edge_attr, Wl1, bl1, Wr1, br1, We1, att1, b1, True)
        h = jax.nn.relu(_ln(h, g1, be1))
        h = _gatv2(h, src, dst, edge_attr, Wl2, bl2, Wr2, br2, We2, att2, b2, False)
        h = jax.nn.relu(_ln(h, g2, be2))
        return h
    edge_index = jnp.stack([src, dst])
    batch0 = jnp.zeros((3125,), jnp.int32)
    x = _layernorm(x + _L0_gnn_ref(x, L0_gnn_Wl1, L0_gnn_bl1, L0_gnn_Wr1, L0_gnn_Wl2, L0_gnn_bl2, L0_gnn_Wr2, edge_index), axis=-1)
    x = _layernorm(x + _L1_gnn_ref(x, edge_index, edge_type_9, 3125, L1_gnn_W_msg, L1_gnn_b_msg, L1_gnn_edge_embed, L1_gnn_W_ih, L1_gnn_W_hh, L1_gnn_b_ih, L1_gnn_b_hh), axis=-1)
    x = _layernorm(x + _L2_gnn_ref(x, edge_index, edge_attr_16, batch0, L2_gnn_vn_emb, L2_gnn_conv_edge_w, L2_gnn_conv_edge_b, L2_gnn_conv_w1, L2_gnn_conv_b1, L2_gnn_conv_w2, L2_gnn_conv_b2, L2_gnn_bn_gamma, L2_gnn_bn_beta, L2_gnn_vn_w1, L2_gnn_vn_b1, L2_gnn_vn_g1, L2_gnn_vn_be1, L2_gnn_vn_w2, L2_gnn_vn_b2, L2_gnn_vn_g2, L2_gnn_vn_be2), axis=-1)
    x = _layernorm(x + _L3_gnn_ref(x, edge_attr_32, src, dst, L3_gnn_Wl0, L3_gnn_bl0, L3_gnn_Wr0, L3_gnn_br0, L3_gnn_We0, L3_gnn_att0, L3_gnn_b0, L3_gnn_g0, L3_gnn_be0, L3_gnn_Wl1, L3_gnn_bl1, L3_gnn_Wr1, L3_gnn_br1, L3_gnn_We1, L3_gnn_att1, L3_gnn_b1, L3_gnn_g1, L3_gnn_be1, L3_gnn_Wl2, L3_gnn_bl2, L3_gnn_Wr2, L3_gnn_br2, L3_gnn_We2, L3_gnn_att2, L3_gnn_b2, L3_gnn_g2, L3_gnn_be2), axis=-1)
    return x

_drawn_inputs = setup_inputs


def setup_inputs(seed=0):
    import zlib

    import numpy as np

    out = dict(_drawn_inputs(seed))
    spreads = {'L0_gnn_bl1': (0.0, 0.1),
     'L0_gnn_bl2': (0.0, 0.1),
     'L2_gnn_vn_emb': (0.0, 0.1),
     'L2_gnn_conv_edge_b': (0.0, 0.8),
     'L2_gnn_conv_b1': (0.0, 0.8),
     'L2_gnn_conv_b2': (0.0, 0.8),
     'L2_gnn_vn_b1': (0.0, 0.8),
     'L2_gnn_vn_g1': (1.0, 0.2),
     'L2_gnn_vn_be1': (0.0, 0.8),
     'L2_gnn_vn_b2': (0.0, 0.8),
     'L2_gnn_vn_g2': (1.0, 0.2),
     'L2_gnn_vn_be2': (0.0, 0.8),
     'L3_gnn_bl0': (0.0, 0.1),
     'L3_gnn_br0': (0.0, 0.8),
     'L3_gnn_b0': (0.0, 0.1),
     'L3_gnn_g0': (1.0, 0.2),
     'L3_gnn_be0': (0.0, 0.1),
     'L3_gnn_bl1': (0.0, 0.1),
     'L3_gnn_br1': (0.0, 0.8),
     'L3_gnn_b1': (0.0, 0.1),
     'L3_gnn_g1': (1.0, 0.2),
     'L3_gnn_be1': (0.0, 0.1),
     'L3_gnn_bl2': (0.0, 0.1),
     'L3_gnn_br2': (0.0, 0.8),
     'L3_gnn_b2': (0.0, 0.1),
     'L3_gnn_g2': (1.0, 0.2),
     'L3_gnn_be2': (0.0, 0.1)}
    factors = {'edge_attr_16': 8.0,
     'edge_attr_32': 8.0,
     'L0_gnn_Wl1': 7.079,
     'L1_gnn_W_hh': 4.349,
     'L1_gnn_b_ih': 5.68,
     'L1_gnn_b_hh': 7.105,
     'L2_gnn_conv_edge_w': 8.0,
     'L2_gnn_bn_gamma': 2.925,
     'L2_gnn_bn_beta': 8.0,
     'L3_gnn_Wr0': 8.0,
     'L3_gnn_We0': 8.0,
     'L3_gnn_att0': 6.815,
     'L3_gnn_Wr1': 8.0,
     'L3_gnn_We1': 8.0,
     'L3_gnn_att1': 8.0,
     'L3_gnn_Wr2': 8.0,
     'L3_gnn_We2': 8.0,
     'L3_gnn_att2': 8.0}
    for name, (base, spread) in spreads.items():
        noise = np.random.default_rng([zlib.crc32(name.encode()), seed]).standard_normal(out[name].shape)
        drawn = base * np.exp(spread * noise) if base else spread * noise
        out[name] = jnp.asarray(drawn.astype(out[name].dtype))
    for name, factor in factors.items():
        out[name] = (out[name] * factor).astype(out[name].dtype)
    return out
```

```python
import concourse.bass as bass
from concourse import mybir
from contextlib import ExitStack

F32, I32 = mybir.dt.float32, mybir.dt.int32
ALU, ACT, AX = mybir.AluOpType, mybir.ActivationFunctionType, mybir.AxisListType

P = 128
D = 128
N, E = 3125, 100000
TILES = -(-N // P)
NP = TILES * P
CH = 4
GE = CH * P
GROUPS = -(-E // GE)
CHUNKS = GROUPS * CH
EP = GROUPS * GE
STEPS = GROUPS + TILES - 1
RING = 4
NSP = STEPS + 4
TYPES = 9
CROWS = 112
BIG = 1e30
EPS = 1e-5
INV = (1.0 + EPS) ** -0.5
COLS = [(a, min(512, NP - a)) for a in range(0, NP, 512)]
assert STEPS % RING == 0 and CHUNKS % CROWS == 0

VEC_COLS = ["L2_gnn_vn_emb", "L2_gnn_conv_b1", "L2_gnn_conv_b2", "L2_gnn_bn_gamma", "L2_gnn_bn_beta", "L2_gnn_vn_b1",
            "L2_gnn_vn_g1", "L2_gnn_vn_be1", "L2_gnn_vn_b2", "L2_gnn_vn_g2", "L2_gnn_vn_be2"]
VEC_ROWS = (["L0_gnn_bl1", "L0_gnn_bl2", "L1_gnn_b_ih", "L1_gnn_b_hh"]
            + [f"L3_gnn_{v}{l}" for l in range(3) for v in ("bl", "br", "att", "b", "g", "be")])


def stages():
    yield from [("pool", "constants"), ("dve", "step tables 1"), ("pe", "sum of tile ends"), ("dve", "step tables 2"),
                ("sp", "store penalties"), ("pe", "transpose x"), ("act", "x transposed")]
    for l in (1, 2):
        yield ("dve", f"sage {l} edges")
        if l == 1:
            yield from [("pe", "degrees"), ("dve", "one over degree")]
        yield from [("pe", f"sage {l} neighbours"), ("dve", f"sage {l} mean"), ("pe", f"sage {l} self"),
                    ("dve", f"sage {l} add"), ("act", f"sage {l} relu")]
        if l == 2:
            yield ("dve", "sage norm a")
            yield ("act", "sage norm root")
            yield ("dve", "sage norm b")
        yield from [("sp", f"sage {l} table"), ("pe", f"sage {l} transpose"), ("act", f"sage {l} transposed")]
    yield from [("dve", "gru edges"), ("pe", "gru messages"), ("act", "gru messages out"),
                ("pe", "gru r"), ("dve", "gru r bias"), ("act", "gru r gate"),
                ("pe", "gru hn"), ("dve", "gru hn gated"), ("pe", "gru in"), ("dve", "gru in add"), ("act", "gru n"),
                ("pe", "gru z"), ("dve", "gru z bias"), ("act", "gru z gate"), ("dve", "gru norm a"),
                ("act", "gru norm root"), ("dve", "gru norm b"), ("pe", "gru transpose"), ("dve", "gru transposed")]
    for l in range(3):
        yield from [("pe", f"gin {l} rows"), ("act", f"gin {l} rows out"), ("sp", f"gin {l} table"),
                    ("dve", f"gin {l} edges"), ("pe", f"gin {l} up 0"), ("act", f"gin {l} up 0 out"),
                    ("pe", f"gin {l} up 1"), ("act", f"gin {l} up 1 out"), ("pe", f"gin {l} down"),
                    ("act", f"gin {l} down out")]
        if l < 2:
            yield from [("pe", f"gin {l} virtual up"), ("act", f"gin {l} virtual up out"),
                        ("pe", f"gin {l} virtual down"), ("act", f"gin {l} virtual down out")]
        yield ("dve", f"gin {l} residual")
    yield from [("pe", "gin transpose"), ("dve", "gin norm a"), ("act", "gin norm root"), ("dve", "gin norm b")]
    for l in range(3):
        yield from [("pe", f"gat {l} transpose"), ("act", f"gat {l} transposed"), ("pe", f"gat {l} left"),
                    ("dve", f"gat {l} left out"), ("sp", f"gat {l} table"), ("pe", f"gat {l} right"),
                    ("dve", f"gat {l} right out"), ("dve", f"gat {l} edges"), ("dve", f"gat {l} norm a"),
                    ("act", f"gat {l} norm root"), ("dve", f"gat {l} norm b"), ("act", f"gat {l} relu")]
    yield from [("dve", "last norm a"), ("act", "last norm root"), ("dve", "last norm b"), ("sp", "store output")]


ORDER = list(stages())
AT = {name: k for k, (_, name) in enumerate(ORDER)}


def build(nc, a, out):
    ctx = ExitStack()
    with ctx:
        def sb(name, shape, dt=F32):
            return ctx.enter_context(nc.sbuf_tensor(name, shape, dt))

        def sem(name):
            return ctx.enter_context(nc.semaphore(name))

        res = sb("res", [P, NP])
        ht = sb("ht", [P, NP])
        agg = sb("agg", [P, NSP * 16])
        hr = sb("hr", [P, NP])
        w1 = sb("w1", [P, NP])
        w2 = sb("w2", [P, NP])
        xr = sb("xr", [P, NP])
        cnt = xr[0:TYPES + 1, :]
        rdeg = sb("rdeg", [P, TILES])
        st = sb("st", [P, 4, TILES])
        rden = sb("rden", [P, TILES, 4])
        mx = sb("mx", [P, TILES * 4])

        ident = sb("ident", [P, P])
        iota_d = sb("iota_d", [P, P])
        iota_t = sb("iota_t", [P, TYPES])
        iota_s = sb("iota_s", [P, NSP])
        pcol = sb("pcol", [P, 3])
        ones = sb("ones", [P, P])
        selcnt = sb("selcnt", [TYPES + 1, 1])
        ends = sb("ends", [P, GROUPS])
        endi = sb("endi", [TILES - 1, GROUPS], I32)
        gl = sb("gl", [P, 1])
        past = sb("past", [P, NSP])
        tstep = sb("tstep", [P, NSP])
        gstep = sb("gstep", [P, NSP])
        tile_i = sb("tile_i", [1, NSP], I32)
        group_i = sb("group_i", [1, NSP], I32)
        idx_in = xr[:, 0:4 * CHUNKS].bitcast(I32).rearrange("p (k c) -> p k c", k=4)
        packed = w1[:, 0:GROUPS * 16]
        fields = agg
        fview = fields[:, :].rearrange("p (s f c) -> p s f c", f=4, c=CH)
        src_i = sb("src_i", [P, NSP * CH], I32)
        dloc = sb("dloc", [P, NSP * CH])
        last = sb("last", [P, NSP * CH])
        etype = sb("etype", [P, NSP * CH])
        RW = CHUNKS // CROWS * P
        rows_i = hr[0:CROWS, 0:RW].bitcast(I32)
        rows_f = w2[0:CROWS, 0:RW]
        pen = w2[0:CROWS, RW:2 * RW]

        G = [sb(f"G{i}", [P, CH * D]) for i in range(RING)]
        OH = [sb(f"OH{i}", [P, CH * P]) for i in range(RING)]
        OHT = [sb(f"OHT{i}", [P, CH * P]) for i in range(RING)]
        TOH = [sb(f"TOH{i}", [P, CH, TYPES + 1]) for i in range(2)]
        ea = [sb(f"ea{i}", [32, GE]) for i in range(RING)]
        ea1 = [x[0:17, :] for x in ea]
        pn = [sb(f"pn{i}", [16, P]) for i in range(RING)]
        WT = [sb(f"WT{i}", [P, CH * 132]) for i in range(2)]
        idx8 = [sb(f"idx8{i}", [P, 2 * CH], I32) for i in range(2)]
        msg = sb("msg", [P, CH * D])
        lk = sb("lk", [P, CH * D])
        score = [sb(f"score{i}", [P, 16]) for i in range(2)]
        scanned = sb("scanned", [16, P])
        segrhs = sb("segrhs", [P, CH * 5])
        spen = sb("spen", [P, CH])
        sval = sb("sval", [P, 16])
        smx = sb("smx", [P, 4])
        mnew = [sb(f"mnew{i}", [P, 4]) for i in range(2)]
        mdif = [sb(f"mdif{i}", [P, 4]) for i in range(2)]
        scl = [sb(f"scl{i}", [P, 4]) for i in range(2)]
        delta = sb("delta", [P, 16])
        vn = sb("vn", [P, 1])
        vsum = sb("vsum", [P, 1])
        vt = sb("vt", [P, 1])
        vm = sb("vm", [P, 2])
        vs1, vb1 = sb("vs1", [P, 4]), sb("vb1", [P, 4])
        vs2, vb2 = sb("vs2", [P, 2]), sb("vb2", [P, 2])
        bnv = sb("bnv", [P, 6])

        W = {}
        loads = []
        for k in ("L0_gnn_Wl1", "L0_gnn_Wr1", "L0_gnn_Wl2", "L0_gnn_Wr2", "L1_gnn_W_msg", "L1_gnn_W_ih", "L1_gnn_W_hh",
                  "L1_aug", "L2_conv_edge", "L2_gnn_conv_w1", "L2_gnn_conv_w2", "L2_gnn_vn_w1", "L2_gnn_vn_w2",
                  *[f"L3_gnn_{v}{l}" for l in range(3) for v in ("Wl", "Wr", "We")], *[f"col_{v}" for v in VEC_COLS]):
            W[k] = sb("w_" + k, list(a[k].shape))
            loads.append((W[k][:, :], a[k]))
        for k in VEC_ROWS:
            n = a[k].shape[1]
            W[k] = sb("r_" + k, [P, n])
            loads.append((W[k][:, :], a[k].to_broadcast([P, n])))

        ps = ctx.enter_context(nc.psum_tensor("ps", [P, 4096], F32))

        def bank(i, n=512, p=P):
            return ps[0:p, 512 * i:512 * i + n]

        table = nc.dram_tensor("node_table", (NP, D), F32, kind="Internal").ap()
        pen_rows = nc.dram_tensor("penalty_rows", (CHUNKS, P), F32, kind="Internal").ap()

        turn = sem("turn")
        loaded = sem("loaded")
        stored = sem("stored")
        dlink = sem("dlink")
        alink = sem("alink")
        plink = sem("plink")
        fcopy = sem("fcopy")
        n_loads = len(loads) + 7

        def sems(name, *kinds):
            d = {k: sem(f"{name}_{k}") for k in kinds}
            d["gathered"] = [sem(f"{name}_gathered{q}") for q in range(RING)]
            return d

        SUM = {p: sems(p, "onehot", "scattered", "added") for p in ("s1", "s2", "gr")}
        GIN = []
        for l in range(3):
            d = sems(f"gin{l}", "onehot", "scattered", "added", "projected", "summed", "rectified")
            d["edge_data"] = [sem(f"gin{l}_edge_data{q}") for q in range(RING)]
            GIN.append(d)
        GAT = []
        for l in range(3):
            d = sems(f"gat{l}", "onehot", "turned", "onehot_t", "projected", "score", "score_t", "scanned", "scan_back",
                     "seg_rhs", "seg_max", "new_max", "scale", "max_of_edge", "delta", "weight", "weighted",
                     "scattered", "added", "slink")
            d["edge_data"] = [sem(f"gat{l}_edge_data{q}") for q in range(RING)]
            GAT.append(d)
        ALL = [SUM["s1"], SUM["s2"], SUM["gr"], *GIN, *GAT]
        EDGES = ["sage 1 edges", "sage 2 edges", "gru edges", *[f"gin {l} edges" for l in range(3)],
                 *[f"gat {l} edges" for l in range(3)]]
        HEADS = [4, 4, 1]

        block = ctx.enter_context(nc.Block())

        def walk(eng, body):
            for u in range(RING):
                body(u, u)
            with eng.Fori(1, STEPS // RING) as j:
                for u in range(RING):
                    body(j * RING + u, u)

        @block.sync
        def _(sp):
            idx_names = ("src_cols", "dst_cols", "next_cols", "type_cols")
            for k, name in enumerate(idx_names):
                sp.dma_start(idx_in[:, k, :], a[name]).then_inc(loaded, 16)
            sp.dma_start(endi[:, :], a["dst_ends"].to_broadcast([TILES - 1, GROUPS])).then_inc(loaded, 16)
            sp.dma_start(rows_i[:, :], a["dst_rows"].rearrange("(p k) e -> p (k e)", p=CROWS)).then_inc(loaded, 16)
            sp.dma_start(res[:, :].rearrange("p (t f) -> p t f", f=D),
                         a["x"].rearrange("(t p) f -> p t f", p=P)).then_inc(loaded, 16)
            for dst, src in loads:
                sp.dma_start(dst, src).then_inc(loaded, 16)
            n = 0

            def store(name, dst, src):
                nonlocal n
                sp.wait_ge(turn, AT[name])
                sp.dma_start(dst, src).then_inc(stored, 16)
                n += 16
                sp.wait_ge(stored, n)
                sp.sem_inc(turn, 1)

            def edge_rows(S, l_at, parts):
                sp.wait_ge(turn, AT[l_at])

                def load(s, u):
                    g = sp.value_load(group_i[0:1, bass.ds(s, 1)], min_val=0, max_val=GROUPS - 1)
                    if not (isinstance(s, int) and s < RING):
                        sp.wait_ge(S["projected"], s - RING + 1)
                    if "scanned" in S and not (isinstance(s, int) and s < RING):
                        sp.wait_ge(S["scanned"], s - RING + 1)
                    parts(g, u)

                for u in range(RING):
                    load(u, u)
                with sp.Fori(1, NSP // RING) as j:
                    for u in range(RING):
                        load(j * RING + u, u)

            store("store penalties", pen_rows.rearrange("(p k) e -> p (k e)", p=CROWS), pen)
            t_rows = table.rearrange("(t p) f -> p t f", p=P)
            for l in (1, 2):
                store(f"sage {l} table", t_rows, (hr if l == 1 else res)[:, :].rearrange("p (t f) -> p t f", f=D))
            for l in range(3):
                store(f"gin {l} table", t_rows, hr[:, :].rearrange("p (t f) -> p t f", f=D))

                def gin_parts(g, u, l=l):
                    sp.dma_start(ea1[u][0:16, :], a["ea16"][:, bass.ds(g * GE, GE)]).then_inc(GIN[l]["edge_data"][u], 16)

                edge_rows(GIN[l], f"gin {l} edges", gin_parts)
            for l in range(3):
                store(f"gat {l} table", t_rows, hr[:, :].rearrange("p (t f) -> p t f", f=D))
                H = HEADS[l]

                def gat_parts(g, u, l=l, H=H):
                    sp.dma_start(ea[u][:, :], a["ea32"][:, bass.ds(g * GE, GE)]).then_inc(GAT[l]["edge_data"][u], 16)
                    rows = pen_rows[bass.ds(g * CH, CH), :]
                    for h in range(H):
                        sp.dma_start(pn[u][h * CH:(h + 1) * CH, :], rows).then_inc(GAT[l]["edge_data"][u], 16)

                edge_rows(GAT[l], f"gat {l} edges", gat_parts)
            t_full = N // P
            sp.wait_ge(turn, AT["store output"])
            sp.dma_start(out[0:t_full * P, :].rearrange("(t p) f -> p t f", p=P),
                         res[:, 0:t_full * D].rearrange("p (t f) -> p t f", f=D)).then_inc(stored, 16)
            sp.dma_start(out[t_full * P:N, :], res[0:N - t_full * P, t_full * D:NP]).then_inc(stored, 16)
            sp.wait_ge(stored, n + 32)

        @block.gpsimd
        def _(pool):
            n = 0

            def link(ins):
                nonlocal n
                n += 1
                ins.then_inc(plink, 1)
                pool.wait_ge(plink, n)

            for m in (ident, ones, selcnt):
                pool.memset(m[:, :], 0.0 if m is not ones else 1.0).then_inc(plink, 1)
                n += 1
            for i in range(2):
                pool.memset(TOH[i][:, :, :], 1.0)
            for i in range(RING):
                pool.memset(ea1[i][:, :], 1.0)
            pool.wait_ge(plink, n)
            link(pool.affine_select(out=ident[:, :], in_=ident[:, :], compare_op=ALU.not_equal, fill=1.0, base=0,
                                    pattern=[[-1, P]], channel_multiplier=1))
            link(pool.affine_select(out=selcnt[:, :], in_=selcnt[:, :], compare_op=ALU.not_equal, fill=1.0, base=-TYPES,
                                    pattern=[[0, 1]], channel_multiplier=1))
            exact = dict(allow_small_or_imprecise_dtypes=True)
            pool.iota(iota_d[:, :], [[1, P]], base=0, channel_multiplier=0, **exact)
            pool.iota(iota_t[:, :], [[1, TYPES]], base=0, channel_multiplier=0, **exact)
            pool.iota(iota_s[:, :], [[1, NSP]], base=0, channel_multiplier=0, **exact)
            pool.iota(pcol[:, 0:1], [[0, 1]], base=0, channel_multiplier=1, **exact)
            pool.iota(pcol[:, 1:2], [[0, 1]], base=P, channel_multiplier=P, **exact).then_inc(turn, 1)

            for S, name in zip(ALL, EDGES):
                src = a["x"] if name == "sage 1 edges" else table
                freed = S["weighted"] if "weighted" in S else S["scattered"]
                pool.wait_ge(turn, AT[name])

                def fetch(s, pair, peeled, S=S, src=src, freed=freed):
                    if not peeled:
                        pool.wait_ge(freed, s + 2 - RING)
                    pool.tensor_copy(idx8[pair][:, :], src_i[:, bass.ds(s * CH, 2 * CH)])
                    pool.drain()
                    for k in range(2 * CH):
                        q = 2 * pair + k // CH
                        pool.indirect_dma_start(
                            out=G[q][:, (k % CH) * D:(k % CH + 1) * D], out_offset=None, in_=src[:, :],
                            in_offset=bass.IndirectOffsetOnAxis(ap=idx8[pair][:, k:k + 1], axis=0),
                        ).then_inc(S["gathered"][q], 16)

                for pair in range(2):
                    fetch(2 * pair, pair, True)
                with pool.Fori(1, NSP // RING) as j:
                    for pair in range(2):
                        fetch(j * RING + 2 * pair, pair, False)

        @block.scalar
        def _(act):
            n = 0

            def stage(name):
                assert ORDER[AT[name]][0] == "act"
                act.wait_ge(turn, AT[name])

            def root(name):
                stage(name)
                act.activation(st[:, 2, :], st[:, 1, :], ACT.Sqrt).then_inc(turn, 1)

            stage("x transposed")
            act.copy(ht[:, :], ps[:, 0:NP]).then_inc(turn, 1)
            for l in (1, 2):
                stage(f"sage {l} relu")
                act.activation(hr[:, :], w1[:, :], ACT.Relu).then_inc(turn, 1)
                if l == 2:
                    root("sage norm root")
                stage(f"sage {l} transposed")
                act.copy(ht[:, :], ps[:, 0:NP]).then_inc(turn, 1)
            stage("gru messages out")
            act.copy(w2[:, :], ps[:, 0:NP]).then_inc(turn, 1)
            stage("gru r gate")
            act.activation(w1[:, :], w1[:, :], ACT.Sigmoid).then_inc(turn, 1)
            stage("gru n")
            act.activation(w1[:, :], w1[:, :], ACT.Tanh).then_inc(turn, 1)
            stage("gru z gate")
            act.activation(w2[:, :], w2[:, :], ACT.Sigmoid).then_inc(turn, 1)
            root("gru norm root")
            for l in range(3):
                stage(f"gin {l} rows out")
                act.copy(hr[:, :], ps[:, 0:NP]).then_inc(turn, 1)
                S = GIN[l]
                act.wait_ge(turn, AT[f"gin {l} edges"])

                def rectify(s, u, S=S):
                    act.wait_ge(S["summed"], s + 1)
                    act.activation(G[u][:, :], G[u][:, :], ACT.Relu).then_inc(S["rectified"], 1)

                rectify(0, 0)
                walk(act, lambda s, u, r=rectify: r(s + 1, (u + 1) % RING))
                for k in range(2):
                    stage(f"gin {l} up {k} out")
                    act.activation((w2 if k == 0 else hr)[:, :], ps[:, 0:NP], ACT.Relu,
                                   bias=W["col_L2_gnn_conv_b1"][:, 2 * l + k:2 * l + k + 1]).then_inc(turn, 1)
                stage(f"gin {l} down out")
                act.activation(w1[:, :], ps[:, 0:NP], ACT.Relu if l < 2 else ACT.Identity,
                               scale=bnv[:, 2 * l:2 * l + 1], bias=bnv[:, 2 * l + 1:2 * l + 2]).then_inc(turn, 1)
                if l < 2:
                    stage(f"gin {l} virtual up out")
                    for k in range(2):
                        v = act.activation(vm[:, k:k + 1], ps[:, 512 * k:512 * k + 1], ACT.Relu,
                                           scale=vs1[:, 2 * l + k:2 * l + k + 1], bias=vb1[:, 2 * l + k:2 * l + k + 1])
                    v.then_inc(turn, 1)
                    stage(f"gin {l} virtual down out")
                    act.activation(vt[:, :], ps[:, 0:1], ACT.Relu, scale=vs2[:, l:l + 1],
                                   bias=vb2[:, l:l + 1]).then_inc(turn, 1)
            root("gin norm root")
            for l in range(3):
                H = HEADS[l]
                C = D // H
                S = GAT[l]
                stage(f"gat {l} transposed")
                act.copy(ht[:, :], ps[:, 0:NP]).then_inc(turn, 1)
                act.wait_ge(turn, AT[f"gat {l} edges"])

                def one_hot_t(s, u, S=S):
                    act.wait_ge(S["turned"], s + 1)
                    act.copy(OHT[u][:, :], bank(0)).then_inc(S["onehot_t"], 1)

                def exps(s, u, S=S, H=H, C=C):
                    act.wait_ge(S["new_max"], s + 1)
                    act.activation(scl[u % 2][:, 0:H], mdif[u % 2][:, 0:H], ACT.Exp).then_inc(S["scale"], 1)
                    act.wait_ge(S["delta"], s + 1)
                    wt = WT[u % 2][:, 0:CH * H * (C + 1)].rearrange("p (k c) -> p k c", c=C + 1)
                    act.activation(wt[:, :, C], delta[:, 0:CH * H], ACT.Exp).then_inc(S["weight"], 1)

                one_hot_t(0, 0)
                one_hot_t(1, 1)

                def body(s, u):
                    one_hot_t(s + 2, (u + 2) % RING)
                    exps(s, u)

                walk(act, body)
                root(f"gat {l} norm root")
                stage(f"gat {l} relu")
                act.activation(w1[:, :], w1[:, :], ACT.Relu).then_inc(turn, 1)
            root("last norm root")

        @block.tensor
        def _(pe):
            def stage(name):
                assert ORDER[AT[name]][0] == "pe"
                pe.wait_ge(turn, AT[name])

            def tiles(f):
                for t in range(TILES):
                    last = f(t)
                last.then_inc(turn, 1)

            def cols(f):
                for c, w in COLS:
                    last = f(c, w)
                last.then_inc(turn, 1)

            def transpose_all(x):
                tiles(lambda t: pe.transpose(ps[:, t * P:(t + 1) * P], x[:, t * P:(t + 1) * P], ident[:, :]))

            def rows_of(xt, w):
                tiles(lambda t: pe.matmul(ps[:, t * P:(t + 1) * P], xt[:, t * P:(t + 1) * P], w, start=True, stop=True))

            def scatter(s, u, S):
                if not (isinstance(s, int) and s < 2):
                    pe.wait_ge(S["added"], s - 1)
                for c in range(CH):
                    m = pe.matmul(bank(u % 2, P), G[u][:, c * D:(c + 1) * D], OH[u][:, c * P:(c + 1) * P],
                                  start=(c == 0), stop=(c == CH - 1))
                return m

            pe.wait_ge(loaded, 16 * n_loads)
            stage("sum of tile ends")
            pe.matmul(bank(0, NSP), ones[0:TILES - 1, :], past[0:TILES - 1, :], start=True, stop=True).then_inc(turn, 1)
            stage("transpose x")
            transpose_all(res)
            for l in (1, 2):
                S = SUM[f"s{l}"]
                pe.wait_ge(turn, AT[f"sage {l} edges"])

                def body(s, u, S=S, l=l):
                    pe.wait_ge(S["gathered"][u], (s - u) * CH * 16 // RING + CH * 16)
                    pe.wait_ge(S["onehot"], s + 1)
                    m = scatter(s, u, S)
                    if l == 1:
                        for c in range(CH):
                            m = pe.matmul(bank(2 + u % 2, P, TYPES + 1), TOH[u % 2][:, c, :],
                                          OH[u][:, c * P:(c + 1) * P], start=(c == 0), stop=(c == CH - 1))
                    m.then_inc(S["scattered"], 1)

                walk(pe, body)
                if l == 1:
                    stage("degrees")
                    tiles(lambda t: pe.matmul(ps[:, t:t + 1], cnt[:, t * P:(t + 1) * P], selcnt[:, :],
                                              start=True, stop=True))
                stage(f"sage {l} neighbours")
                rows_of(agg, W[f"L0_gnn_Wl{l}"][:, :])
                stage(f"sage {l} self")
                rows_of(ht, W[f"L0_gnn_Wr{l}"][:, :])
                stage(f"sage {l} transpose")
                transpose_all(hr if l == 1 else res)

            S = SUM["gr"]
            pe.wait_ge(turn, AT["gru edges"])

            def body(s, u):
                pe.wait_ge(S["gathered"][u], (s - u) * CH * 16 // RING + CH * 16)
                pe.wait_ge(S["onehot"], s + 1)
                scatter(s, u, S).then_inc(S["scattered"], 1)

            walk(pe, body)
            stage("gru messages")

            def messages(c, w):
                pe.matmul(ps[:, c:c + w], W["L1_gnn_W_msg"][:, :], agg[:, c:c + w], start=True, stop=False)
                return pe.matmul(ps[:, c:c + w], W["L1_aug"][:, :], cnt[:, c:c + w], start=False, stop=True)

            cols(messages)

            def gate(k):
                def f(t):
                    o, i, w = ps[:, t * P:(t + 1) * P], slice(t * P, (t + 1) * P), slice(k * D, (k + 1) * D)
                    pe.matmul(o, w2[:, i], W["L1_gnn_W_ih"][:, w], start=True, stop=False)
                    return pe.matmul(o, ht[:, i], W["L1_gnn_W_hh"][:, w], start=False, stop=True)
                return f

            stage("gru r")
            tiles(gate(0))
            stage("gru hn")
            rows_of(ht, W["L1_gnn_W_hh"][:, 2 * D:3 * D])
            stage("gru in")
            rows_of(w2, W["L1_gnn_W_ih"][:, 2 * D:3 * D])
            stage("gru z")
            tiles(gate(1))
            stage("gru transpose")
            transpose_all(res)

            for l in range(3):
                stage(f"gin {l} rows")
                transpose_all(ht)
                S = GIN[l]
                pe.wait_ge(turn, AT[f"gin {l} edges"])

                def project(s, u, S=S, l=l):
                    pe.wait_ge(S["edge_data"][u], (s - u) * 16 // RING + 16)
                    if not (isinstance(s, int) and s < 2):
                        pe.wait_ge(S["summed"], s - 1)
                    for c in range(CH):
                        m = pe.matmul(ps[:, 1024 + 512 * (u % 2) + c * D:1024 + 512 * (u % 2) + (c + 1) * D],
                                      ea1[u][:, c * P:(c + 1) * P], W["L2_conv_edge"][:, l * D:(l + 1) * D],
                                      start=True, stop=True)
                    m.then_inc(S["projected"], 1)

                project(0, 0)

                def body(s, u, S=S, project=project):
                    project(s + 1, (u + 1) % RING)
                    pe.wait_ge(S["onehot"], s + 1)
                    pe.wait_ge(S["rectified"], s + 1)
                    scatter(s, u, S).then_inc(S["scattered"], 1)

                walk(pe, body)
                for k in range(2):
                    stage(f"gin {l} up {k}")
                    cols(lambda c, w: pe.matmul(ps[:, c:c + w], W["L2_gnn_conv_w1"][:, (2 * l + k) * D:(2 * l + k + 1) * D],
                                                w1[:, c:c + w], start=True, stop=True))
                stage(f"gin {l} down")

                def down(c, w):
                    o = ps[:, c:c + w]
                    pe.matmul(o, W["L2_gnn_conv_w2"][:, 2 * l * D:(2 * l + 1) * D], w2[:, c:c + w], start=True, stop=False)
                    return pe.matmul(o, W["L2_gnn_conv_w2"][:, (2 * l + 1) * D:(2 * l + 2) * D], hr[:, c:c + w],
                                     start=False, stop=True)

                cols(down)
                if l < 2:
                    stage(f"gin {l} virtual up")
                    for k in range(2):
                        m = pe.matmul(ps[:, 512 * k:512 * k + 1], W["L2_gnn_vn_w1"][:, (2 * l + k) * D:(2 * l + k + 1) * D],
                                      vsum[:, :], start=True, stop=True)
                    m.then_inc(turn, 1)
                    stage(f"gin {l} virtual down")
                    for k in range(2):
                        m = pe.matmul(ps[:, 0:1], W["L2_gnn_vn_w2"][:, (2 * l + k) * D:(2 * l + k + 1) * D],
                                      vm[:, k:k + 1], start=(k == 0), stop=(k == 1))
                    m.then_inc(turn, 1)
            stage("gin transpose")
            transpose_all(w1)

            for l in range(3):
                H = HEADS[l]
                C = D // H
                KH = CH * H
                S = GAT[l]
                stage(f"gat {l} transpose")
                transpose_all(res if l == 0 else w1)
                stage(f"gat {l} left")
                rows_of(ht, W[f"L3_gnn_Wl{l}"][:, :])
                stage(f"gat {l} right")
                rows_of(ht, W[f"L3_gnn_Wr{l}"][:, :])
                pe.wait_ge(turn, AT[f"gat {l} edges"])
                turned, term = bank(0), [bank(1), bank(2)]
                score_t, scan_back, seg_max = bank(3, P, KH), bank(4, KH), bank(5, CH * (H + 1))
                max_of_edge, sums = bank(6, KH), bank(7, H * (C + 1))

                def turn_one_hot(s, u, S=S):
                    pe.wait_ge(S["onehot"], s + 1)
                    if not (isinstance(s, int) and s < 1):
                        pe.wait_ge(S["onehot_t"], s)
                    for c in range(CH):
                        m = pe.transpose(turned[:, c * P:(c + 1) * P], OH[u][:, c * P:(c + 1) * P], ident[:, :])
                    m.then_inc(S["turned"], 1)

                def project(s, u, S=S, l=l, H=H):
                    t = pe.value_load(tile_i[0:1, bass.ds(s, 1)], min_val=0, max_val=TILES - 1)
                    pe.wait_ge(S["edge_data"][u], (s - u) * 16 * (1 + H) // RING + 16 * (1 + H))
                    if not (isinstance(s, int) and s < 2):
                        pe.wait_ge(S["score"], s - 1)
                    pe.wait_ge(S["onehot_t"], s + 1)
                    for c in range(CH):
                        o = term[u % 2][:, c * D:(c + 1) * D]
                        pe.matmul(o, ea[u][:, c * P:(c + 1) * P], W[f"L3_gnn_We{l}"][:, :], start=True, stop=False)
                        m = pe.matmul(o, OHT[u][:, c * P:(c + 1) * P], xr[:, bass.ds(t * D, D)], start=False, stop=True)
                    m.then_inc(S["projected"], 1)

                for s in range(2):
                    turn_one_hot(s, s)
                    project(s, s)

                def body(s, u, S=S, H=H, C=C, KH=KH):
                    pe.wait_ge(S["score"], s + 1)
                    pe.transpose(score_t, score[u % 2][:, 0:KH], ident[:, :]).then_inc(S["score_t"], 1)
                    pe.wait_ge(S["scanned"], s + 1)
                    pe.matmul(scan_back, scanned[0:KH, :], ident[0:KH, 0:KH], start=True,
                              stop=True).then_inc(S["scan_back"], 1)
                    turn_one_hot(s + 2, (u + 2) % RING)
                    pe.wait_ge(S["seg_rhs"], s + 1)
                    for c in range(CH):
                        m = pe.matmul(seg_max[:, c * (H + 1):(c + 1) * (H + 1)], OH[u][:, c * P:(c + 1) * P],
                                      segrhs[:, c * (H + 1):(c + 1) * (H + 1)], start=True, stop=True)
                    m.then_inc(S["seg_max"], 1)
                    pe.wait_ge(S["new_max"], s + 1)
                    for c in range(CH):
                        m = pe.matmul(max_of_edge[:, c * H:(c + 1) * H], OHT[u][:, c * P:(c + 1) * P],
                                      mnew[u % 2][:, 0:H], start=True, stop=True)
                    m.then_inc(S["max_of_edge"], 1)
                    project(s + 2, (u + 2) % RING)
                    pe.wait_ge(S["weighted"], s + 1)
                    if not (isinstance(s, int) and s < 1):
                        pe.wait_ge(S["added"], s)
                    for c in range(CH):
                        m = pe.matmul(sums, OH[u][:, c * P:(c + 1) * P],
                                      WT[u % 2][:, c * H * (C + 1):(c + 1) * H * (C + 1)],
                                      start=(c == 0), stop=(c == CH - 1))
                    m.then_inc(S["scattered"], 1)

                walk(pe, body)

        @block.vector
        def _(dve):
            n = 0

            def link(ins):
                nonlocal n
                n += 1
                ins.then_inc(dlink, 1)
                dve.wait_ge(dlink, n)

            def stage(name):
                assert ORDER[AT[name]][0] == "dve"
                dve.wait_ge(turn, AT[name])

            def tiled(x, w=D):
                return x.rearrange("p (t f) -> p t f", f=w)

            def per_tile(x):
                return x[:, :, None].to_broadcast([P, TILES, D])

            def per_row(name):
                return W[name][:, None, :].to_broadcast([P, TILES, D])

            def norm_a(name, x):
                link(dve.tensor_reduce(st[:, 0, :], tiled(x), AX.X, ALU.add))
                link(dve.tensor_scalar(st[:, 0, :], st[:, 0, :], -1.0 / D, None, ALU.mult))
                link(dve.tensor_tensor(tiled(x), tiled(x), per_tile(st[:, 0, :]), ALU.add))
                link(dve.tensor_tensor(w2[:, :], x, x, ALU.mult))
                link(dve.tensor_reduce(st[:, 1, :], tiled(w2[:, :]), AX.X, ALU.add))
                dve.tensor_scalar(st[:, 1, :], st[:, 1, :], 1.0 / D, EPS, ALU.mult, ALU.add).then_inc(turn, 1)

            def norm_b(name, dst, x, more=None):
                stage(name)
                link(dve.reciprocal(st[:, 3, :], st[:, 2, :]))
                ins = dve.tensor_tensor(tiled(dst), tiled(x), per_tile(st[:, 3, :]), ALU.mult)
                if more:
                    link(ins)
                    ins = more()
                ins.then_inc(turn, 1)

            def one_hot(s, u, S):
                dve.tensor_tensor(OH[u][:, :].rearrange("p (c d) -> p c d", d=P),
                                  dloc[:, bass.ds(s * CH, CH)][:, :, None].to_broadcast([P, CH, P]),
                                  iota_d[:, None, :].to_broadcast([P, CH, P]), ALU.is_equal).then_inc(S["onehot"], 1)

            def finish(S, rows=0):
                for q in range(RING):
                    dve.wait_ge(S["gathered"][q], CH * 16 * NSP // RING)
                    if rows:
                        dve.wait_ge(S["edge_data"][q], rows * 16 * NSP // RING)
                dve.wait_ge(S["added"], STEPS)
                dve.sem_inc(turn, 1)

            stage("step tables 1")
            dve.wait_ge(loaded, 16 * n_loads)
            link(dve.tensor_copy(ends[0:TILES - 1, :], endi[:, :]))
            link(dve.tensor_scalar(pcol[:, 2:3], pcol[:, 0:1], float(P - 1), None, ALU.is_equal))
            link(dve.tensor_scalar(ends[0:TILES - 1, :], ends[0:TILES - 1, :], pcol[0:TILES - 1, 1:2], None, ALU.is_lt))
            link(dve.tensor_reduce(gl[0:TILES - 1, :], ends[0:TILES - 1, :], AX.X, ALU.add))
            link(dve.tensor_tensor(gl[0:TILES - 1, :], gl[0:TILES - 1, :], pcol[0:TILES - 1, 0:1], ALU.add))
            dve.tensor_scalar(past[0:TILES - 1, :], iota_s[0:TILES - 1, :], gl[0:TILES - 1, 0:1], None,
                              ALU.is_gt).then_inc(turn, 1)
            stage("step tables 2")
            link(dve.tensor_copy(tstep[:, :], bank(0, NSP)))
            link(dve.tensor_tensor(gstep[:, :], iota_s[:, :], tstep[:, :], ALU.subtract))
            link(dve.tensor_scalar(gstep[:, :], gstep[:, :], float(GROUPS - 1), None, ALU.min))
            link(dve.tensor_copy(tile_i[0:1, :], tstep[0:1, :]))
            link(dve.tensor_copy(group_i[0:1, :], gstep[0:1, :]))
            pk = packed.rearrange("p (g f c) -> p f g c", f=4, c=CH)

            def chunks(k):
                return idx_in[:, k, :].rearrange("p (g c) -> p g c", c=CH)

            link(dve.tensor_copy(pk[:, 0], chunks(0)))
            link(dve.tensor_copy(pk[:, 1], chunks(1)))
            link(dve.tensor_copy(pk[:, 3], chunks(3)))
            link(dve.tensor_copy(pk[:, 2], chunks(2)))
            link(dve.tensor_tensor(pk[:, 2], pk[:, 2], pk[:, 1], ALU.not_equal))
            link(dve.tensor_scalar(pk[:, 2], pk[:, 2], pcol[:, 2:3], None, ALU.max))
            link(dve.tensor_scalar(pk[:, 3], pk[:, 3], 0.0, float(TYPES - 1), ALU.max, ALU.min))
            with dve.Fori(0, NSP) as s:
                g = dve.value_load(group_i[0:1, bass.ds(s, 1)], min_val=0, max_val=GROUPS - 1)
                dve.tensor_copy(fields[:, bass.ds(s * 16, 16)], packed[:, bass.ds(g * 16, 16)]).then_inc(fcopy, 1)
            dve.wait_ge(fcopy, NSP)

            def stepped(x):
                return x[:, :].rearrange("p (s c) -> p s c", c=CH)

            dve.tensor_copy(stepped(src_i), fview[:, :, 0])
            dve.tensor_copy(stepped(last), fview[:, :, 2])
            dve.tensor_copy(stepped(etype), fview[:, :, 3])
            link(dve.tensor_scalar(tstep[:, :], tstep[:, :], float(P), None, ALU.mult))
            link(dve.tensor_tensor(stepped(dloc), fview[:, :, 1], tstep[:, :, None].to_broadcast([P, NSP, CH]),
                                   ALU.subtract))
            rv, pv = rows_f.rearrange("p (k e) -> p k e", e=P), pen.rearrange("p (k e) -> p k e", e=P)
            link(dve.tensor_copy(rows_f, rows_i[:, :]))
            link(dve.memset(pv[:, :, 0:1], -BIG))
            link(dve.tensor_tensor(pv[:, :, 1:P], rv[:, :, 1:P], rv[:, :, 0:P - 1], ALU.is_equal))
            link(dve.tensor_scalar(pv[:, :, 1:P], pv[:, :, 1:P], 1.0, BIG, ALU.subtract, ALU.mult))
            V = {k[7:]: W["col_" + k] for k in VEC_COLS}
            for l in range(3):
                link(dve.tensor_scalar(bnv[:, 2 * l:2 * l + 1], V["bn_gamma"][:, l:l + 1], INV, None, ALU.mult))
                link(dve.tensor_tensor(bnv[:, 2 * l + 1:2 * l + 2], V["conv_b2"][:, l:l + 1], bnv[:, 2 * l:2 * l + 1],
                                       ALU.mult))
                link(dve.tensor_tensor(bnv[:, 2 * l + 1:2 * l + 2], bnv[:, 2 * l + 1:2 * l + 2],
                                       V["bn_beta"][:, l:l + 1], ALU.add))
            for scale, bias, g, b, be in ((vs1, vb1, "vn_g1", "vn_b1", "vn_be1"), (vs2, vb2, "vn_g2", "vn_b2", "vn_be2")):
                link(dve.tensor_scalar(scale[:, :], V[g][:, :], INV, None, ALU.mult))
                link(dve.tensor_tensor(bias[:, :], V[b][:, :], scale[:, :], ALU.mult))
                link(dve.tensor_tensor(bias[:, :], bias[:, :], V[be][:, :], ALU.add))
            dve.tensor_copy(vn[:, :], V["vn_emb"][:, :]).then_inc(turn, 1)

            def sum_pass(S, first=False):
                link(dve.memset(agg[:, 0:NP], 0.0))
                if first:
                    link(dve.memset(cnt[:, :], 0.0))

                def one_hot_all(s, u):
                    if first:
                        dve.tensor_tensor(TOH[u % 2][:, :, 0:TYPES],
                                          etype[:, bass.ds(s * CH, CH)][:, :, None].to_broadcast([P, CH, TYPES]),
                                          iota_t[:, None, :].to_broadcast([P, CH, TYPES]), ALU.is_equal)
                    one_hot(s, u, S)

                one_hot_all(0, 0)

                def body(s, u):
                    one_hot_all(s + 1, (u + 1) % RING)
                    add_sums(s, u, S, first)

                walk(dve, body)
                finish(S)

            def add_sums(s, u, S, first=False):
                t = dve.value_load(tile_i[0:1, bass.ds(s, 1)], min_val=0, max_val=TILES - 1)
                if not (isinstance(s, int) and s < 1):
                    dve.wait_ge(S["added"], s)
                dve.wait_ge(S["scattered"], s + 1)
                w = agg[:, bass.ds(t * P, P)]
                if first:
                    cw = cnt[:, bass.ds(t * P, P)]
                    dve.tensor_tensor(cw, cw, bank(2 + u % 2, P, TYPES + 1), ALU.add)
                dve.tensor_tensor(w, w, bank(u % 2, P), ALU.add).then_inc(S["added"], 1)

            for l in (1, 2):
                stage(f"sage {l} edges")
                sum_pass(SUM[f"s{l}"], first=(l == 1))
                if l == 1:
                    stage("one over degree")
                    link(dve.tensor_scalar(rdeg[:, :], ps[:, 0:TILES], 1.0, None, ALU.max))
                    dve.reciprocal(rdeg[:, :], rdeg[:, :]).then_inc(turn, 1)
                stage(f"sage {l} mean")
                link(dve.tensor_tensor(tiled(w1[:, :]), tiled(ps[:, 0:NP]), per_tile(rdeg[:, :]), ALU.mult))
                dve.tensor_tensor(tiled(w1[:, :]), tiled(w1[:, :]), per_row(f"L0_gnn_bl{l}"), ALU.add).then_inc(turn, 1)
                stage(f"sage {l} add")
                dve.tensor_tensor(w1[:, :], w1[:, :], ps[:, 0:NP], ALU.add).then_inc(turn, 1)
            stage("sage norm a")
            link(dve.tensor_tensor(w1[:, :], hr[:, :], res[:, :], ALU.add))
            norm_a("sage", w1[:, :])
            norm_b("sage norm b", res[:, :], w1[:, :])

            stage("gru edges")
            sum_pass(SUM["gr"])
            bih, bhh = W["L1_gnn_b_ih"], W["L1_gnn_b_hh"]

            def gate_bias(b, k):
                return b[:, k * D:(k + 1) * D][:, None, :].to_broadcast([P, TILES, D])

            stage("gru r bias")
            link(dve.tensor_tensor(tiled(w1[:, :]), tiled(ps[:, 0:NP]), gate_bias(bih, 0), ALU.add))
            dve.tensor_tensor(tiled(w1[:, :]), tiled(w1[:, :]), gate_bias(bhh, 0), ALU.add).then_inc(turn, 1)
            stage("gru hn gated")
            link(dve.tensor_tensor(tiled(hr[:, :]), tiled(ps[:, 0:NP]), gate_bias(bhh, 2), ALU.add))
            dve.tensor_tensor(w1[:, :], w1[:, :], hr[:, :], ALU.mult).then_inc(turn, 1)
            stage("gru in add")
            link(dve.tensor_tensor(w1[:, :], w1[:, :], ps[:, 0:NP], ALU.add))
            dve.tensor_tensor(tiled(w1[:, :]), tiled(w1[:, :]), gate_bias(bih, 2), ALU.add).then_inc(turn, 1)
            stage("gru z bias")
            link(dve.tensor_tensor(tiled(w2[:, :]), tiled(ps[:, 0:NP]), gate_bias(bih, 1), ALU.add))
            dve.tensor_tensor(tiled(w2[:, :]), tiled(w2[:, :]), gate_bias(bhh, 1), ALU.add).then_inc(turn, 1)
            stage("gru norm a")
            link(dve.tensor_tensor(hr[:, :], res[:, :], w1[:, :], ALU.subtract))
            link(dve.tensor_tensor(hr[:, :], hr[:, :], w2[:, :], ALU.mult))
            link(dve.tensor_tensor(hr[:, :], hr[:, :], w1[:, :], ALU.add))
            link(dve.tensor_tensor(w1[:, :], hr[:, :], res[:, :], ALU.add))
            norm_a("gru", w1[:, :])
            norm_b("gru norm b", res[:, :], w1[:, :])

            def node_sum():
                link(dve.tensor_reduce(vsum[:, :], ht[:, 0:N], AX.X, ALU.add))
                return dve.tensor_tensor(vsum[:, :], vsum[:, :], vn[:, :], ALU.add)

            stage("gru transposed")
            link(dve.tensor_scalar(ht[:, :], ps[:, 0:NP], vn[:, 0:1], None, ALU.add))
            node_sum().then_inc(turn, 1)
            for l in range(3):
                S = GIN[l]
                stage(f"gin {l} edges")
                link(dve.memset(agg[:, 0:NP], 0.0))

                def add_term(s, u, S=S):
                    dve.wait_ge(S["gathered"][u], (s - u) * CH * 16 // RING + CH * 16)
                    dve.wait_ge(S["projected"], s + 1)
                    dve.tensor_tensor(G[u][:, :], G[u][:, :], bank(2 + u % 2), ALU.add).then_inc(S["summed"], 1)

                one_hot(0, 0, S)
                add_term(0, 0)

                def body(s, u, S=S, add_term=add_term):
                    one_hot(s + 1, (u + 1) % RING, S)
                    add_term(s + 1, (u + 1) % RING)
                    add_sums(s, u, S)

                walk(dve, body)
                dve.wait_ge(S["rectified"], STEPS + 1)
                dve.wait_ge(S["added"], STEPS)
                link(dve.tensor_tensor(w1[:, :], agg[:, 0:NP], ht[:, :], ALU.add))
                finish(S, 1)
                stage(f"gin {l} residual")
                if l < 2:
                    link(dve.tensor_tensor(vn[:, :], vn[:, :], vt[:, :], ALU.add))
                    link(dve.tensor_tensor(w1[:, :], w1[:, :], ht[:, :], ALU.add))
                    link(dve.tensor_scalar(ht[:, :], w1[:, :], vn[:, 0:1], None, ALU.add))
                    node_sum().then_inc(turn, 1)
                else:
                    dve.tensor_tensor(w1[:, :], w1[:, :], ht[:, :], ALU.add).then_inc(turn, 1)
            stage("gin norm a")
            link(dve.tensor_tensor(w1[:, :], ps[:, 0:NP], res[:, :], ALU.add))
            norm_a("gin", w1[:, :])
            norm_b("gin norm b", res[:, :], w1[:, :])

            for l in range(3):
                H = HEADS[l]
                C = D // H
                KH = CH * H
                HC = H * (C + 1)
                S = GAT[l]
                stage(f"gat {l} left out")
                dve.tensor_tensor(tiled(hr[:, :]), tiled(ps[:, 0:NP]), per_row(f"L3_gnn_bl{l}"), ALU.add).then_inc(turn, 1)
                stage(f"gat {l} right out")
                dve.tensor_tensor(tiled(xr[:, :]), tiled(ps[:, 0:NP]), per_row(f"L3_gnn_br{l}"), ALU.add).then_inc(turn, 1)
                stage(f"gat {l} edges")
                link(dve.memset(agg[:, 0:TILES * HC], 0.0))
                link(dve.memset(mx[:, :], -BIG))
                term = [bank(1), bank(2)]
                score_t, scan_back, seg_max = bank(3, P, KH), bank(4, KH), bank(5, CH * (H + 1))
                max_of_edge, sums = bank(6, KH), bank(7, HC)
                att = W[f"L3_gnn_att{l}"]
                SL = 8
                sl = S["slink"]

                def logits(s, u, part):
                    first = (isinstance(s, int) and s == 0)
                    if part == 0:
                        dve.wait_ge(S["gathered"][u], (s - u) * CH * 16 // RING + CH * 16)
                        dve.wait_ge(S["projected"], s + 1)
                        dve.tensor_tensor(msg[:, :], G[u][:, :], term[u % 2], ALU.add).then_inc(lg, 1)
                    if part == 1:
                        dve.wait_ge(lg, 3 * s + 1)
                        dve.scalar_tensor_tensor(out=lk[:, :], in0=msg[:, :], scalar=0.2, in1=msg[:, :],
                                                 op0=ALU.mult, op1=ALU.max).then_inc(lg, 1)
                    if part == 2:
                        dve.wait_ge(lg, 3 * s + 2)
                        dve.tensor_tensor(lk[:, :].rearrange("p (c f) -> p c f", f=D),
                                          lk[:, :].rearrange("p (c f) -> p c f", f=D),
                                          att[:, None, :].to_broadcast([P, CH, D]), ALU.mult).then_inc(lg, 1)
                        dve.wait_ge(lg, 3 * s + 3)
                        dve.tensor_reduce(score[u % 2][:, 0:KH].rearrange("p (h c) -> p c h", h=H),
                                          lk[:, :].rearrange("p (c h k) -> p c h k", c=CH, h=H), AX.X,
                                          ALU.add).then_inc(S["score"], 1)

                lg = sem(f"gat{l}_logit_parts")

                def slot(s, k):
                    return s * SL + k

                def take_sums(s, u):
                    t = dve.value_load(tile_i[0:1, bass.ds(s, 1)], min_val=0, max_val=TILES - 1)
                    if not (isinstance(s, int) and s < 1):
                        dve.wait_ge(S["added"], s)
                    w = agg[:, bass.ds(t * HC, HC)]
                    dve.wait_ge(S["scale"], s + 1)
                    dve.tensor_tensor(w.rearrange("p (h c) -> p h c", h=H), w.rearrange("p (h c) -> p h c", h=H),
                                      scl[u % 2][:, 0:H, None].to_broadcast([P, H, C + 1]), ALU.mult).then_inc(rescaled, 1)
                    dve.wait_ge(rescaled, s + 1)
                    dve.wait_ge(S["scattered"], s + 1)
                    dve.tensor_tensor(w, w, sums, ALU.add).then_inc(S["added"], 1)

                rescaled = sem(f"gat{l}_rescaled")

                def body(s, u, first=False):
                    dve.wait_ge(S["score_t"], s + 1)
                    dve.tensor_tensor_scan(out=scanned[0:KH, :], data0=pn[u][0:KH, :], data1=score_t, initial=-BIG,
                                           op0=ALU.add, op1=ALU.max).then_inc(S["scanned"], 1)
                    one_hot(s + 2, (u + 2) % RING, S)
                    if not first:
                        take_sums(s - 1, (u - 1) % RING)
                    dve.wait_ge(S["scan_back"], s + 1)
                    rhs = segrhs[:, 0:CH * (H + 1)].rearrange("p (c h) -> p c h", c=CH)
                    lst = last[:, bass.ds(s * CH, CH)]
                    dve.tensor_scalar(rhs[:, :, H], lst, 1.0, None, ALU.mult)
                    dve.tensor_tensor(rhs[:, :, 0:H], scan_back.rearrange("p (h c) -> p c h", h=H),
                                      lst[:, :, None].to_broadcast([P, CH, H]), ALU.mult).then_inc(S["seg_rhs"], 1)
                    logits(s + 1, (u + 1) % RING, 0)
                    t = dve.value_load(tile_i[0:1, bass.ds(s, 1)], min_val=0, max_val=TILES - 1)
                    mt = mx[:, bass.ds(t * 4, H)]
                    sm = seg_max.rearrange("p (c h) -> p c h", c=CH)
                    dve.wait_ge(S["seg_max"], s + 1)
                    dve.tensor_scalar(spen[:, :], sm[:, :, H], 1.0, BIG, ALU.subtract, ALU.mult).then_inc(sl, 1)
                    dve.wait_ge(sl, slot(s, 1))
                    dve.tensor_tensor(sval[:, 0:KH].rearrange("p (c h) -> p c h", c=CH), sm[:, :, 0:H],
                                      spen[:, :, None].to_broadcast([P, CH, H]), ALU.add).then_inc(sl, 1)
                    dve.wait_ge(sl, slot(s, 2))
                    dve.tensor_reduce(smx[:, 0:H], sval[:, 0:KH].rearrange("p (c h) -> p h c", c=CH), AX.X,
                                      ALU.max).then_inc(sl, 1)
                    dve.wait_ge(sl, slot(s, 3))
                    dve.tensor_tensor(mnew[u % 2][:, 0:H], smx[:, 0:H], mt, ALU.max).then_inc(sl, 1)
                    dve.wait_ge(sl, slot(s, 4))
                    dve.tensor_tensor(mdif[u % 2][:, 0:H], mt, mnew[u % 2][:, 0:H], ALU.subtract).then_inc(sl, 1)
                    dve.wait_ge(sl, slot(s, 5))
                    dve.tensor_scalar(mt, mnew[u % 2][:, 0:H], 1.0, None, ALU.mult).then_inc(S["new_max"], 1)
                    logits(s + 1, (u + 1) % RING, 1)
                    dve.wait_ge(S["max_of_edge"], s + 1)
                    dve.tensor_tensor(delta[:, 0:KH].rearrange("p (c h) -> p c h", c=CH),
                                      score[u % 2][:, 0:KH].rearrange("p (h c) -> p c h", h=H),
                                      max_of_edge.rearrange("p (c h) -> p c h", c=CH), ALU.subtract).then_inc(sl, 1)
                    dve.wait_ge(sl, slot(s, 6))
                    dve.tensor_scalar(delta[:, 0:KH], delta[:, 0:KH], 0.0, None, ALU.min).then_inc(S["delta"], 1)
                    dve.sem_inc(sl, SL - 6)
                    logits(s + 1, (u + 1) % RING, 2)
                    dve.wait_ge(S["weight"], s + 1)
                    wt = WT[u % 2][:, 0:KH * (C + 1)].rearrange("p (k c) -> p k c", c=C + 1)
                    dve.tensor_tensor(wt[:, :, 0:C], G[u][:, :].rearrange("p (k c) -> p k c", c=C),
                                      wt[:, :, C:C + 1].to_broadcast([P, KH, C]), ALU.mult).then_inc(S["weighted"], 1)

                one_hot(0, 0, S)
                one_hot(1, 1, S)
                for part in range(3):
                    logits(0, 0, part)
                walk(dve, lambda s, u, body=body: body(s, u, first=(isinstance(s, int) and s == 0)))
                take_sums(STEPS - 1, (STEPS - 1) % RING)
                dve.wait_ge(S["projected"], STEPS + 2)
                dve.wait_ge(S["turned"], STEPS + 2)
                finish(S, 1 + H)

                stage(f"gat {l} norm a")
                av = agg[:, 0:TILES * HC].rearrange("p (t h c) -> p t h c", h=H, c=C + 1)
                rd = rden[:, :, 0:H]
                link(dve.tensor_scalar(rd, av[:, :, :, C], 1e-30, None, ALU.max))
                link(dve.reciprocal(rd, rd))
                for h in range(H):
                    link(dve.tensor_tensor(tiled(w1[:, :])[:, :, h * C:(h + 1) * C], av[:, :, h, 0:C],
                                           rden[:, :, h:h + 1].to_broadcast([P, TILES, C]), ALU.mult))
                link(dve.tensor_tensor(tiled(w1[:, :]), tiled(w1[:, :]), per_row(f"L3_gnn_b{l}"), ALU.add))
                norm_a("gat", w1[:, :])

                def affine(l=l):
                    link(dve.tensor_tensor(tiled(w1[:, :]), tiled(w1[:, :]), per_row(f"L3_gnn_g{l}"), ALU.mult))
                    return dve.tensor_tensor(tiled(w1[:, :]), tiled(w1[:, :]), per_row(f"L3_gnn_be{l}"), ALU.add)

                norm_b(f"gat {l} norm b", w1[:, :], w1[:, :], affine)
            stage("last norm a")
            link(dve.tensor_tensor(w1[:, :], w1[:, :], res[:, :], ALU.add))
            norm_a("last", w1[:, :])
            norm_b("last norm b", res[:, :], w1[:, :])


def kernel(**inputs):
    import numpy as np
    import concourse.bacc as bacc
    from concourse.bass_utils import run_bass_kernel_spmd

    inp = {k: np.asarray(v) for k, v in inputs.items()}
    host = {}

    def pad(v, n, fill):
        return np.concatenate([v, np.full((n - len(v),) + v.shape[1:], fill, v.dtype)])

    def columns(v):
        return v.reshape(CHUNKS, P).T

    dst = pad(inp["dst"], EP + 1, 1 << 20)
    host["x"] = pad(inp["x"], NP, 0)
    host["src_cols"] = columns(pad(inp["src"], EP, 0))
    host["dst_cols"] = columns(dst[:EP])
    host["next_cols"] = columns(dst[1:])
    host["type_cols"] = columns(pad(inp["edge_type_9"], EP, 0))
    host["dst_rows"] = dst[:EP].reshape(CHUNKS, P)
    host["dst_ends"] = dst[GE - 1:EP:GE].reshape(1, GROUPS)
    host["ea16"] = pad(inp["edge_attr_16"], EP, 0).T
    host["ea32"] = pad(inp["edge_attr_32"], EP, 0).T
    for k in ("L0_gnn_Wl1", "L0_gnn_Wr1", "L0_gnn_Wl2", "L0_gnn_Wr2",
              *[f"L3_gnn_{v}{l}" for l in range(3) for v in ("Wl", "Wr", "We")]):
        host[k] = inp[k]
    for k in ("L1_gnn_W_msg", "L1_gnn_W_ih", "L1_gnn_W_hh"):
        host[k] = inp[k].T
    host["L1_aug"] = np.concatenate([inp["L1_gnn_edge_embed"], inp["L1_gnn_b_msg"][None]])
    host["L2_conv_edge"] = np.concatenate([inp["L2_gnn_conv_edge_w"].transpose(1, 0, 2).reshape(16, 3 * D),
                                           inp["L2_gnn_conv_edge_b"].reshape(1, 3 * D)])
    for k in ("L2_gnn_conv_w1", "L2_gnn_vn_w1"):
        host[k] = inp[k].transpose(1, 0, 2).reshape(D, -1)
    for k in ("L2_gnn_conv_w2", "L2_gnn_vn_w2"):
        host[k] = inp[k].reshape(-1, 2, D, D).transpose(2, 0, 1, 3).reshape(D, -1)
    for k in VEC_COLS:
        host["col_" + k] = inp[k].reshape(-1, D).T
    for k in VEC_ROWS:
        host[k] = inp[k].reshape(1, -1)

    nc = bacc.Bacc("TRN2", target_bir_lowering=False, num_devices=1)
    arrays, args = {}, {}
    for name, v in host.items():
        v = np.ascontiguousarray(v)
        arrays[f"in_{name}"] = v
        args[name] = nc.dram_tensor(f"in_{name}", v.shape, mybir.dt.from_np(v.dtype), kind="ExternalInput").ap()
    out = nc.dram_tensor("out", (N, D), F32, kind="ExternalOutput").ap()
    build(nc, args, out)
    r = run_bass_kernel_spmd(nc, [arrays], core_ids=[0])
    return r.results[0]["out"]
```

```python
import concourse.bass as bass
from concourse import mybir
from contextlib import ExitStack

F32, I32 = mybir.dt.float32, mybir.dt.int32
ALU, ACT, AX = mybir.AluOpType, mybir.ActivationFunctionType, mybir.AxisListType

P = 128
D = 128
N, E = 3125, 100000
TILES = -(-N // P)
NP = TILES * P
CH = 4
GE = CH * P
GROUPS = -(-E // GE)
CHUNKS = GROUPS * CH
EP = GROUPS * GE
STEPS = GROUPS + TILES - 1
RING = 8
PEEL = 12
NSG = STEPS + 4
NSP = STEPS + 12
BF16 = mybir.dt.bfloat16
TYPES = 9
CROWS = GROUPS // 2
BIG = 1e30
EPS = 1e-5
INV = (1.0 + EPS) ** -0.5
COLS = [(a, min(512, NP - a)) for a in range(0, NP, 512)]
SHARE = 80
AHEAD = 7
assert (STEPS - PEEL) % RING == 0 and NSG % (2 * RING) == 0 and CHUNKS % CROWS == 0

VEC_COLS = ["L2_gnn_vn_emb", "L2_gnn_conv_b1", "L2_gnn_conv_b2", "L2_gnn_bn_gamma", "L2_gnn_bn_beta", "L2_gnn_vn_b1",
            "L2_gnn_vn_g1", "L2_gnn_vn_be1", "L2_gnn_vn_b2", "L2_gnn_vn_g2", "L2_gnn_vn_be2"]
VEC_ROWS = (["L0_gnn_bl1", "L0_gnn_bl2", "L1_gnn_b_ih", "L1_gnn_b_hh"]
            + [f"L3_gnn_{v}{l}" for l in range(3) for v in ("bl", "br", "att", "b", "g", "be")])


def stages():
    yield from [("pool", "constants"), ("dve", "step tables 1"), ("pe", "sum of tile ends"), ("dve", "step tables 2"),
                ("dve", "step order"),                ("sp", "store penalties"), ("pe", "transpose x"), ("act", "x transposed")]
    for l in (1, 2):
        yield ("dve", f"sage {l} edges")
        if l == 1:
            yield from [("pe", "degrees"), ("dve", "one over degree")]
        yield from [("pe", f"sage {l} neighbours"), ("dve", f"sage {l} mean"), ("pe", f"sage {l} self"),
                    ("dve", f"sage {l} add"), ("act", f"sage {l} relu")]
        if l == 2:
            yield ("dve", "sage norm a")
            yield ("act", "sage norm root")
            yield ("dve", "sage norm b")
        yield from [("sp", f"sage {l} table"), ("pe", f"sage {l} transpose"), ("act", f"sage {l} transposed")]
    yield from [("dve", "gru edges"), ("pe", "gru messages"), ("act", "gru messages out"),
                ("pe", "gru r"), ("dve", "gru r bias"), ("act", "gru r gate"),
                ("pe", "gru hn"), ("dve", "gru hn gated"), ("pe", "gru in"), ("dve", "gru in add"), ("act", "gru n"),
                ("pe", "gru z"), ("dve", "gru z bias"), ("act", "gru z gate"), ("dve", "gru norm a"),
                ("act", "gru norm root"), ("dve", "gru norm b"), ("pe", "gru transpose"), ("dve", "gru transposed")]
    for l in range(3):
        yield from [("pe", f"gin {l} rows"), ("act", f"gin {l} rows out"), ("sp", f"gin {l} table"),
                    ("dve", f"gin {l} edges"), ("pe", f"gin {l} up 0"), ("act", f"gin {l} up 0 out"),
                    ("pe", f"gin {l} up 1"), ("act", f"gin {l} up 1 out"), ("pe", f"gin {l} down"),
                    ("act", f"gin {l} down out")]
        if l < 2:
            yield from [("pe", f"gin {l} virtual up"), ("act", f"gin {l} virtual up out"),
                        ("pe", f"gin {l} virtual down"), ("act", f"gin {l} virtual down out")]
        yield ("dve", f"gin {l} residual")
    yield from [("pe", "gin transpose"), ("dve", "gin norm a"), ("act", "gin norm root"), ("dve", "gin norm b")]
    for l in range(3):
        yield from [("pe", f"gat {l} transpose"), ("act", f"gat {l} transposed"), ("pe", f"gat {l} left"),
                    ("dve", f"gat {l} left out"), ("sp", f"gat {l} table"), ("pe", f"gat {l} right"),
                    ("dve", f"gat {l} right out"), ("dve", f"gat {l} edges"), ("dve", f"gat {l} norm a"),
                    ("act", f"gat {l} norm root"), ("dve", f"gat {l} norm b"), ("act", f"gat {l} relu")]
    yield from [("dve", "last norm a"), ("act", "last norm root"), ("dve", "last norm b"), ("sp", "store output")]


ORDER = list(stages())
AT = {name: k for k, (_, name) in enumerate(ORDER)}


def build(nc, a, out):
    ctx = ExitStack()
    with ctx:
        def sb(name, shape, dt=F32):
            return ctx.enter_context(nc.sbuf_tensor(name, shape, dt))

        def sem(name):
            return ctx.enter_context(nc.semaphore(name))

        res = sb("res", [P, NP])
        ht = sb("ht", [P, NP])
        agg = sb("agg", [P, NSP * 16])
        hr = sb("hr", [P, NP])
        w1 = sb("w1", [P, NP])
        w2 = sb("w2", [P, NP])
        xrb = sb("xrb", [P, TILES * 3 * D], BF16)
        xr = xrb[:, :].bitcast(F32)
        cnt = xr[0:TYPES + 1, :]
        rdeg = sb("rdeg", [P, TILES])
        st = sb("st", [P, 4, TILES])
        rden = sb("rden", [P, TILES, 4])
        mx = sb("mx", [P, TILES * 4])

        ident = sb("ident", [P, P])
        iota_d = sb("iota_d", [P, P])
        iota_t = sb("iota_t", [P, TYPES])
        iota_s = sb("iota_s", [P, NSP])
        pcol = sb("pcol", [P, 3])
        ones = sb("ones", [P, P])
        selcnt = sb("selcnt", [TYPES + 1, 1])
        ends, endi, past_g = hr[:, 2000:2000 + GROUPS], hr[0:TILES - 1, 2200:2200 + GROUPS].bitcast(I32), \
            hr[:, 2400:2400 + GROUPS]
        past, gstep = hr[:, 2600:2600 + NSP], hr[:, 2900:2900 + NSP]
        gl = sb("gl", [P, 1])
        tstep = sb("tstep", [P, NSP])
        tile_i = sb("tile_i", [1, NSP], I32)
        group_i = sb("group_i", [1, NSP], I32)
        idx_in = xr[:, 0:4 * CHUNKS].bitcast(I32).rearrange("p (k c) -> p k c", k=4)
        packed = w1[:, 0:GROUPS * 16]
        fields = agg
        fview = fields[:, :].rearrange("p (s f c) -> p s f c", f=4, c=CH)
        src_i = sb("src_i", [P, NSP * CH], I32)
        dloc = sb("dloc", [P, NSP * CH])
        last = sb("last", [P, NSP * CH])
        etype = hr[:, 1024:1024 + NSP * CH]
        src_g = sb("src_g", [P, CHUNKS + 2 * CH], I32)
        taken_g = sb("taken_g", [1, GROUPS])
        taken_i = sb("taken_i", [1, GROUPS], I32)
        need_i = sb("need_i", [1, NSP], I32)
        slot_i = sb("slot_i", [1, NSP], I32)
        RW = CHUNKS // CROWS * P
        rows_i = hr[0:CROWS, 0:RW].bitcast(I32)
        rows_f = w2[0:CROWS, 0:RW]
        pen = w2[0:CROWS, RW:2 * RW]

        Gall = sb("gathered_rows", [P, RING * CH * D])
        G = [Gall[:, i * CH * D:(i + 1) * CH * D] for i in range(RING)]
        OH = [sb(f"OH{i}", [P, CH * P]) for i in range(RING)]
        TOH = [sb(f"TOH{i}", [P, CH, TYPES + 1]) for i in range(2)]
        ea1 = [sb(f"ea1{i}", [65, P]) for i in range(4)]
        pn = [sb(f"pn{i}", [16, P]) for i in range(RING)]
        ea4 = [hr[:, i * P:(i + 1) * P] for i in range(RING)]
        WT = [hr[:, RING * P + i * CH * 132:RING * P + (i + 1) * CH * 132] for i in range(2)]
        spare = [w[:, k * 512:(k + 1) * 512] for w in (w1, w2) for k in range(6)]
        rows = spare[0:RING]
        OHT, msg, lk = spare[0:RING], spare[RING:RING + 2], spare[RING + 2:RING + 4]
        far = hr[:, 2080:2080 + CH * P]
        OHTB = [hr[:, 2592 + i * 256:2592 + (i + 1) * 256].bitcast(BF16) for i in range(2)]
        idx8 = [sb(f"idx8{i}", [P, 2 * CH], I32) for i in range(RING)]
        score = [sb(f"score{i}", [P, 16]) for i in range(4)]
        scanned = sb("scanned", [16, P])
        segrhs = sb("segrhs", [P, CH * 5])
        segout = [sb(f"segout{i}", [P, CH * 5]) for i in range(2)]
        sval = sb("sval", [P, 16])
        smx = sb("smx", [P, 4])
        mnew = sb("mnew", [P, 4])
        mdif = [sb(f"mdif{i}", [P, 4]) for i in range(2)]
        scl = [sb(f"scl{i}", [P, 4]) for i in range(2)]
        delta = sb("delta", [P, 16])
        fall = sb("fall", [P, 16])
        vn = sb("vn", [P, 1])
        vsum = sb("vsum", [P, 1])
        vt = sb("vt", [P, 1])
        vm = sb("vm", [P, 2])
        vs1, vb1 = sb("vs1", [P, 4]), sb("vb1", [P, 4])
        vs2, vb2 = sb("vs2", [P, 2]), sb("vb2", [P, 2])
        bnv = sb("bnv", [P, 6])

        W = {}
        loads = []
        for k in ("L0_gnn_Wl1", "L0_gnn_Wr1", "L0_gnn_Wl2", "L0_gnn_Wr2", "L1_gnn_W_msg", "L1_gnn_W_ih", "L1_gnn_W_hh",
                  "L1_aug", "L2_conv_edge", "L2_gnn_conv_w1", "L2_gnn_conv_w2", "L2_gnn_vn_w1", "L2_gnn_vn_w2",
                  *[f"L3_gnn_{v}{l}" for l in range(3) for v in ("Wl", "Wr", "We")], *[f"col_{v}" for v in VEC_COLS]):
            W[k] = sb("w_" + k, list(a[k].shape))
            loads.append((W[k][:, :], a[k]))
        for k in VEC_ROWS:
            n = a[k].shape[1]
            W[k] = sb("r_" + k, [P, n])
            loads.append((W[k][:, :], a[k].to_broadcast([P, n])))

        ps = ctx.enter_context(nc.psum_tensor("ps", [P, 4096], F32))

        def bank(i, n=512, p=P):
            return ps[0:p, 512 * i:512 * i + n]

        table = nc.dram_tensor("node_table", (NP, D), F32, kind="Internal").ap()
        pen_rows = nc.dram_tensor("penalty_rows", (GROUPS * 16, P), F32, kind="Internal").ap()

        turn = sem("turn")
        loaded = sem("loaded")
        stored = sem("stored")
        dlink = sem("dlink")
        alink = sem("alink")
        plink = sem("plink")
        fcopy = sem("fcopy")
        n_loads = len(loads) + 7

        by_step = [sem(f"gathered_steps{q}") for q in range(RING)]
        by_group = [sem(f"gathered_groups{q}") for q in range(RING)]
        edge_rows_in = [sem(f"edge_rows{q}") for q in range(RING)]
        pairs_begun = sem("pairs_begun")
        lists_made, groups_landed = sem("lists_made"), sem("groups_landed")
        before = dict(rows=0, listed=0)

        def sems(name, layer, *kinds, rows=0):
            d = {k: sem(f"{name}_{k}") for k in ("onehot", "scattered", "added", *kinds)}
            if name[:3] == "gat":
                d["gathered"], d["gathered before"] = by_step, layer * 16 * CH * NSG // RING
            else:
                d["gathered"], d["landed"], d["passes before"] = by_group, groups_landed, len(EDGES)
            d["listed"], d["listed before"] = lists_made, before["listed"]
            before["listed"] += (GROUPS if "landed" in d else NSG) // 2 + 1
            if rows:
                d["edge_data"], d["rows"], d["rows before"] = edge_rows_in, rows, before["rows"]
                before["rows"] += 16 * rows * NSG // RING
            EDGES.append(name)
            return d

        EDGES = []
        SUM = {p: sems(p, 0, "rows_out") for p in ("sage 1 edges", "sage 2 edges", "gru edges")}
        GIN = [sems(f"gin {l} edges", l, "projected", "summed", "rectified", rows=1) for l in range(3)]
        GAT = [sems(f"gat {l} edges", l, "turned", "onehot_t", "projected", "summed", "leaky", "attended", "score",
                    "score_t", "scanned", "scan_back", "seg_rhs", "seg_max", "seg_out", "chunk_max", "step_max", "new_max", "max_drop", "kept",
                    "far", "scale", "max_of_edge", "delta", "fall", "weight", "weighted", "rescaled", rows=2)
               for l in range(3)]
        ALL = [*SUM.values(), *GIN, *GAT]
        HEADS = [4, 4, 1]

        block = ctx.enter_context(nc.Block())

        def held(eng, semaphore, value):
            if not (isinstance(value, int) and value < 1):
                eng.wait_ge(semaphore, value)

        def on(s):
            return not isinstance(s, int) or s >= 0

        def walk(eng, body, ahead=0):
            for s in range(-ahead, PEEL):
                body(s, s % RING)
            with eng.Fori(0, (STEPS - PEEL) // RING) as j:
                for u in range(RING):
                    body(j * RING + (PEEL + u), (PEEL + u) % RING)

        def landed(s, u, S, what):
            n, before = (CH, S["gathered before"]) if what == "gathered" else (S["rows"], S["rows before"])
            return (s - u) * (16 * n // RING) + (16 * n + before)

        @block.sync
        def _(sp):
            idx_names = ("src_cols", "dst_cols", "next_cols", "type_cols")
            for k, name in enumerate(idx_names):
                sp.dma_start(idx_in[:, k, :], a[name]).then_inc(loaded, 16)
            sp.dma_start(endi[:, :], a["dst_ends"].to_broadcast([TILES - 1, GROUPS])).then_inc(loaded, 16)
            sp.dma_start(rows_i[:, :], a["dst_rows"].rearrange("(p k) e -> p (k e)", p=CROWS)).then_inc(loaded, 16)
            sp.dma_start(res[:, :].rearrange("p (t f) -> p t f", f=D),
                         a["x"].rearrange("(t p) f -> p t f", p=P)).then_inc(loaded, 16)
            for dst, src in loads:
                sp.dma_start(dst, src).then_inc(loaded, 16)
            n = 0

            def store(name, dst, src):
                nonlocal n
                sp.wait_ge(turn, AT[name])
                sp.dma_start(dst, src).then_inc(stored, 16)
                n += 16
                sp.wait_ge(stored, n)
                sp.sem_inc(turn, 1)

            def edge_rows(S, l_at, depth, parts):
                sp.wait_ge(turn, AT[l_at])

                def load(s, u):
                    g = sp.value_load(group_i[0:1, bass.ds(s, 1)], min_val=0, max_val=GROUPS - 1)
                    held(sp, S["projected"], s - depth + 1)
                    if "scanned" in S:
                        held(sp, S["scanned"], s - RING + 1)
                    parts(g, u)

                for u in range(RING):
                    load(u, u)
                with sp.Fori(1, NSG // RING) as j:
                    for u in range(RING):
                        load(j * RING + u, u)

            sp.wait_ge(turn, AT["store penalties"])
            pen_dst = pen_rows.rearrange("(p k h c) e -> h p k (c e)", k=2, h=4, c=CH)
            for h in range(4):
                sp.dma_start(pen_dst[h], pen.rearrange("p (k x) -> p k x", k=2)).then_inc(stored, 16)
            n += 64
            sp.wait_ge(stored, n)
            sp.sem_inc(turn, 1)
            t_rows = table.rearrange("(t p) f -> p t f", p=P)
            for l in (1, 2):
                store(f"sage {l} table", t_rows, (hr if l == 1 else res)[:, :].rearrange("p (t f) -> p t f", f=D))
            for l in range(3):
                store(f"gin {l} table", t_rows, hr[:, :].rearrange("p (t f) -> p t f", f=D))

                def gin_parts(g, u, l=l):
                    sp.dma_start(ea1[u % 4][0:64, :], a["ea16"][bass.ds(g * 64, 64), :]).then_inc(GIN[l]["edge_data"][u], 16)

                edge_rows(GIN[l], f"gin {l} edges", 4, gin_parts)
            for l in range(3):
                store(f"gat {l} table", t_rows, hr[:, :].rearrange("p (t f) -> p t f", f=D))
                H = HEADS[l]

                def gat_parts(g, u, l=l, H=H):
                    sp.dma_start(ea4[u][:, :], a["ea32"][bass.ds(g * P, P), :]).then_inc(GAT[l]["edge_data"][u], 16)
                    sp.dma_start(pn[u][0:CH * H, :],
                                 pen_rows[bass.ds(g * 16, CH * H), :]).then_inc(GAT[l]["edge_data"][u], 16)

                edge_rows(GAT[l], f"gat {l} edges", RING, gat_parts)
            t_full = N // P
            sp.wait_ge(turn, AT["store output"])
            sp.dma_start(out[0:t_full * P, :].rearrange("(t p) f -> p t f", p=P),
                         res[:, 0:t_full * D].rearrange("p (t f) -> p t f", f=D)).then_inc(stored, 16)
            sp.dma_start(out[t_full * P:N, :], res[0:N - t_full * P, t_full * D:NP]).then_inc(stored, 16)
            sp.wait_ge(stored, n + 32)

        @block.gpsimd
        def _(pool):
            n = 0

            def link(ins):
                nonlocal n
                n += 1
                ins.then_inc(plink, 1)
                pool.wait_ge(plink, n)

            for m in (ident, ones, selcnt):
                pool.memset(m[:, :], 0.0 if m is not ones else 1.0).then_inc(plink, 1)
                n += 1
            for i in range(2):
                pool.memset(TOH[i][:, :, :], 1.0)
            for i in range(4):
                pool.memset(ea1[i][:, :], 1.0)
            pool.wait_ge(plink, n)
            link(pool.affine_select(out=ident[:, :], in_=ident[:, :], compare_op=ALU.not_equal, fill=1.0, base=0,
                                    pattern=[[-1, P]], channel_multiplier=1))
            link(pool.affine_select(out=selcnt[:, :], in_=selcnt[:, :], compare_op=ALU.not_equal, fill=1.0, base=-TYPES,
                                    pattern=[[0, 1]], channel_multiplier=1))
            exact = dict(allow_small_or_imprecise_dtypes=True)
            pool.iota(iota_d[:, :], [[1, P]], base=0, channel_multiplier=0, **exact)
            pool.iota(iota_t[:, :], [[1, TYPES]], base=0, channel_multiplier=0, **exact)
            pool.iota(iota_s[:, :], [[1, NSP]], base=0, channel_multiplier=0, **exact)
            pool.iota(pcol[:, 0:1], [[0, 1]], base=0, channel_multiplier=1, **exact)
            pool.iota(pcol[:, 1:2], [[0, 1]], base=P, channel_multiplier=P, **exact).then_inc(turn, 1)

            def order_fields(s):
                g = pool.value_load(group_i[0:1, bass.ds(s, 1)], min_val=0, max_val=GROUPS - 1)
                pool.tensor_copy(fields[:, bass.ds(s * 16, 16)], packed[:, bass.ds(g * 16, 16)]).then_inc(fcopy, 1)

            pool.wait_ge(turn, AT["step order"])
            with pool.Fori(0, (NSP - 2 * SHARE) // 8) as j:
                for k in range(8):
                    order_fields(j * 8 + (2 * SHARE + k))

            for S, name in zip(ALL, EDGES):
                src = a["x"] if name == "sage 1 edges" else table
                attention = "rows before" in S and "turned" in S
                index = src_i if attention else src_g
                pool.wait_ge(turn, AT[name])

                def list_rows(k, slot, S=S, index=index):
                    pool.tensor_copy(idx8[slot][:, :], index[:, bass.ds(k * 2 * CH, 2 * CH)]).then_inc(S["listed"], 1)

                def fetch_rows(slot, part, S=S, src=src):
                    for i in range(part * CH, (part + 1) * CH):
                        q = (2 * slot + part) % RING
                        pool.indirect_dma_start(
                            out=G[q][:, (i % CH) * D:(i % CH + 1) * D], out_offset=None, in_=src[:, :],
                            in_offset=bass.IndirectOffsetOnAxis(ap=idx8[slot][:, i:i + 1], axis=0),
                        ).then_inc(S["gathered"][q], 16)

                def fetch_steps(k, slot, S=S, list_rows=list_rows, fetch_rows=fetch_rows):
                    held(pool, S["weighted"], 2 * k + 2 - RING)
                    pool.wait_ge(S["listed"], k + (1 + S["listed before"]))
                    list_rows(k + 1, (slot + 1) % RING)
                    for part in range(2):
                        fetch_rows(slot, part)

                def announce(k, slot, S=S):
                    for part in range(2):
                        q = (2 * slot + part) % RING
                        uses = -(-(GROUPS - q) // RING)
                        pool.wait_ge(S["gathered"][q], (k * 2 + (part - q)) * (16 * CH // RING)
                                     + 16 * CH * (1 + S["passes before"] * uses))
                    pool.sem_inc(S["landed"], 2)

                def fetch_groups(k, slot, S=S, list_rows=list_rows, fetch_rows=fetch_rows, announce=announce):
                    if not (isinstance(k, int) and k < RING // 2):
                        done = pool.value_load(taken_i[0:1, bass.ds(k * 2 + (1 - RING), 1)], min_val=1, max_val=STEPS)
                        pool.wait_ge(S["summed"] if "summed" in S else S["rows_out"], done)
                        pool.sem_inc(pairs_begun, 1)
                    pool.wait_ge(S["listed"], k + (1 + S["listed before"]))
                    list_rows(k + 1, (slot + 1) % RING)
                    fetch_rows(slot, 0)
                    if not (isinstance(k, int) and k < 1):
                        announce(k - 1, (slot - 1) % RING)
                    fetch_rows(slot, 1)

                pairs, fetch = (NSG // 2, fetch_steps) if attention else (GROUPS // 2, fetch_groups)
                peeled = RING + pairs % RING
                list_rows(0, 0)
                for k in range(peeled):
                    fetch(k, k % RING)
                with pool.Fori(0, (pairs - peeled) // RING) as j:
                    for k in range(peeled, peeled + RING):
                        fetch(j * RING + k, k % RING)
                pool.wait_ge(S["listed"], pairs + 1 + S["listed before"])
                if not attention:
                    announce(pairs - 1, (pairs - 1) % RING)

        @block.scalar
        def _(act):
            n = 0

            def stage(name):
                assert ORDER[AT[name]][0] == "act"
                act.wait_ge(turn, AT[name])

            def root(name):
                stage(name)
                act.activation(st[:, 2, :], st[:, 1, :], ACT.Sqrt).then_inc(turn, 1)

            def order_fields(s):
                g = act.value_load(group_i[0:1, bass.ds(s, 1)], min_val=0, max_val=GROUPS - 1)
                act.copy(fields[:, bass.ds(s * 16, 16)], packed[:, bass.ds(g * 16, 16)]).then_inc(fcopy, 1)

            act.wait_ge(turn, AT["step order"])
            with act.Fori(0, SHARE // 8) as j:
                for k in range(8):
                    order_fields(j * 8 + (SHARE + k))

            def copy_rows(name):
                S = SUM[name]
                act.wait_ge(turn, AT[name])

                def body(s, u):
                    need = act.value_load(need_i[0:1, bass.ds(s, 1)], min_val=1, max_val=GROUPS)
                    at = act.value_load(slot_i[0:1, bass.ds(s, 1)], min_val=0, max_val=(RING - 1) * CH * D)
                    held(act, S["scattered"], s - RING + 1)
                    act.wait_ge(S["landed"], need + S["passes before"] * GROUPS)
                    act.copy(rows[u], Gall[:, bass.ds(at, CH * D)]).then_inc(S["rows_out"], 1)

                walk(act, body)

            stage("x transposed")
            act.copy(ht[:, :], ps[:, 0:NP]).then_inc(turn, 1)
            for l in (1, 2):
                copy_rows(f"sage {l} edges")
                stage(f"sage {l} relu")
                act.activation(hr[:, :], w1[:, :], ACT.Relu).then_inc(turn, 1)
                if l == 2:
                    root("sage norm root")
                stage(f"sage {l} transposed")
                act.copy(ht[:, :], ps[:, 0:NP]).then_inc(turn, 1)
            copy_rows("gru edges")
            stage("gru messages out")
            act.copy(w2[:, :], ps[:, 0:NP]).then_inc(turn, 1)
            stage("gru r gate")
            act.activation(w1[:, :], w1[:, :], ACT.Sigmoid).then_inc(turn, 1)
            stage("gru n")
            act.activation(w1[:, :], w1[:, :], ACT.Tanh).then_inc(turn, 1)
            stage("gru z gate")
            act.activation(w2[:, :], w2[:, :], ACT.Sigmoid).then_inc(turn, 1)
            root("gru norm root")
            for l in range(3):
                stage(f"gin {l} rows out")
                act.copy(hr[:, :], ps[:, 0:NP]).then_inc(turn, 1)
                S = GIN[l]
                act.wait_ge(turn, AT[f"gin {l} edges"])

                def rectify(s, u, S=S):
                    act.wait_ge(S["summed"], s + 1)
                    act.activation(rows[u], rows[u], ACT.Relu).then_inc(S["rectified"], 1)

                rectify(0, 0)
                walk(act, lambda s, u, r=rectify: r(s + 1, (u + 1) % RING))
                for k in range(2):
                    stage(f"gin {l} up {k} out")
                    act.activation((w2 if k == 0 else hr)[:, :], ps[:, 0:NP], ACT.Relu,
                                   bias=W["col_L2_gnn_conv_b1"][:, 2 * l + k:2 * l + k + 1]).then_inc(turn, 1)
                stage(f"gin {l} down out")
                act.activation(w1[:, :], ps[:, 0:NP], ACT.Relu if l < 2 else ACT.Identity,
                               scale=bnv[:, 2 * l:2 * l + 1], bias=bnv[:, 2 * l + 1:2 * l + 2]).then_inc(turn, 1)
                if l < 2:
                    stage(f"gin {l} virtual up out")
                    for k in range(2):
                        v = act.activation(vm[:, k:k + 1], ps[:, 512 * k:512 * k + 1], ACT.Relu,
                                           scale=vs1[:, 2 * l + k:2 * l + k + 1], bias=vb1[:, 2 * l + k:2 * l + k + 1])
                    v.then_inc(turn, 1)
                    stage(f"gin {l} virtual down out")
                    act.activation(vt[:, :], ps[:, 0:1], ACT.Relu, scale=vs2[:, l:l + 1],
                                   bias=vb2[:, l:l + 1]).then_inc(turn, 1)
            root("gin norm root")
            for l in range(3):
                H = HEADS[l]
                C = D // H
                S = GAT[l]
                stage(f"gat {l} transposed")
                act.copy(ht[:, :], ps[:, 0:NP]).then_inc(turn, 1)
                act.wait_ge(turn, AT[f"gat {l} edges"])

                def body(s, u, S=S, H=H, C=C, KH=CH * H):
                    if on(s):
                        act.wait_ge(S["max_drop"], s + 1)
                        act.activation(scl[u % 2][:, 0:H], mdif[u % 2][:, 0:H], ACT.Exp).then_inc(S["scale"], 1)
                        act.wait_ge(S["delta"], s + 1)
                        act.activation(fall[:, 0:KH], delta[:, 0:KH], ACT.Relu, scale=-1.0).then_inc(S["fall"], 1)
                        act.wait_ge(S["fall"], s + 1)
                        wt = WT[u % 2][:, 0:KH * (C + 1)].rearrange("p (k c) -> p k c", c=C + 1)
                        act.activation(wt[:, :, C], fall[:, 0:KH], ACT.Exp, scale=-1.0).then_inc(S["weight"], 1)
                    if on(s + 5):
                        act.wait_ge(S["turned"], s + 6)
                        act.copy(OHT[(u + 5) % RING], bank(0))
                        held(act, S["projected"], s + 4)
                        act.copy(OHTB[(u + 1) % 2], bank(0)).then_inc(S["onehot_t"], 1)
                    if on(s + 2):
                        act.wait_ge(S["seg_max"], s + 3)
                        act.copy(segout[u % 2][:, 0:CH * (H + 1)], bank(5, CH * (H + 1))).then_inc(S["seg_out"], 1)
                    held(act, S["onehot"], s + AHEAD)
                    for c in range(CH):
                        act.activation(far[:, c * P:(c + 1) * P], iota_d[:, :], ACT.Abs, scale=-1.0,
                                       bias=dloc[:, bass.ds((s + AHEAD) * CH + c, 1)]).then_inc(S["far"], 1)
                    act.wait_ge(S["far"], (s + AHEAD + 1) * CH)
                    held(act, S["scattered"], s)
                    act.activation(OH[(u + AHEAD) % RING][:, :], far, ACT.Relu, scale=-1.0,
                                   bias=1.0).then_inc(S["onehot"], 1)

                walk(act, body, AHEAD)
                root(f"gat {l} norm root")
                stage(f"gat {l} relu")
                act.activation(w1[:, :], w1[:, :], ACT.Relu).then_inc(turn, 1)
            root("last norm root")

        @block.tensor
        def _(pe):
            def stage(name):
                assert ORDER[AT[name]][0] == "pe"
                pe.wait_ge(turn, AT[name])

            def tiles(f):
                for t in range(TILES):
                    last = f(t)
                last.then_inc(turn, 1)

            def cols(f):
                for c, w in COLS:
                    last = f(c, w)
                last.then_inc(turn, 1)

            def transpose_all(x):
                tiles(lambda t: pe.transpose(ps[:, t * P:(t + 1) * P], x[:, t * P:(t + 1) * P], ident[:, :]))

            def rows_of(xt, w):
                tiles(lambda t: pe.matmul(ps[:, t * P:(t + 1) * P], xt[:, t * P:(t + 1) * P], w, start=True, stop=True))

            def scatter(s, u, S):
                if not (isinstance(s, int) and s < 2):
                    pe.wait_ge(S["added"], s - 1)
                for c in range(CH):
                    m = pe.matmul(bank(u % 2, P), rows[u][:, c * D:(c + 1) * D], OH[u][:, c * P:(c + 1) * P],
                                  start=(c == 0), stop=(c == CH - 1))
                return m

            pe.wait_ge(loaded, 16 * n_loads)
            stage("sum of tile ends")
            pe.matmul(bank(1, GROUPS, 1), ones[0:TILES - 1, 0:1], past_g[0:TILES - 1, :], start=True, stop=True)
            pe.matmul(bank(0, NSP), ones[0:TILES - 1, :], past[0:TILES - 1, :], start=True, stop=True).then_inc(turn, 1)
            stage("transpose x")
            transpose_all(res)
            for l in (1, 2):
                S = SUM[f"sage {l} edges"]
                pe.wait_ge(turn, AT[f"sage {l} edges"])

                def body(s, u, S=S, l=l):
                    pe.wait_ge(S["rows_out"], s + 1)
                    pe.wait_ge(S["onehot"], s + 1)
                    m = scatter(s, u, S)
                    if l == 1:
                        for c in range(CH):
                            m = pe.matmul(bank(2 + u % 2, P, TYPES + 1), TOH[u % 2][:, c, :],
                                          OH[u][:, c * P:(c + 1) * P], start=(c == 0), stop=(c == CH - 1))
                    m.then_inc(S["scattered"], 1)

                walk(pe, body)
                if l == 1:
                    stage("degrees")
                    tiles(lambda t: pe.matmul(ps[:, t:t + 1], cnt[:, t * P:(t + 1) * P], selcnt[:, :],
                                              start=True, stop=True))
                stage(f"sage {l} neighbours")
                rows_of(agg, W[f"L0_gnn_Wl{l}"][:, :])
                stage(f"sage {l} self")
                rows_of(ht, W[f"L0_gnn_Wr{l}"][:, :])
                stage(f"sage {l} transpose")
                transpose_all(hr if l == 1 else res)

            S = SUM["gru edges"]
            pe.wait_ge(turn, AT["gru edges"])

            def body(s, u):
                pe.wait_ge(S["rows_out"], s + 1)
                pe.wait_ge(S["onehot"], s + 1)
                scatter(s, u, S).then_inc(S["scattered"], 1)

            walk(pe, body)
            stage("gru messages")

            def messages(c, w):
                pe.matmul(ps[:, c:c + w], W["L1_gnn_W_msg"][:, :], agg[:, c:c + w], start=True, stop=False)
                return pe.matmul(ps[:, c:c + w], W["L1_aug"][:, :], cnt[:, c:c + w], start=False, stop=True)

            cols(messages)

            def gate(k):
                def f(t):
                    o, i, w = ps[:, t * P:(t + 1) * P], slice(t * P, (t + 1) * P), slice(k * D, (k + 1) * D)
                    pe.matmul(o, w2[:, i], W["L1_gnn_W_ih"][:, w], start=True, stop=False)
                    return pe.matmul(o, ht[:, i], W["L1_gnn_W_hh"][:, w], start=False, stop=True)
                return f

            stage("gru r")
            tiles(gate(0))
            stage("gru hn")
            rows_of(ht, W["L1_gnn_W_hh"][:, 2 * D:3 * D])
            stage("gru in")
            rows_of(w2, W["L1_gnn_W_ih"][:, 2 * D:3 * D])
            stage("gru z")
            tiles(gate(1))
            stage("gru transpose")
            transpose_all(res)

            for l in range(3):
                stage(f"gin {l} rows")
                transpose_all(ht)
                S = GIN[l]
                pe.wait_ge(turn, AT[f"gin {l} edges"])

                def project(s, u, S=S, l=l):
                    pe.wait_ge(S["edge_data"][u], landed(s, u, S, "rows"))
                    if not (isinstance(s, int) and s < 2):
                        pe.wait_ge(S["summed"], s - 1)
                    pe.matmul(bank(2 + u % 2), ea1[u % 4][:, :], W["L2_conv_edge"][:, l * CH * D:(l + 1) * CH * D],
                              start=True, stop=True).then_inc(S["projected"], 1)

                project(0, 0)

                def body(s, u, S=S, project=project):
                    project(s + 1, (u + 1) % RING)
                    pe.wait_ge(S["onehot"], s + 1)
                    pe.wait_ge(S["rectified"], s + 1)
                    scatter(s, u, S).then_inc(S["scattered"], 1)

                walk(pe, body)
                for k in range(2):
                    stage(f"gin {l} up {k}")
                    cols(lambda c, w: pe.matmul(ps[:, c:c + w], W["L2_gnn_conv_w1"][:, (2 * l + k) * D:(2 * l + k + 1) * D],
                                                w1[:, c:c + w], start=True, stop=True))
                stage(f"gin {l} down")

                def down(c, w):
                    o = ps[:, c:c + w]
                    pe.matmul(o, W["L2_gnn_conv_w2"][:, 2 * l * D:(2 * l + 1) * D], w2[:, c:c + w], start=True, stop=False)
                    return pe.matmul(o, W["L2_gnn_conv_w2"][:, (2 * l + 1) * D:(2 * l + 2) * D], hr[:, c:c + w],
                                     start=False, stop=True)

                cols(down)
                if l < 2:
                    stage(f"gin {l} virtual up")
                    for k in range(2):
                        m = pe.matmul(ps[:, 512 * k:512 * k + 1], W["L2_gnn_vn_w1"][:, (2 * l + k) * D:(2 * l + k + 1) * D],
                                      vsum[:, :], start=True, stop=True)
                    m.then_inc(turn, 1)
                    stage(f"gin {l} virtual down")
                    for k in range(2):
                        m = pe.matmul(ps[:, 0:1], W["L2_gnn_vn_w2"][:, (2 * l + k) * D:(2 * l + k + 1) * D],
                                      vm[:, k:k + 1], start=(k == 0), stop=(k == 1))
                    m.then_inc(turn, 1)
            stage("gin transpose")
            transpose_all(w1)

            for l in range(3):
                H = HEADS[l]
                C = D // H
                KH = CH * H
                S = GAT[l]
                stage(f"gat {l} transpose")
                transpose_all(res if l == 0 else w1)
                stage(f"gat {l} left")
                rows_of(ht, W[f"L3_gnn_Wl{l}"][:, :])
                stage(f"gat {l} right")
                rows_of(ht, W[f"L3_gnn_Wr{l}"][:, :])
                pe.wait_ge(turn, AT[f"gat {l} edges"])
                turned, term = bank(0), [bank(1), bank(2)]
                score_t, scan_back, seg_max = bank(3, P, KH), bank(4, KH), bank(5, CH * (H + 1))
                max_of_edge, sums = bank(6, KH), bank(7, H * (C + 1))

                def project(s, u, S=S, l=l):
                    t = pe.value_load(tile_i[0:1, bass.ds(s, 1)], min_val=0, max_val=TILES - 1)
                    right = [xrb[:, bass.ds(t * (3 * D) + k * D, D)] for k in range(3)]
                    pe.wait_ge(S["edge_data"][u], landed(s, u, S, "rows"))
                    held(pe, S["summed"], s - 1)
                    pe.matmul(term[u % 2], ea4[u], W[f"L3_gnn_We{l}"][:, :], start=True, stop=False)
                    pe.wait_ge(S["onehot_t"], s + 1)
                    for c in range(CH):
                        for k in range(3):
                            m = pe.matmul(term[u % 2][:, c * D:(c + 1) * D], OHTB[u % 2][:, c * P:(c + 1) * P],
                                          right[k], start=False, stop=(c == CH - 1 and k == 2))
                    m.then_inc(S["projected"], 1)

                def body(s, u, S=S, H=H, C=C, KH=KH, project=project):
                    if on(s):
                        pe.wait_ge(S["new_max"], s + 1)
                        for c in range(CH):
                            m = pe.matmul(max_of_edge[:, c * H:(c + 1) * H], OHT[u][:, c * P:(c + 1) * P],
                                          mnew[:, 0:H], start=True, stop=True)
                        m.then_inc(S["max_of_edge"], 1)
                    if on(s + 2):
                        pe.wait_ge(S["scanned"], s + 3)
                        pe.matmul(scan_back, scanned[0:KH, :], ident[0:KH, 0:KH], start=True,
                                  stop=True).then_inc(S["scan_back"], 1)
                    if on(s + 5):
                        pe.wait_ge(S["onehot"], s + 6)
                        held(pe, S["onehot_t"], s + 5)
                        for c in range(CH):
                            m = pe.transpose(turned[:, c * P:(c + 1) * P], OH[(u + 5) % RING][:, c * P:(c + 1) * P],
                                             ident[:, :])
                        m.then_inc(S["turned"], 1)
                    if on(s + 4):
                        project(s + 4, (u + 4) % RING)
                    if on(s + 2):
                        pe.wait_ge(S["seg_rhs"], s + 3)
                        held(pe, S["seg_out"], s + 2)
                        for c in range(CH):
                            m = pe.matmul(seg_max[:, c * (H + 1):(c + 1) * (H + 1)],
                                          OH[(u + 2) % RING][:, c * P:(c + 1) * P],
                                          segrhs[:, c * (H + 1):(c + 1) * (H + 1)], start=True, stop=True)
                        m.then_inc(S["seg_max"], 1)
                    if on(s + 3):
                        pe.wait_ge(S["score"], s + 4)
                        pe.transpose(score_t, score[(u + 3) % 4][:, 0:KH], ident[:, :]).then_inc(S["score_t"], 1)
                    if on(s):
                        pe.wait_ge(S["weighted"], s + 1)
                        held(pe, S["added"], s)
                        for c in range(CH):
                            m = pe.matmul(sums, OH[u][:, c * P:(c + 1) * P],
                                          WT[u % 2][:, c * H * (C + 1):(c + 1) * H * (C + 1)],
                                          start=(c == 0), stop=(c == CH - 1))
                        m.then_inc(S["scattered"], 1)

                walk(pe, body, AHEAD)

        @block.vector
        def _(dve):
            n = 0

            def link(ins):
                nonlocal n
                n += 1
                ins.then_inc(dlink, 1)
                dve.wait_ge(dlink, n)

            def stage(name):
                assert ORDER[AT[name]][0] == "dve"
                dve.wait_ge(turn, AT[name])

            def tiled(x, w=D):
                return x.rearrange("p (t f) -> p t f", f=w)

            def per_tile(x):
                return x[:, :, None].to_broadcast([P, TILES, D])

            def per_row(name):
                return W[name][:, None, :].to_broadcast([P, TILES, D])

            def norm_a(name, x):
                link(dve.tensor_reduce(st[:, 0, :], tiled(x), AX.X, ALU.add))
                link(dve.tensor_scalar(st[:, 0, :], st[:, 0, :], -1.0 / D, None, ALU.mult))
                link(dve.tensor_tensor(tiled(x), tiled(x), per_tile(st[:, 0, :]), ALU.add))
                link(dve.tensor_tensor(w2[:, :], x, x, ALU.mult))
                link(dve.tensor_reduce(st[:, 1, :], tiled(w2[:, :]), AX.X, ALU.add))
                dve.tensor_scalar(st[:, 1, :], st[:, 1, :], 1.0 / D, EPS, ALU.mult, ALU.add).then_inc(turn, 1)

            def norm_b(name, dst, x, more=None):
                stage(name)
                link(dve.reciprocal(st[:, 3, :], st[:, 2, :]))
                ins = dve.tensor_tensor(tiled(dst), tiled(x), per_tile(st[:, 3, :]), ALU.mult)
                if more:
                    link(ins)
                    ins = more()
                ins.then_inc(turn, 1)

            def one_hot(s, u, S):
                dve.tensor_tensor(OH[u][:, :].rearrange("p (c d) -> p c d", d=P),
                                  dloc[:, bass.ds(s * CH, CH)][:, :, None].to_broadcast([P, CH, P]),
                                  iota_d[:, None, :].to_broadcast([P, CH, P]), ALU.is_equal).then_inc(S["onehot"], 1)

            def finish(S):
                if "landed" in S:
                    dve.wait_ge(S["landed"], GROUPS * (1 + S["passes before"]))
                for q in range(RING):
                    if "landed" not in S:
                        dve.wait_ge(S["gathered"][q], landed(NSG - RING + q, q, S, "gathered"))
                    if "rows" in S:
                        dve.wait_ge(S["edge_data"][q], landed(NSG - RING + q, q, S, "rows"))
                dve.wait_ge(S["added"], STEPS)
                dve.sem_inc(turn, 1)

            stage("step tables 1")
            dve.wait_ge(loaded, 16 * n_loads)
            link(dve.tensor_copy(ends[0:TILES - 1, :], endi[:, :]))
            link(dve.tensor_scalar(pcol[:, 2:3], pcol[:, 0:1], float(P - 1), None, ALU.is_equal))
            link(dve.tensor_scalar(ends[0:TILES - 1, :], ends[0:TILES - 1, :], pcol[0:TILES - 1, 1:2], None, ALU.is_lt))
            link(dve.tensor_reduce(gl[0:TILES - 1, :], ends[0:TILES - 1, :], AX.X, ALU.add))
            link(dve.tensor_scalar(past_g[0:TILES - 1, :], iota_s[0:TILES - 1, 0:GROUPS], gl[0:TILES - 1, 0:1], None,
                                   ALU.is_ge))
            link(dve.tensor_tensor(gl[0:TILES - 1, :], gl[0:TILES - 1, :], pcol[0:TILES - 1, 0:1], ALU.add))
            dve.tensor_scalar(past[0:TILES - 1, :], iota_s[0:TILES - 1, :], gl[0:TILES - 1, 0:1], None,
                              ALU.is_gt).then_inc(turn, 1)
            stage("step tables 2")
            link(dve.tensor_copy(tstep[:, :], bank(0, NSP)))
            link(dve.tensor_tensor(gstep[:, :], iota_s[:, :], tstep[:, :], ALU.subtract))
            link(dve.tensor_scalar(gstep[:, :], gstep[:, :], float(GROUPS - 1), None, ALU.min))
            link(dve.tensor_copy(tile_i[0:1, :], tstep[0:1, :]))
            link(dve.tensor_copy(group_i[0:1, :], gstep[0:1, :]))
            link(dve.tensor_scalar(gstep[0:1, :], gstep[0:1, :], 1.0, None, ALU.add))
            link(dve.tensor_copy(need_i[0:1, :], gstep[0:1, :]))
            link(dve.tensor_scalar(slot_i[0:1, :], group_i[0:1, :], RING - 1, (CH * D).bit_length() - 1,
                                   ALU.bitwise_and, ALU.logical_shift_left))
            link(dve.tensor_tensor(taken_g[:, :], bank(1, GROUPS, 1), iota_s[0:1, 0:GROUPS], ALU.add))
            link(dve.tensor_scalar(taken_i[:, :], taken_g[:, :], 1.0, None, ALU.add))
            link(dve.memset(src_g[:, CHUNKS:CHUNKS + 2 * CH], 0))
            link(dve.tensor_copy(src_g[:, 0:CHUNKS], idx_in[:, 0, :]))
            pk = packed.rearrange("p (g f c) -> p f g c", f=4, c=CH)

            def chunks(k):
                return idx_in[:, k, :].rearrange("p (g c) -> p g c", c=CH)

            link(dve.tensor_copy(pk[:, 0], chunks(0)))
            link(dve.tensor_copy(pk[:, 1], chunks(1)))
            link(dve.tensor_copy(pk[:, 3], chunks(3)))
            link(dve.tensor_copy(pk[:, 2], chunks(2)))
            link(dve.tensor_tensor(pk[:, 2], pk[:, 2], pk[:, 1], ALU.not_equal))
            link(dve.tensor_scalar(pk[:, 2], pk[:, 2], pcol[:, 2:3], None, ALU.max))
            dve.tensor_scalar(pk[:, 3], pk[:, 3], 0.0, float(TYPES - 1), ALU.max, ALU.min).then_inc(turn, 1)
            stage("step order")

            def order_fields(s):
                g = dve.value_load(group_i[0:1, bass.ds(s, 1)], min_val=0, max_val=GROUPS - 1)
                dve.tensor_copy(fields[:, bass.ds(s * 16, 16)], packed[:, bass.ds(g * 16, 16)]).then_inc(fcopy, 1)

            with dve.Fori(0, SHARE // 8) as j:
                for k in range(8):
                    order_fields(j * 8 + k)
            dve.wait_ge(fcopy, NSP)

            def stepped(x):
                return x[:, :].rearrange("p (s c) -> p s c", c=CH)

            dve.tensor_copy(stepped(src_i), fview[:, :, 0])
            dve.tensor_copy(stepped(last), fview[:, :, 2])
            dve.tensor_copy(stepped(etype), fview[:, :, 3])
            link(dve.tensor_scalar(tstep[:, :], tstep[:, :], float(P), None, ALU.mult))
            link(dve.tensor_tensor(stepped(dloc), fview[:, :, 1], tstep[:, :, None].to_broadcast([P, NSP, CH]),
                                   ALU.subtract))
            rv, pv = rows_f.rearrange("p (k e) -> p k e", e=P), pen.rearrange("p (k e) -> p k e", e=P)
            link(dve.tensor_copy(rows_f, rows_i[:, :]))
            link(dve.memset(pv[:, :, 0:1], -BIG))
            link(dve.tensor_tensor(pv[:, :, 1:P], rv[:, :, 1:P], rv[:, :, 0:P - 1], ALU.is_equal))
            link(dve.tensor_scalar(pv[:, :, 1:P], pv[:, :, 1:P], 1.0, BIG, ALU.subtract, ALU.mult))
            V = {k[7:]: W["col_" + k] for k in VEC_COLS}
            for l in range(3):
                link(dve.tensor_scalar(bnv[:, 2 * l:2 * l + 1], V["bn_gamma"][:, l:l + 1], INV, None, ALU.mult))
                link(dve.tensor_tensor(bnv[:, 2 * l + 1:2 * l + 2], V["conv_b2"][:, l:l + 1], bnv[:, 2 * l:2 * l + 1],
                                       ALU.mult))
                link(dve.tensor_tensor(bnv[:, 2 * l + 1:2 * l + 2], bnv[:, 2 * l + 1:2 * l + 2],
                                       V["bn_beta"][:, l:l + 1], ALU.add))
            for scale, bias, g, b, be in ((vs1, vb1, "vn_g1", "vn_b1", "vn_be1"), (vs2, vb2, "vn_g2", "vn_b2", "vn_be2")):
                link(dve.tensor_scalar(scale[:, :], V[g][:, :], INV, None, ALU.mult))
                link(dve.tensor_tensor(bias[:, :], V[b][:, :], scale[:, :], ALU.mult))
                link(dve.tensor_tensor(bias[:, :], bias[:, :], V[be][:, :], ALU.add))
            dve.tensor_copy(vn[:, :], V["vn_emb"][:, :]).then_inc(turn, 1)

            def sum_pass(S, first=False):
                link(dve.memset(agg[:, 0:NP], 0.0))
                if first:
                    link(dve.memset(cnt[:, :], 0.0))

                def one_hot_all(s, u):
                    if first:
                        dve.tensor_tensor(TOH[u % 2][:, :, 0:TYPES],
                                          etype[:, bass.ds(s * CH, CH)][:, :, None].to_broadcast([P, CH, TYPES]),
                                          iota_t[:, None, :].to_broadcast([P, CH, TYPES]), ALU.is_equal)
                    one_hot(s, u, S)

                one_hot_all(0, 0)

                def body(s, u):
                    one_hot_all(s + 1, (u + 1) % RING)
                    add_sums(s, u, S, first)

                walk(dve, body)
                finish(S)

            def add_sums(s, u, S, first=False):
                t = dve.value_load(tile_i[0:1, bass.ds(s, 1)], min_val=0, max_val=TILES - 1)
                if not (isinstance(s, int) and s < 1):
                    dve.wait_ge(S["added"], s)
                dve.wait_ge(S["scattered"], s + 1)
                w = agg[:, bass.ds(t * P, P)]
                if first:
                    cw = cnt[:, bass.ds(t * P, P)]
                    dve.tensor_tensor(cw, cw, bank(2 + u % 2, P, TYPES + 1), ALU.add)
                dve.tensor_tensor(w, w, bank(u % 2, P), ALU.add).then_inc(S["added"], 1)

            for l in (1, 2):
                stage(f"sage {l} edges")
                sum_pass(SUM[f"sage {l} edges"], first=(l == 1))
                if l == 1:
                    stage("one over degree")
                    link(dve.tensor_scalar(rdeg[:, :], ps[:, 0:TILES], 1.0, None, ALU.max))
                    dve.reciprocal(rdeg[:, :], rdeg[:, :]).then_inc(turn, 1)
                stage(f"sage {l} mean")
                link(dve.tensor_tensor(tiled(w1[:, :]), tiled(ps[:, 0:NP]), per_tile(rdeg[:, :]), ALU.mult))
                dve.tensor_tensor(tiled(w1[:, :]), tiled(w1[:, :]), per_row(f"L0_gnn_bl{l}"), ALU.add).then_inc(turn, 1)
                stage(f"sage {l} add")
                dve.tensor_tensor(w1[:, :], w1[:, :], ps[:, 0:NP], ALU.add).then_inc(turn, 1)
            stage("sage norm a")
            link(dve.tensor_tensor(w1[:, :], hr[:, :], res[:, :], ALU.add))
            norm_a("sage", w1[:, :])
            norm_b("sage norm b", res[:, :], w1[:, :])

            stage("gru edges")
            sum_pass(SUM["gru edges"])
            bih, bhh = W["L1_gnn_b_ih"], W["L1_gnn_b_hh"]

            def gate_bias(b, k):
                return b[:, k * D:(k + 1) * D][:, None, :].to_broadcast([P, TILES, D])

            stage("gru r bias")
            link(dve.tensor_tensor(tiled(w1[:, :]), tiled(ps[:, 0:NP]), gate_bias(bih, 0), ALU.add))
            dve.tensor_tensor(tiled(w1[:, :]), tiled(w1[:, :]), gate_bias(bhh, 0), ALU.add).then_inc(turn, 1)
            stage("gru hn gated")
            link(dve.tensor_tensor(tiled(hr[:, :]), tiled(ps[:, 0:NP]), gate_bias(bhh, 2), ALU.add))
            dve.tensor_tensor(w1[:, :], w1[:, :], hr[:, :], ALU.mult).then_inc(turn, 1)
            stage("gru in add")
            link(dve.tensor_tensor(w1[:, :], w1[:, :], ps[:, 0:NP], ALU.add))
            dve.tensor_tensor(tiled(w1[:, :]), tiled(w1[:, :]), gate_bias(bih, 2), ALU.add).then_inc(turn, 1)
            stage("gru z bias")
            link(dve.tensor_tensor(tiled(w2[:, :]), tiled(ps[:, 0:NP]), gate_bias(bih, 1), ALU.add))
            dve.tensor_tensor(tiled(w2[:, :]), tiled(w2[:, :]), gate_bias(bhh, 1), ALU.add).then_inc(turn, 1)
            stage("gru norm a")
            link(dve.tensor_tensor(hr[:, :], res[:, :], w1[:, :], ALU.subtract))
            link(dve.tensor_tensor(hr[:, :], hr[:, :], w2[:, :], ALU.mult))
            link(dve.tensor_tensor(hr[:, :], hr[:, :], w1[:, :], ALU.add))
            link(dve.tensor_tensor(w1[:, :], hr[:, :], res[:, :], ALU.add))
            norm_a("gru", w1[:, :])
            norm_b("gru norm b", res[:, :], w1[:, :])

            def node_sum():
                link(dve.tensor_reduce(vsum[:, :], ht[:, 0:N], AX.X, ALU.add))
                return dve.tensor_tensor(vsum[:, :], vsum[:, :], vn[:, :], ALU.add)

            stage("gru transposed")
            link(dve.tensor_scalar(ht[:, :], ps[:, 0:NP], vn[:, 0:1], None, ALU.add))
            node_sum().then_inc(turn, 1)
            for l in range(3):
                S = GIN[l]
                stage(f"gin {l} edges")
                link(dve.memset(agg[:, 0:NP], 0.0))

                def add_term(s, u, S=S):
                    need = dve.value_load(need_i[0:1, bass.ds(s, 1)], min_val=1, max_val=GROUPS)
                    at = dve.value_load(slot_i[0:1, bass.ds(s, 1)], min_val=0, max_val=(RING - 1) * CH * D)
                    dve.wait_ge(S["landed"], need + S["passes before"] * GROUPS)
                    dve.wait_ge(S["projected"], s + 1)
                    dve.tensor_tensor(rows[u], Gall[:, bass.ds(at, CH * D)], bank(2 + u % 2),
                                      ALU.add).then_inc(S["summed"], 1)

                one_hot(0, 0, S)
                add_term(0, 0)

                def body(s, u, S=S, add_term=add_term):
                    one_hot(s + 1, (u + 1) % RING, S)
                    add_term(s + 1, (u + 1) % RING)
                    add_sums(s, u, S)

                walk(dve, body)
                dve.wait_ge(S["rectified"], STEPS + 1)
                dve.wait_ge(S["added"], STEPS)
                link(dve.tensor_tensor(w1[:, :], agg[:, 0:NP], ht[:, :], ALU.add))
                finish(S)
                stage(f"gin {l} residual")
                if l < 2:
                    link(dve.tensor_tensor(vn[:, :], vn[:, :], vt[:, :], ALU.add))
                    link(dve.tensor_tensor(w1[:, :], w1[:, :], ht[:, :], ALU.add))
                    link(dve.tensor_scalar(ht[:, :], w1[:, :], vn[:, 0:1], None, ALU.add))
                    node_sum().then_inc(turn, 1)
                else:
                    dve.tensor_tensor(w1[:, :], w1[:, :], ht[:, :], ALU.add).then_inc(turn, 1)
            stage("gin norm a")
            link(dve.tensor_tensor(w1[:, :], ps[:, 0:NP], res[:, :], ALU.add))
            norm_a("gin", w1[:, :])
            norm_b("gin norm b", res[:, :], w1[:, :])

            for l in range(3):
                H = HEADS[l]
                C = D // H
                KH = CH * H
                HC = H * (C + 1)
                S = GAT[l]
                stage(f"gat {l} left out")
                dve.tensor_tensor(tiled(hr[:, :]), tiled(ps[:, 0:NP]), per_row(f"L3_gnn_bl{l}"), ALU.add).then_inc(turn, 1)
                stage(f"gat {l} right out")
                link(dve.tensor_tensor(tiled(w1[:, :]), tiled(ps[:, 0:NP]), per_row(f"L3_gnn_br{l}"), ALU.add))
                parts = xrb[:, :].rearrange("p (t k f) -> p k t f", k=3, f=D)
                link(dve.tensor_copy(parts[:, 0], tiled(w1[:, :])))
                for k in (1, 2):
                    link(dve.tensor_tensor(tiled(w1[:, :]), tiled(w1[:, :]), parts[:, k - 1], ALU.subtract))
                    ins = dve.tensor_copy(parts[:, k], tiled(w1[:, :]))
                    if k == 1:
                        link(ins)
                ins.then_inc(turn, 1)
                stage(f"gat {l} edges")
                link(dve.memset(agg[:, 0:TILES * HC], 0.0))
                link(dve.memset(mx[:, :], -BIG))
                term = [bank(1), bank(2)]
                score_t, scan_back, seg_max = bank(3, P, KH), bank(4, KH), bank(5, CH * (H + 1))
                max_of_edge, sums = bank(6, KH), bank(7, HC)
                att = W[f"L3_gnn_att{l}"]

                def tile_of(s):
                    return dve.value_load(tile_i[0:1, bass.ds(s, 1)], min_val=0, max_val=TILES - 1)

                def by_chunk(x, heads_first=False):
                    return x.rearrange("p (h c) -> p c h" if heads_first else "p (c h) -> p c h", c=CH)

                def chunk_max(s, u):
                    so = by_chunk(segout[u % 2][:, 0:CH * (H + 1)])
                    dve.wait_ge(S["seg_out"], s + 1)
                    dve.scalar_tensor_tensor(out=by_chunk(sval[:, 0:KH]), in0=so[:, :, H:H + 1].to_broadcast([P, CH, H]),
                                             scalar=-BIG, in1=so[:, :, 0:H], op0=ALU.add,
                                             op1=ALU.min).then_inc(S["chunk_max"], 1)

                def step_max(s, u):
                    dve.wait_ge(S["chunk_max"], s + 1)
                    dve.tensor_reduce(smx[:, 0:H], sval[:, 0:KH].rearrange("p (c h) -> p h c", c=CH), AX.X,
                                      ALU.max).then_inc(S["step_max"], 1)

                tile_max = {}

                def new_max(s, u):
                    tile_max[0] = mt = mx[:, bass.ds(tile_of(s) * 4, H)]
                    held(dve, S["kept"], s)
                    dve.wait_ge(S["step_max"], s + 1)
                    dve.tensor_tensor(mnew[:, 0:H], smx[:, 0:H], mt, ALU.max).then_inc(S["new_max"], 1)

                def max_drop(s, u):
                    dve.wait_ge(S["new_max"], s + 1)
                    dve.tensor_tensor(mdif[u % 2][:, 0:H], tile_max[0], mnew[:, 0:H],
                                      ALU.subtract).then_inc(S["max_drop"], 1)

                def keep_max(s, u):
                    dve.wait_ge(S["max_drop"], s + 1)
                    dve.tensor_scalar(tile_max[0], mnew[:, 0:H], 1.0, None, ALU.mult).then_inc(S["kept"], 1)

                def add_terms(s, u):
                    dve.wait_ge(S["gathered"][u], landed(s, u, S, "gathered"))
                    dve.wait_ge(S["projected"], s + 1)
                    dve.tensor_tensor(msg[u % 2], G[u][:, :], term[u % 2], ALU.add).then_inc(S["summed"], 1)

                def scan(s, u):
                    dve.wait_ge(S["score_t"], s + 1)
                    dve.tensor_tensor_scan(out=scanned[0:KH, :], data0=pn[u][0:KH, :], data1=score_t, initial=-BIG,
                                           op0=ALU.add, op1=ALU.max).then_inc(S["scanned"], 1)

                def leak(s, u):
                    dve.wait_ge(S["summed"], s + 1)
                    dve.scalar_tensor_tensor(out=lk[u % 2], in0=msg[u % 2], scalar=0.2, in1=msg[u % 2], op0=ALU.mult,
                                             op1=ALU.max).then_inc(S["leaky"], 1)

                def attend(s, u):
                    dve.wait_ge(S["leaky"], s + 1)
                    x = lk[u % 2].rearrange("p (c f) -> p c f", f=D)
                    dve.tensor_tensor(x, x, att[:, None, :].to_broadcast([P, CH, D]), ALU.mult).then_inc(S["attended"], 1)

                def sum_scores(s, u):
                    dve.wait_ge(S["attended"], s + 1)
                    dve.tensor_reduce(by_chunk(score[u % 4][:, 0:KH], True),
                                      lk[u % 2].rearrange("p (c h k) -> p c h k", c=CH, h=H), AX.X,
                                      ALU.add).then_inc(S["score"], 1)

                def below_max(s, u):
                    dve.wait_ge(S["max_of_edge"], s + 1)
                    dve.tensor_tensor(by_chunk(delta[:, 0:KH]), by_chunk(score[u % 4][:, 0:KH], True),
                                      by_chunk(max_of_edge), ALU.subtract).then_inc(S["delta"], 1)

                def seg_rhs(s, u):
                    rhs = by_chunk(segrhs[:, 0:CH * (H + 1)])
                    lst = last[:, bass.ds(s * CH, CH)]
                    dve.wait_ge(S["scan_back"], s + 1)
                    dve.tensor_scalar(rhs[:, :, H], lst, 2 * BIG, None, ALU.mult)
                    dve.tensor_tensor(rhs[:, :, 0:H], by_chunk(scan_back, True),
                                      lst[:, :, None].to_broadcast([P, CH, H]), ALU.mult).then_inc(S["seg_rhs"], 1)

                def rescale(s, u):
                    tile_sums[0] = w = agg[:, bass.ds(tile_of(s) * HC, HC)]
                    held(dve, S["added"], s)
                    dve.wait_ge(S["scale"], s + 1)
                    wh = w.rearrange("p (h c) -> p h c", h=H)
                    dve.tensor_tensor(wh, wh, scl[u % 2][:, 0:H, None].to_broadcast([P, H, C + 1]),
                                      ALU.mult).then_inc(S["rescaled"], 1)

                tile_sums = {}

                def take_sums(s, u):
                    dve.wait_ge(S["rescaled"], s + 1)
                    dve.wait_ge(S["scattered"], s + 1)
                    dve.tensor_tensor(tile_sums[0], tile_sums[0], sums, ALU.add).then_inc(S["added"], 1)

                def weigh(s, u):
                    dve.wait_ge(S["weight"], s + 1)
                    wt = WT[u % 2][:, 0:KH * (C + 1)].rearrange("p (k c) -> p k c", c=C + 1)
                    dve.tensor_tensor(wt[:, :, 0:C], G[u][:, :].rearrange("p (k c) -> p k c", c=C),
                                      wt[:, :, C:C + 1].to_broadcast([P, KH, C]), ALU.mult).then_inc(S["weighted"], 1)

                plan = [(new_max, 0), (add_terms, 3), (max_drop, 0), (scan, 2), (rescale, -1), (leak, 3), (keep_max, 0),
                        (below_max, 0), (attend, 3), (chunk_max, 1), (seg_rhs, 2), (step_max, 1), (sum_scores, 3),
                        (take_sums, -1), (weigh, 0)]

                def body(s, u):
                    for work, k in plan:
                        if on(s + k):
                            work(s + k, (u + k) % RING)

                walk(dve, body, AHEAD)
                rescale(STEPS - 1, (STEPS - 1) % RING)
                take_sums(STEPS - 1, (STEPS - 1) % RING)
                for k, more in (("projected", 4), ("turned", 5), ("onehot_t", 5), ("onehot", AHEAD), ("seg_out", 2),
                                ("score_t", 3), ("scan_back", 2)):
                    dve.wait_ge(S[k], STEPS + more)
                finish(S)

                stage(f"gat {l} norm a")
                av = agg[:, 0:TILES * HC].rearrange("p (t h c) -> p t h c", h=H, c=C + 1)
                rd = rden[:, :, 0:H]
                link(dve.tensor_scalar(rd, av[:, :, :, C], 1e-30, None, ALU.max))
                link(dve.reciprocal(rd, rd))
                for h in range(H):
                    link(dve.tensor_tensor(tiled(w1[:, :])[:, :, h * C:(h + 1) * C], av[:, :, h, 0:C],
                                           rden[:, :, h:h + 1].to_broadcast([P, TILES, C]), ALU.mult))
                link(dve.tensor_tensor(tiled(w1[:, :]), tiled(w1[:, :]), per_row(f"L3_gnn_b{l}"), ALU.add))
                norm_a("gat", w1[:, :])

                def affine(l=l):
                    link(dve.tensor_tensor(tiled(w1[:, :]), tiled(w1[:, :]), per_row(f"L3_gnn_g{l}"), ALU.mult))
                    return dve.tensor_tensor(tiled(w1[:, :]), tiled(w1[:, :]), per_row(f"L3_gnn_be{l}"), ALU.add)

                norm_b(f"gat {l} norm b", w1[:, :], w1[:, :], affine)
            stage("last norm a")
            link(dve.tensor_tensor(w1[:, :], w1[:, :], res[:, :], ALU.add))
            norm_a("last", w1[:, :])
            norm_b("last norm b", res[:, :], w1[:, :])


def kernel(**inputs):
    import numpy as np
    import concourse.bacc as bacc
    from concourse.bass_utils import run_bass_kernel_spmd

    inp = {k: np.asarray(v) for k, v in inputs.items()}
    host = {}

    def pad(v, n, fill):
        return np.concatenate([v, np.full((n - len(v),) + v.shape[1:], fill, v.dtype)])

    def columns(v):
        return v.reshape(CHUNKS, P).T

    dst = pad(inp["dst"], EP + 1, 1 << 20)
    host["x"] = pad(inp["x"], NP, 0)
    host["src_cols"] = columns(pad(inp["src"], EP, 0))
    host["dst_cols"] = columns(dst[:EP])
    host["next_cols"] = columns(dst[1:])
    host["type_cols"] = columns(pad(inp["edge_type_9"], EP, 0))
    host["dst_rows"] = dst[:EP].reshape(CHUNKS, P)
    host["dst_ends"] = dst[GE - 1:EP:GE].reshape(1, GROUPS)
    host["ea16"] = pad(inp["edge_attr_16"], EP, 0).reshape(CHUNKS, P, 16).transpose(0, 2, 1).reshape(CHUNKS * 16, P)
    host["ea32"] = pad(inp["edge_attr_32"], EP, 0).reshape(CHUNKS, P, 32).transpose(0, 2, 1).reshape(CHUNKS * 32, P)
    for k in ("L0_gnn_Wl1", "L0_gnn_Wr1", "L0_gnn_Wl2", "L0_gnn_Wr2",
              *[f"L3_gnn_{v}{l}" for l in range(3) for v in ("Wl", "Wr")]):
        host[k] = inp[k]

    def blocks(w):
        b = np.zeros((CH, w.shape[0], CH, D), w.dtype)
        for c in range(CH):
            b[c, :, c] = w
        return b.reshape(-1, CH * D)

    for l in range(3):
        host[f"L3_gnn_We{l}"] = blocks(inp[f"L3_gnn_We{l}"])
    for k in ("L1_gnn_W_msg", "L1_gnn_W_ih", "L1_gnn_W_hh"):
        host[k] = inp[k].T
    host["L1_aug"] = np.concatenate([inp["L1_gnn_edge_embed"], inp["L1_gnn_b_msg"][None]])
    host["L2_conv_edge"] = np.concatenate([np.concatenate([blocks(inp["L2_gnn_conv_edge_w"][l]),
                                                           np.tile(inp["L2_gnn_conv_edge_b"][l], CH)[None]])
                                           for l in range(3)], 1)
    for k in ("L2_gnn_conv_w1", "L2_gnn_vn_w1"):
        host[k] = inp[k].transpose(1, 0, 2).reshape(D, -1)
    for k in ("L2_gnn_conv_w2", "L2_gnn_vn_w2"):
        host[k] = inp[k].reshape(-1, 2, D, D).transpose(2, 0, 1, 3).reshape(D, -1)
    for k in VEC_COLS:
        host["col_" + k] = inp[k].reshape(-1, D).T
    for k in VEC_ROWS:
        host[k] = inp[k].reshape(1, -1)

    nc = bacc.Bacc("TRN2", target_bir_lowering=False, num_devices=1)
    arrays, args = {}, {}
    for name, v in host.items():
        v = np.ascontiguousarray(v)
        arrays[f"in_{name}"] = v
        args[name] = nc.dram_tensor(f"in_{name}", v.shape, mybir.dt.from_np(v.dtype), kind="ExternalInput").ap()
    out = nc.dram_tensor("out", (N, D), F32, kind="ExternalOutput").ap()
    build(nc, args, out)
    r = run_bass_kernel_spmd(nc, [arrays], core_ids=[0])
    return r.results[0]["out"]
```

```python
import concourse.bass as bass
from concourse import mybir
from contextlib import ExitStack

F32, I32 = mybir.dt.float32, mybir.dt.int32
ALU, ACT, AX = mybir.AluOpType, mybir.ActivationFunctionType, mybir.AxisListType

P = 128
D = 128
N, E = 3125, 100000
TILES = -(-N // P)
NP = TILES * P
CH = 4
GE = CH * P
GROUPS = -(-E // GE)
CHUNKS = GROUPS * CH
EP = GROUPS * GE
STEPS = GROUPS + TILES - 1
RING = 8
PEEL = 12
NSG = STEPS + 4
NSP = STEPS + 12
BF16 = mybir.dt.bfloat16
TYPES = 9
CROWS = GROUPS // 2
BIG = 1e30
EPS = 1e-5
INV = (1.0 + EPS) ** -0.5
COLS = [(a, min(512, NP - a)) for a in range(0, NP, 512)]
DVE_SHARE, ACT_SHARE = 72, 96
AHEAD = 7
assert (STEPS - PEEL) % (2 * RING) == 0 and NSG % (2 * RING) == 0 and CHUNKS % CROWS == 0

VEC_COLS = ["L2_gnn_vn_emb", "L2_gnn_conv_b1", "L2_gnn_conv_b2", "L2_gnn_bn_gamma", "L2_gnn_bn_beta", "L2_gnn_vn_b1",
            "L2_gnn_vn_g1", "L2_gnn_vn_be1", "L2_gnn_vn_b2", "L2_gnn_vn_g2", "L2_gnn_vn_be2", "L1_gnn_b_ih", "L1_gnn_b_hh",
            "L3_gnn_g0", "L3_gnn_be0", "L3_gnn_g1", "L3_gnn_be1"]
VEC_ROWS = (["L0_gnn_bl1", "L0_gnn_bl2", "L3_gnn_g2", "L3_gnn_be2"]
            + [f"L3_gnn_{v}{l}" for l in range(3) for v in ("bl", "br", "att", "b")])


def stages():
    whole = lambda *names: [(*n, False) for n in names]
    pieces = lambda *names: [(*n, True) for n in names]

    def norm(name):
        return pieces(("dve", f"{name} norm stats"), ("act", f"{name} norm root"), ("dve", f"{name} norm out"))

    yield from whole(("pool", "constants"), ("dve", "step tables 1"), ("pe", "sum of tile ends"),
                     ("dve", "step tables 2"))
    yield from pieces(("pe", "transpose x"), ("act", "x transposed"))
    yield from whole(("dve", "step order"))
    for l in (1, 2):
        yield from whole(("dve", f"sage {l} edges"))
        if l == 1:
            yield from whole(("pe", "degrees"), ("dve", "one over degree"))
        yield from pieces(("pe", f"sage {l} neighbours"), ("dve", f"sage {l} mean"), ("pe", f"sage {l} self"),
                          ("dve", f"sage {l} add"), ("act", f"sage {l} relu"))
        if l == 2:
            yield from norm("sage")
        yield from pieces(("pe", f"sage {l} transpose"), ("act", f"sage {l} transposed"))
    yield from whole(("dve", "gru edges"))
    yield from pieces(("pe", "gru messages"), ("act", "gru messages out"), ("pe", "gru r"), ("act", "gru r gate"),
                      ("pe", "gru hn"), ("dve", "gru hn gated"), ("pe", "gru in"), ("dve", "gru in add"),
                      ("act", "gru n"), ("pe", "gru z"), ("act", "gru z gate"), ("dve", "gru state"),
                      ("pe", "gru state rows"))
    yield from norm("gru")
    yield from pieces(("pe", "gru transpose"), ("act", "gru transposed"))
    for l in range(3):
        yield from pieces(("pe", f"gin {l} rows"), ("act", f"gin {l} rows out"))
        yield from whole(("dve", f"gin {l} edges"))
        if l < 2:
            yield from whole(("pe", f"gin {l} virtual up"), ("act", f"gin {l} virtual up out"),
                             ("pe", f"gin {l} virtual down"), ("act", f"gin {l} virtual down out"),
                             ("dve", f"gin {l} virtual node"))
        yield from pieces(("dve", f"gin {l} add"), ("pe", f"gin {l} up 0"), ("act", f"gin {l} up 0 out"),
                          ("pe", f"gin {l} up 1"), ("act", f"gin {l} up 1 out"), ("pe", f"gin {l} down"),
                          ("act", f"gin {l} down out"), ("dve", f"gin {l} residual"))
    yield from pieces(("pe", "gin transpose"))
    yield from norm("gin")
    for l in range(3):
        yield from pieces(("pe", f"gat {l} transpose"), ("act", f"gat {l} transposed"), ("pe", f"gat {l} left"),
                          ("dve", f"gat {l} left out"), ("pe", f"gat {l} right"), ("dve", f"gat {l} right out"),
                          ("act", f"gat {l} right part 0"), ("dve", f"gat {l} right rest 1"),
                          ("act", f"gat {l} right part 1"), ("dve", f"gat {l} right rest 2"),
                          ("act", f"gat {l} right part 2"))
        yield from whole(("dve", f"gat {l} edges"))
        yield from norm(f"gat {l}")
    yield from pieces(("dve", "gat 2 affine"), ("act", "gat 2 relu"))
    yield from norm("last")


ORDER = list(stages())
ENGINE = {name: engine for engine, name, _ in ORDER}
TURNS = {name: sum(not s[2] for s in ORDER[:k]) for k, (_, name, _) in enumerate(ORDER)}
PIECES = {name: sum(s[2] for s in ORDER[:k]) for k, (_, name, _) in enumerate(ORDER)}


def build(nc, a, out):
    ctx = ExitStack()
    with ctx:
        def sb(name, shape, dt=F32):
            return ctx.enter_context(nc.sbuf_tensor(name, shape, dt))

        def sem(name):
            return ctx.enter_context(nc.semaphore(name))

        res = sb("res", [P, NP])
        ht = sb("ht", [P, NP])
        agg = sb("agg", [P, NSP * 16])
        hr = sb("hr", [P, NP])
        w1 = sb("w1", [P, NP])
        w2 = sb("w2", [P, NP])
        xrb = sb("xrb", [P, TILES * 3 * D], BF16)
        right_parts = xrb[:, :].rearrange("p (t k f) -> p k t f", k=3, f=D)
        xr = xrb[:, :].bitcast(F32)
        cnt = xr[0:TYPES + 1, :]
        rdeg = sb("rdeg", [P, TILES])
        halves = sb("halves", [P, TILES, 6])
        st = sb("st", [P, TILES, 2])
        root, rstd = sb("root", [P, TILES]), sb("rstd", [P, TILES])
        eps = sb("eps", [P, 1])
        rden = sb("rden", [P, TILES, 4])
        mx = sb("mx", [P, TILES * 4])

        ident = sb("ident", [P, P])
        identb = sb("identb", [P, P], BF16)
        iota_d = sb("iota_d", [P, P])
        iota_t = sb("iota_t", [P, TYPES])
        iota_s = sb("iota_s", [P, NSP])
        pcol = sb("pcol", [P, 3])
        ones = sb("ones", [P, P])
        selcnt = sb("selcnt", [TYPES + 1, 1])
        ends, endi, past_g = hr[:, 2000:2000 + GROUPS], hr[0:TILES - 1, 2200:2200 + GROUPS].bitcast(I32), \
            hr[:, 2400:2400 + GROUPS]
        past, gstep = hr[:, 2600:2600 + NSP], hr[:, 2900:2900 + NSP]
        gl = sb("gl", [P, 1])
        tstep = sb("tstep", [P, NSP])
        tile_i = sb("tile_i", [1, NSP], I32)
        group_i = sb("group_i", [1, NSP], I32)
        idx_in = xr[:, 0:3 * CHUNKS].bitcast(I32).rearrange("p (k c) -> p k c", k=3)
        packed = w1[:, 0:GROUPS * 16]
        fields = agg
        fview = fields[:, :].rearrange("p (s f c) -> p s f c", f=4, c=CH)
        src_i = sb("src_i", [P, NSP * CH], I32)
        dloc = sb("dloc", [P, NSP * CH])
        last = sb("last", [P, NSP * CH])
        etype = hr[:, 1024:1024 + NSP * CH]
        src_g = sb("src_g", [P, CHUNKS + 2 * CH], I32)
        taken_g = sb("taken_g", [1, GROUPS])
        taken_i = sb("taken_i", [1, GROUPS], I32)
        need_i = sb("need_i", [1, NSP], I32)
        slot_i = sb("slot_i", [1, NSP], I32)
        RW = CHUNKS // CROWS * P
        rows_i = hr[0:CROWS, 0:RW].bitcast(I32)
        rows_f = w2[0:CROWS, 0:RW]
        pen = w2[0:CROWS, RW:2 * RW]

        Gall = sb("gathered_rows", [P, RING * CH * D])
        G = [Gall[:, i * CH * D:(i + 1) * CH * D] for i in range(RING)]
        OH = [sb(f"OH{i}", [P, CH * P]) for i in range(RING)]
        OHB = [sb(f"OHB{i}", [P, CH * P], BF16) for i in range(2)]
        TOH = [sb(f"TOH{i}", [P, CH, TYPES + 1]) for i in range(2)]
        ea1 = [sb(f"ea1{i}", [65, P]) for i in range(4)]
        pn = [sb(f"pn{i}", [16, P]) for i in range(RING)]
        ea4 = [hr[:, i * P:(i + 1) * P] for i in range(RING)]
        WT = [hr[:, RING * P + i * CH * 132:RING * P + (i + 1) * CH * 132] for i in range(2)]
        spare = [w[:, k * 512:(k + 1) * 512] for w in (w1, w2) for k in range(6)]
        rows = spare[0:RING]
        OHT, msg, lk = spare[0:RING], spare[RING:RING + 2], spare[RING + 2:RING + 4]
        far = hr[:, 2080:2080 + CH * P]
        OHTB = [hr[:, 2592 + i * 256:2592 + (i + 1) * 256].bitcast(BF16) for i in range(2)]
        idx8 = [sb(f"idx8{i}", [P, 2 * CH], I32) for i in range(RING)]
        score = [sb(f"score{i}", [P, 16]) for i in range(4)]
        scanned = sb("scanned", [20, P])
        segrhs = sb("segrhs", [P, CH * 5])
        segout = [sb(f"segout{i}", [P, CH * 5]) for i in range(2)]
        sval = sb("sval", [P, 16])
        smx = sb("smx", [P, 4])
        mnew = sb("mnew", [P, 4])
        mdif = [sb(f"mdif{i}", [P, 4]) for i in range(2)]
        scl = [sb(f"scl{i}", [P, 4]) for i in range(2)]
        delta = sb("delta", [P, 16])
        fall = sb("fall", [P, 16])
        vn = sb("vn", [P, 1])
        vsum = sb("vsum", [P, 1])
        vt = sb("vt", [P, 1])
        vm = sb("vm", [P, 2])
        vs1, vb1 = sb("vs1", [P, 4]), sb("vb1", [P, 4])
        vs2, vb2 = sb("vs2", [P, 2]), sb("vb2", [P, 2])
        bnv = sb("bnv", [P, 6])
        gbias = sb("gbias", [P, 2])

        W = {}
        loads = []
        for k in ("L0_gnn_Wl1", "L0_gnn_Wr1", "L0_gnn_Wl2", "L0_gnn_Wr2", "L1_gnn_W_msg", "L1_gnn_W_ih", "L1_gnn_W_hh",
                  "L1_aug", "L2_conv_edge", "L2_gnn_conv_w1", "L2_gnn_conv_w2", "L2_gnn_vn_w1", "L2_gnn_vn_w2",
                  *[f"L3_gnn_{v}{l}" for l in range(3) for v in ("Wl", "Wr", "We")], *[f"col_{v}" for v in VEC_COLS]):
            W[k] = sb("w_" + k, list(a[k].shape))
            loads.append((W[k][:, :], a[k]))
        for k in VEC_ROWS:
            n = a[k].shape[1]
            W[k] = sb("r_" + k, [P, n])
            loads.append((W[k][:, :], a[k].to_broadcast([P, n])))

        ps = ctx.enter_context(nc.psum_tensor("ps", [P, 4096], F32))

        def bank(i, n=512, p=P):
            return ps[0:p, 512 * i:512 * i + n]

        turned = bank(0, CH * P // 2).bitcast(BF16)

        table = nc.dram_tensor("node_table", (NP, D), F32, kind="Internal").ap()
        pen_rows = nc.dram_tensor("penalty_rows", (GROUPS * 16, P), F32, kind="Internal").ap()

        turn = sem("turn")
        piece = [sem(f"piece{p}") for p in range(len(COLS))]
        loaded = sem("loaded")
        lists_in = sem("lists_in")
        stored = sem("stored")
        dlink = sem("dlink")
        alink = sem("alink")
        plink = sem("plink")
        fcopy = sem("fcopy")
        n_loads, n_lists = len(loads) + 1, 6

        gathered = [sem(f"gathered{q}") for q in range(RING)]
        edge_rows_in = [sem(f"edge_rows{q}") for q in range(RING)]
        pairs_begun = sem("pairs_begun")
        lists_made, groups_landed = sem("lists_made"), sem("groups_landed")
        before = dict(rows=0, listed=0, gathered=[0] * RING)

        def sems(name, *kinds, rows=0):
            d = {k: sem(f"{name}_{k}") for k in ("onehot", "scattered", "added", *kinds)}
            d["gathered"], d["gathered before"] = gathered, list(before["gathered"])
            if name[:3] == "gat":
                used = [NSG // RING] * RING
            else:
                used = [-(-(GROUPS - q) // RING) for q in range(RING)]
                d["landed"], d["passes before"] = groups_landed, len(EDGES)
            before["gathered"] = [b + 16 * CH * k for b, k in zip(before["gathered"], used)]
            d["listed"], d["listed before"] = lists_made, before["listed"]
            before["listed"] += (GROUPS if "landed" in d else NSG) // 2 + 1
            if rows:
                d["edge_data"], d["rows"], d["rows before"] = edge_rows_in, rows, before["rows"]
                before["rows"] += 16 * rows * NSG // RING
            EDGES.append(name)
            return d

        EDGES = []
        SUM = {p: sems(p, "rows_out") for p in ("sage 1 edges", "sage 2 edges", "gru edges")}
        GIN = [sems(f"gin {l} edges", "projected", "summed", "rectified", rows=1) for l in range(3)]
        GAT = [sems(f"gat {l} edges", "turned", "onehot_t", "projected", "summed", "leaky", "attended", "score",
                    "score_t", "scanned", "scan_back", "seg_rhs", "seg_max", "seg_out", "chunk_max", "step_max",
                    "new_max", "max_drop", "kept",
                    "far", "scale", "max_of_edge", "delta", "fall", "weight", "weighted", "rescaled", rows=2)
               for l in range(3)]
        ALL = [*SUM.values(), *GIN, *GAT]
        HEADS = [4, 4, 1]

        def begin(eng, name):
            if TURNS[name]:
                eng.wait_ge(turn, TURNS[name])
            if PIECES[name]:
                for p in range(len(COLS)):
                    eng.wait_ge(piece[p], PIECES[name])

        def by_piece(eng, name):
            assert (name, True) in [s[1:] for s in ORDER]
            eng.wait_ge(turn, TURNS[name])
            for p, (c, w) in enumerate(COLS):
                if PIECES[name]:
                    eng.wait_ge(piece[p], PIECES[name])
                yield p, slice(c, c + w), range(c // P, (c + w) // P)

        STORES = 16 * 4
        PASS_TABLES = ("sage 2 edges", "gru edges", *[f"gin {l} edges" for l in range(3)],
                       *[f"gat {l} edges" for l in range(3)])
        IN_TABLE = {name: STORES + 16 * len(COLS) * (k + 1) for k, name in enumerate(PASS_TABLES)}

        block = ctx.enter_context(nc.Block())

        def held(eng, semaphore, value):
            if not (isinstance(value, int) and value < 1):
                eng.wait_ge(semaphore, value)

        def on(s):
            return not isinstance(s, int) or s >= 0

        def walk(eng, body, ahead=0, rounds=1, each_turn=None):
            for s in range(-ahead, PEEL):
                body(s, s % RING)
            span = rounds * RING
            with eng.Fori(0, (STEPS - PEEL) // span) as j:
                if each_turn:
                    each_turn()
                for k in range(PEEL, PEEL + span):
                    body(j * span + k, k % RING)

        def landed(s, u, S, what):
            n, before = (CH, S["gathered before"][u]) if what == "gathered" else (S["rows"], S["rows before"])
            return (s - u) * (16 * n // RING) + (16 * n + before)

        @block.sync
        def _(sp):
            sp.dma_start(src_g[:, 0:CHUNKS], a["src_cols"]).then_inc(lists_in, 16)
            sp.dma_start(endi[:, :], a["dst_ends"].to_broadcast([TILES - 1, GROUPS])).then_inc(lists_in, 16)
            for k, name in enumerate(("dst_cols", "next_cols", "type_cols")):
                sp.dma_start(idx_in[:, k, :], a[name]).then_inc(lists_in, 16)
            sp.dma_start(rows_i[:, :], a["dst_rows"].rearrange("(p k) e -> p (k e)", p=CROWS)).then_inc(lists_in, 16)
            sp.dma_start(res[:, :].rearrange("p (t f) -> p t f", f=D),
                         a["x"].rearrange("(t p) f -> p t f", p=P)).then_inc(loaded, 16)
            for dst, src in loads:
                sp.dma_start(dst, src).then_inc(loaded, 16)

            def store(made, x, dst):
                for p, (c, w) in enumerate(COLS):
                    sp.wait_ge(piece[p], PIECES[made] + 1)
                    t = c // P
                    sp.dma_start(dst[t * P:t * P + w].rearrange("(t p) f -> p t f", p=P),
                                 x[:, c:c + w].rearrange("p (t f) -> p t f", f=D)).then_inc(stored, 16)

            def edge_rows(S, l_at, depth, parts):
                sp.wait_ge(stored, IN_TABLE[l_at])

                def load(s, u):
                    g = sp.value_load(group_i[0:1, bass.ds(s, 1)], min_val=0, max_val=GROUPS - 1)
                    held(sp, S["projected"], s - depth + 1)
                    if "scanned" in S:
                        held(sp, S["scanned"], s - RING + 1)
                    parts(g, u)

                for u in range(RING):
                    load(u, u)
                with sp.Fori(1, NSG // RING) as j:
                    for u in range(RING):
                        load(j * RING + u, u)

            sp.wait_ge(turn, TURNS["step order"] + 1)
            pen_dst = pen_rows.rearrange("(p k h c) e -> h p k (c e)", k=2, h=4, c=CH)
            for h in range(4):
                sp.dma_start(pen_dst[h], pen.rearrange("p (k x) -> p k x", k=2)).then_inc(stored, 16)
            store("sage 1 relu", hr, table)
            store("sage norm out", res, table)
            for l in range(3):
                store(f"gin {l} rows out", hr, table)

                def gin_parts(g, u, l=l):
                    sp.dma_start(ea1[u % 4][0:64, :], a["ea16"][bass.ds(g * 64, 64), :]).then_inc(GIN[l]["edge_data"][u], 16)

                edge_rows(GIN[l], f"gin {l} edges", 4, gin_parts)
            for l in range(3):
                store(f"gat {l} left out", hr, table)
                H = HEADS[l]

                def gat_parts(g, u, l=l, H=H):
                    sp.dma_start(ea4[u][:, :], a["ea32"][bass.ds(g * P, P), :]).then_inc(GAT[l]["edge_data"][u], 16)
                    sp.dma_start(pn[u][0:CH * H, :],
                                 pen_rows[bass.ds(g * 16, CH * H), :]).then_inc(GAT[l]["edge_data"][u], 16)

                edge_rows(GAT[l], f"gat {l} edges", RING, gat_parts)
            for p, (c, w) in enumerate(COLS):
                sp.wait_ge(piece[p], PIECES["last norm out"] + 1)
                if c + w <= N:
                    sp.dma_start(out[c:c + w].rearrange("(t p) f -> p t f", p=P),
                                 res[:, c:c + w].rearrange("p (t f) -> p t f", f=D)).then_inc(stored, 16)
                else:
                    assert w == P
                    sp.dma_start(out[c:N], res[0:N - c, c:c + w]).then_inc(stored, 16)
            sp.wait_ge(stored, IN_TABLE["gat 2 edges"] + 16 * len(COLS))

        @block.gpsimd
        def _(pool):
            n = 0

            def link(ins):
                nonlocal n
                n += 1
                ins.then_inc(plink, 1)
                pool.wait_ge(plink, n)

            for m in (ident, ones, selcnt):
                pool.memset(m[:, :], 0.0 if m is not ones else 1.0).then_inc(plink, 1)
                n += 1
            pool.memset(eps[:, :], EPS)
            pool.memset(src_g[:, CHUNKS:CHUNKS + 2 * CH], 0).then_inc(plink, 1)
            n += 1
            for i in range(2):
                pool.memset(TOH[i][:, :, :], 1.0)
            for i in range(4):
                pool.memset(ea1[i][:, :], 1.0)
            pool.wait_ge(plink, n)
            link(pool.affine_select(out=ident[:, :], in_=ident[:, :], compare_op=ALU.not_equal, fill=1.0, base=0,
                                    pattern=[[-1, P]], channel_multiplier=1))
            link(pool.affine_select(out=selcnt[:, :], in_=selcnt[:, :], compare_op=ALU.not_equal, fill=1.0, base=-TYPES,
                                    pattern=[[0, 1]], channel_multiplier=1))
            exact = dict(allow_small_or_imprecise_dtypes=True)
            pool.iota(iota_d[:, :], [[1, P]], base=0, channel_multiplier=0, **exact)
            pool.iota(iota_t[:, :], [[1, TYPES]], base=0, channel_multiplier=0, **exact)
            pool.iota(iota_s[:, :], [[1, NSP]], base=0, channel_multiplier=0, **exact)
            pool.iota(pcol[:, 0:1], [[0, 1]], base=0, channel_multiplier=1, **exact)
            pool.iota(pcol[:, 1:2], [[0, 1]], base=P, channel_multiplier=P, **exact).then_inc(turn, 1)

            def order_fields(s):
                g = pool.value_load(group_i[0:1, bass.ds(s, 1)], min_val=0, max_val=GROUPS - 1)
                pool.tensor_copy(fields[:, bass.ds(s * 16, 16)], packed[:, bass.ds(g * 16, 16)]).then_inc(fcopy, 1)

            for S, name in zip(ALL, EDGES):
                src = a["x"] if name == "sage 1 edges" else table
                attention = "rows before" in S and "turned" in S
                index = src_i if attention else src_g
                if name == "sage 1 edges":
                    pool.wait_ge(lists_in, 16 * n_lists)
                else:
                    pool.wait_ge(stored, IN_TABLE[name])

                def list_rows(k, slot, S=S, index=index):
                    pool.tensor_copy(idx8[slot][:, :], index[:, bass.ds(k * 2 * CH, 2 * CH)]).then_inc(S["listed"], 1)

                def fetch_rows(slot, part, S=S, src=src):
                    for i in range(part * CH, (part + 1) * CH):
                        q = (2 * slot + part) % RING
                        pool.indirect_dma_start(
                            out=G[q][:, (i % CH) * D:(i % CH + 1) * D], out_offset=None, in_=src[:, :],
                            in_offset=bass.IndirectOffsetOnAxis(ap=idx8[slot][:, i:i + 1], axis=0),
                        ).then_inc(S["gathered"][q], 16)

                def fetch_steps(k, slot, S=S, list_rows=list_rows, fetch_rows=fetch_rows):
                    held(pool, S["weighted"], 2 * k + 2 - RING)
                    pool.wait_ge(S["listed"], k + (1 + S["listed before"]))
                    list_rows(k + 1, (slot + 1) % RING)
                    for part in range(2):
                        fetch_rows(slot, part)

                def announce(k, slot, S=S):
                    for part in range(2):
                        q = (2 * slot + part) % RING
                        pool.wait_ge(S["gathered"][q], (k * 2 + (part - q)) * (16 * CH // RING)
                                     + (16 * CH + S["gathered before"][q]))
                    pool.sem_inc(S["landed"], 2)

                def fetch_groups(k, slot, S=S, list_rows=list_rows, fetch_rows=fetch_rows, announce=announce):
                    if not (isinstance(k, int) and k < RING // 2):
                        done = pool.value_load(taken_i[0:1, bass.ds(k * 2 + (1 - RING), 1)], min_val=1, max_val=STEPS)
                        pool.wait_ge(S["summed"] if "summed" in S else S["rows_out"], done)
                        pool.sem_inc(pairs_begun, 1)
                    pool.wait_ge(S["listed"], k + (1 + S["listed before"]))
                    list_rows(k + 1, (slot + 1) % RING)
                    fetch_rows(slot, 0)
                    if not (isinstance(k, int) and k < 1):
                        announce(k - 1, (slot - 1) % RING)
                    fetch_rows(slot, 1)

                pairs, fetch = (NSG // 2, fetch_steps) if attention else (GROUPS // 2, fetch_groups)
                peeled = RING + pairs % RING
                list_rows(0, 0)
                for k in range(peeled):
                    if name == "sage 1 edges" and k == RING // 2:
                        pool.wait_ge(turn, TURNS["step order"])
                        with pool.Fori(0, (NSP - DVE_SHARE - ACT_SHARE) // 8) as j:
                            for i in range(8):
                                order_fields(j * 8 + (DVE_SHARE + ACT_SHARE + i))
                    fetch(k, k % RING)
                with pool.Fori(0, (pairs - peeled) // RING) as j:
                    for k in range(peeled, peeled + RING):
                        fetch(j * RING + k, k % RING)
                pool.wait_ge(S["listed"], pairs + 1 + S["listed before"])
                if not attention:
                    announce(pairs - 1, (pairs - 1) % RING)

        @block.scalar
        def _(act):
            n = 0

            def stage(name):
                assert ENGINE[name] == "act"
                begin(act, name)

            def pieces(name):
                assert ENGINE[name] == "act"
                return by_piece(act, name)

            def root_of(name):
                for p, _, ts in pieces(name):
                    act.activation(root[:, ts.start:ts.stop], st[:, ts.start:ts.stop, 1], ACT.Sqrt,
                                   bias=eps[:, 0:1]).then_inc(piece[p], 1)

            def out_of_psum(name, dst, func=ACT.Copy, **more):
                for p, cs, _ in pieces(name):
                    if func == ACT.Copy:
                        act.copy(dst[:, cs], ps[:, cs]).then_inc(piece[p], 1)
                    else:
                        act.activation(dst[:, cs], ps[:, cs], func, **more).then_inc(piece[p], 1)

            def order_fields(s):
                g = act.value_load(group_i[0:1, bass.ds(s, 1)], min_val=0, max_val=GROUPS - 1)
                act.copy(fields[:, bass.ds(s * 16, 16)], packed[:, bass.ds(g * 16, 16)]).then_inc(fcopy, 1)

            act.wait_ge(turn, TURNS["step order"])
            with act.Fori(0, ACT_SHARE // 8) as j:
                for k in range(8):
                    order_fields(j * 8 + (DVE_SHARE + k))

            def copy_rows(name):
                S = SUM[name]
                begin(act, name)

                def body(s, u):
                    need = act.value_load(need_i[0:1, bass.ds(s, 1)], min_val=1, max_val=GROUPS)
                    at = act.value_load(slot_i[0:1, bass.ds(s, 1)], min_val=0, max_val=(RING - 1) * CH * D)
                    held(act, S["scattered"], s - RING + 1)
                    act.wait_ge(S["landed"], need + S["passes before"] * GROUPS)
                    act.copy(rows[u], Gall[:, bass.ds(at, CH * D)]).then_inc(S["rows_out"], 1)

                walk(act, body)

            out_of_psum("x transposed", ht)
            act.wait_ge(stored, STORES)
            for l in (1, 2):
                copy_rows(f"sage {l} edges")
                for p, cs, _ in pieces(f"sage {l} relu"):
                    act.activation(hr[:, cs], w1[:, cs], ACT.Relu).then_inc(piece[p], 1)
                if l == 2:
                    root_of("sage norm root")
                out_of_psum(f"sage {l} transposed", ht)
            copy_rows("gru edges")
            out_of_psum("gru messages out", w2)
            out_of_psum("gru r gate", w1, ACT.Sigmoid, bias=gbias[:, 0:1])
            for p, cs, _ in pieces("gru n"):
                act.activation(w1[:, cs], w1[:, cs], ACT.Tanh, bias=W["col_L1_gnn_b_ih"][:, 2:3]).then_inc(piece[p], 1)
            out_of_psum("gru z gate", w2, ACT.Sigmoid, bias=gbias[:, 1:2])
            root_of("gru norm root")
            out_of_psum("gru transposed", ht, ACT.Identity, bias=vn[:, 0:1])
            for l in range(3):
                out_of_psum(f"gin {l} rows out", hr)
                S = GIN[l]
                begin(act, f"gin {l} edges")

                def rectify(s, u, S=S):
                    act.wait_ge(S["summed"], s + 1)
                    act.activation(rows[u], rows[u], ACT.Relu).then_inc(S["rectified"], 1)

                rectify(0, 0)
                walk(act, lambda s, u, r=rectify: r(s + 1, (u + 1) % RING))
                if l < 2:
                    stage(f"gin {l} virtual up out")
                    for k in range(2):
                        v = act.activation(vm[:, k:k + 1], ps[:, 512 * k:512 * k + 1], ACT.Relu,
                                           scale=vs1[:, 2 * l + k:2 * l + k + 1], bias=vb1[:, 2 * l + k:2 * l + k + 1])
                    v.then_inc(turn, 1)
                    stage(f"gin {l} virtual down out")
                    act.activation(vt[:, :], ps[:, 0:1], ACT.Relu, scale=vs2[:, l:l + 1],
                                   bias=vb2[:, l:l + 1]).then_inc(turn, 1)
                for k in range(2):
                    out_of_psum(f"gin {l} up {k} out", w2 if k == 0 else hr, ACT.Relu,
                                bias=W["col_L2_gnn_conv_b1"][:, 2 * l + k:2 * l + k + 1])
                out_of_psum(f"gin {l} down out", w1, ACT.Relu if l < 2 else ACT.Identity,
                            scale=bnv[:, 2 * l:2 * l + 1], bias=bnv[:, 2 * l + 1:2 * l + 2])
            root_of("gin norm root")
            for l in range(3):
                H = HEADS[l]
                C = D // H
                S = GAT[l]
                if l == 0:
                    out_of_psum("gat 0 transposed", ht)
                else:
                    out_of_psum(f"gat {l} transposed", ht, ACT.Relu, scale=W[f"col_L3_gnn_g{l - 1}"][:, 0:1],
                                bias=W[f"col_L3_gnn_be{l - 1}"][:, 0:1])
                for k in range(3):
                    for p, cs, ts in pieces(f"gat {l} right part {k}"):
                        act.copy(right_parts[:, k, ts.start:ts.stop],
                                 w1[:, cs].rearrange("p (t f) -> p t f", f=D)).then_inc(piece[p], 1)
                begin(act, f"gat {l} edges")
                act.wait_ge(stored, IN_TABLE[f"gat {l} edges"])

                def body(s, u, S=S, H=H, C=C, KH=CH * H):
                    if on(s):
                        act.wait_ge(S["max_drop"], s + 1)
                        act.activation(scl[u % 2][:, 0:H], mdif[u % 2][:, 0:H], ACT.Exp).then_inc(S["scale"], 1)
                        act.wait_ge(S["delta"], s + 1)
                        act.activation(fall[:, 0:KH], delta[:, 0:KH], ACT.Relu, scale=-1.0).then_inc(S["fall"], 1)
                        act.wait_ge(S["fall"], s + 1)
                        wt = WT[u % 2][:, 0:KH * (C + 1)].rearrange("p (k c) -> p k c", c=C + 1)
                        act.activation(wt[:, :, C], fall[:, 0:KH], ACT.Exp, scale=-1.0).then_inc(S["weight"], 1)
                    if on(s + 5):
                        act.wait_ge(S["turned"], s + 6)
                        act.copy(OHT[(u + 5) % RING], turned)
                        held(act, S["projected"], s + 4)
                        act.copy(OHTB[(u + 1) % 2], turned).then_inc(S["onehot_t"], 1)
                    if on(s + 2):
                        act.wait_ge(S["seg_max"], s + 3)
                        act.copy(segout[u % 2][:, 0:CH * (H + 1)], bank(5, CH * (H + 1))).then_inc(S["seg_out"], 1)
                    held(act, S["onehot"], s + AHEAD)
                    for c in range(CH):
                        act.activation(far[:, c * P:(c + 1) * P], iota_d[:, :], ACT.Abs, scale=-1.0,
                                       bias=dloc[:, bass.ds((s + AHEAD) * CH + c, 1)]).then_inc(S["far"], 1)
                    act.wait_ge(S["far"], (s + AHEAD + 1) * CH)
                    act.activation(OHB[(u + AHEAD) % 2][:, :], far, ACT.Relu, scale=-1.0, bias=1.0)
                    held(act, S["scattered"], s)
                    act.activation(OH[(u + AHEAD) % RING][:, :], far, ACT.Relu, scale=-1.0,
                                   bias=1.0).then_inc(S["onehot"], 1)

                walk(act, body, AHEAD, rounds=2)
                root_of(f"gat {l} norm root")
            for p, cs, _ in pieces("gat 2 relu"):
                act.activation(w1[:, cs], w1[:, cs], ACT.Relu).then_inc(piece[p], 1)
            root_of("last norm root")

        @block.tensor
        def _(pe):
            def stage(name):
                assert ENGINE[name] == "pe"
                begin(pe, name)

            def pieces(name):
                assert ENGINE[name] == "pe"
                return by_piece(pe, name)

            def transpose_all(name, x):
                for p, _, ts in pieces(name):
                    for t in ts:
                        m = pe.transpose(ps[:, t * P:(t + 1) * P], x[:, t * P:(t + 1) * P], ident[:, :])
                    m.then_inc(piece[p], 1)

            def rows_of(name, xt, w):
                for p, _, ts in pieces(name):
                    for t in ts:
                        m = pe.matmul(ps[:, t * P:(t + 1) * P], xt[:, t * P:(t + 1) * P], w, start=True, stop=True)
                    m.then_inc(piece[p], 1)

            def features_of(name, *terms):
                for p, cs, _ in pieces(name):
                    for k, (w, x) in enumerate(terms):
                        m = pe.matmul(ps[:, cs], w, x[:, cs], start=(k == 0), stop=(k == len(terms) - 1))
                    m.then_inc(piece[p], 1)

            def scatter(s, u, S):
                if not (isinstance(s, int) and s < 2):
                    pe.wait_ge(S["added"], s - 1)
                for c in range(CH):
                    m = pe.matmul(bank(u % 2, P), rows[u][:, c * D:(c + 1) * D], OH[u][:, c * P:(c + 1) * P],
                                  start=(c == 0), stop=(c == CH - 1))
                return m

            stage("sum of tile ends")
            pe.matmul(bank(1, GROUPS, 1), ones[0:TILES - 1, 0:1], past_g[0:TILES - 1, :], start=True, stop=True)
            pe.matmul(bank(0, NSP), ones[0:TILES - 1, :], past[0:TILES - 1, :], start=True, stop=True).then_inc(turn, 1)
            pe.wait_ge(loaded, 16 * n_loads)
            transpose_all("transpose x", res)
            for l in (1, 2):
                S = SUM[f"sage {l} edges"]
                begin(pe, f"sage {l} edges")

                def body(s, u, S=S, l=l):
                    pe.wait_ge(S["rows_out"], s + 1)
                    pe.wait_ge(S["onehot"], s + 1)
                    m = scatter(s, u, S)
                    if l == 1:
                        for c in range(CH):
                            m = pe.matmul(bank(2 + u % 2, P, TYPES + 1), TOH[u % 2][:, c, :],
                                          OH[u][:, c * P:(c + 1) * P], start=(c == 0), stop=(c == CH - 1))
                    m.then_inc(S["scattered"], 1)

                walk(pe, body)
                if l == 1:
                    stage("degrees")
                    for t in range(TILES):
                        m = pe.matmul(ps[:, t:t + 1], cnt[:, t * P:(t + 1) * P], selcnt[:, :], start=True, stop=True)
                    m.then_inc(turn, 1)
                rows_of(f"sage {l} neighbours", agg, W[f"L0_gnn_Wl{l}"][:, :])
                rows_of(f"sage {l} self", ht, W[f"L0_gnn_Wr{l}"][:, :])
                transpose_all(f"sage {l} transpose", hr if l == 1 else res)

            S = SUM["gru edges"]
            begin(pe, "gru edges")

            def body(s, u):
                pe.wait_ge(S["rows_out"], s + 1)
                pe.wait_ge(S["onehot"], s + 1)
                scatter(s, u, S).then_inc(S["scattered"], 1)

            walk(pe, body)
            Wih, Whh = ([W[f"L1_gnn_W_{v}h"][:, k * D:(k + 1) * D] for k in range(3)] for v in "ih")
            features_of("gru messages", (W["L1_gnn_W_msg"][:, :], agg), (W["L1_aug"][:, :], cnt))
            features_of("gru r", (Wih[0], w2), (Whh[0], ht))
            features_of("gru hn", (Whh[2], ht))
            features_of("gru in", (Wih[2], w2))
            features_of("gru z", (Wih[1], w2), (Whh[1], ht))
            transpose_all("gru state rows", hr)
            transpose_all("gru transpose", res)

            for l in range(3):
                transpose_all(f"gin {l} rows", ht)
                S = GIN[l]
                begin(pe, f"gin {l} edges")

                def project(s, u, S=S, l=l):
                    pe.wait_ge(S["edge_data"][u], landed(s, u, S, "rows"))
                    if not (isinstance(s, int) and s < 2):
                        pe.wait_ge(S["summed"], s - 1)
                    pe.matmul(bank(2 + u % 2), ea1[u % 4][:, :], W["L2_conv_edge"][:, l * CH * D:(l + 1) * CH * D],
                              start=True, stop=True).then_inc(S["projected"], 1)

                project(0, 0)

                def body(s, u, S=S, project=project):
                    project(s + 1, (u + 1) % RING)
                    pe.wait_ge(S["onehot"], s + 1)
                    pe.wait_ge(S["rectified"], s + 1)
                    scatter(s, u, S).then_inc(S["scattered"], 1)

                walk(pe, body)
                if l < 2:
                    stage(f"gin {l} virtual up")
                    for k in range(2):
                        m = pe.matmul(ps[:, 512 * k:512 * k + 1], W["L2_gnn_vn_w1"][:, (2 * l + k) * D:(2 * l + k + 1) * D],
                                      vsum[:, :], start=True, stop=True)
                    m.then_inc(turn, 1)
                    stage(f"gin {l} virtual down")
                    for k in range(2):
                        m = pe.matmul(ps[:, 0:1], W["L2_gnn_vn_w2"][:, (2 * l + k) * D:(2 * l + k + 1) * D],
                                      vm[:, k:k + 1], start=(k == 0), stop=(k == 1))
                    m.then_inc(turn, 1)
                up, down = ([W[f"L2_gnn_conv_w{v}"][:, (2 * l + k) * D:(2 * l + k + 1) * D] for k in range(2)]
                            for v in "12")
                for k in range(2):
                    features_of(f"gin {l} up {k}", (up[k], w1))
                features_of(f"gin {l} down", (down[0], w2), (down[1], hr))
            transpose_all("gin transpose", w1)

            for l in range(3):
                H = HEADS[l]
                C = D // H
                KH = CH * H
                S = GAT[l]
                transpose_all(f"gat {l} transpose", res if l == 0 else w1)
                rows_of(f"gat {l} left", ht, W[f"L3_gnn_Wl{l}"][:, :])
                rows_of(f"gat {l} right", ht, W[f"L3_gnn_Wr{l}"][:, :])
                begin(pe, f"gat {l} edges")
                term = [bank(1), bank(2)]
                score_t, scan_back, seg_max = bank(3, P, KH), bank(4, KH + CH), bank(5, CH * (H + 1))
                max_of_edge, sums = bank(6, KH), bank(7, H * (C + 1))

                def project(s, u, S=S, l=l):
                    t = pe.value_load(tile_i[0:1, bass.ds(s, 1)], min_val=0, max_val=TILES - 1)
                    right = [xrb[:, bass.ds(t * (3 * D) + k * D, D)] for k in range(3)]
                    pe.wait_ge(S["edge_data"][u], landed(s, u, S, "rows"))
                    held(pe, S["summed"], s - 1)
                    pe.matmul(term[u % 2], ea4[u], W[f"L3_gnn_We{l}"][:, :], start=True, stop=False)
                    pe.wait_ge(S["onehot_t"], s + 1)
                    for c in range(CH):
                        for k in range(3):
                            m = pe.matmul(term[u % 2][:, c * D:(c + 1) * D], OHTB[u % 2][:, c * P:(c + 1) * P],
                                          right[k], start=False, stop=(c == CH - 1 and k == 2))
                    m.then_inc(S["projected"], 1)

                def body(s, u, S=S, H=H, C=C, KH=KH, project=project):
                    if on(s):
                        pe.wait_ge(S["new_max"], s + 1)
                        for c in range(CH):
                            m = pe.matmul(max_of_edge[:, c * H:(c + 1) * H], OHT[u][:, c * P:(c + 1) * P],
                                          mnew[:, 0:H], start=True, stop=True)
                        m.then_inc(S["max_of_edge"], 1)
                    if on(s + 2):
                        pe.wait_ge(S["scanned"], s + 3)
                        pe.matmul(scan_back, scanned[0:KH + CH, :], ident[0:KH + CH, 0:KH + CH], start=True,
                                  stop=True).then_inc(S["scan_back"], 1)
                    if on(s + 5):
                        pe.wait_ge(S["onehot"], s + 6)
                        held(pe, S["onehot_t"], s + 5)
                        for c in range(CH):
                            m = pe.transpose(turned[:, c * P:(c + 1) * P], OHB[(u + 1) % 2][:, c * P:(c + 1) * P],
                                             identb[:, :])
                        m.then_inc(S["turned"], 1)
                    if on(s + 4):
                        project(s + 4, (u + 4) % RING)
                    if on(s + 2):
                        pe.wait_ge(S["seg_rhs"], s + 3)
                        held(pe, S["seg_out"], s + 2)
                        for c in range(CH):
                            m = pe.matmul(seg_max[:, c * (H + 1):(c + 1) * (H + 1)],
                                          OH[(u + 2) % RING][:, c * P:(c + 1) * P],
                                          segrhs[:, c * (H + 1):(c + 1) * (H + 1)], start=True, stop=True)
                        m.then_inc(S["seg_max"], 1)
                    if on(s + 3):
                        pe.wait_ge(S["score"], s + 4)
                        pe.transpose(score_t, score[(u + 3) % 4][:, 0:KH], ident[:, :]).then_inc(S["score_t"], 1)
                    if on(s):
                        pe.wait_ge(S["weighted"], s + 1)
                        held(pe, S["added"], s)
                        for c in range(CH):
                            m = pe.matmul(sums, OH[u][:, c * P:(c + 1) * P],
                                          WT[u % 2][:, c * H * (C + 1):(c + 1) * H * (C + 1)],
                                          start=(c == 0), stop=(c == CH - 1))
                        m.then_inc(S["scattered"], 1)

                walk(pe, body, AHEAD, rounds=2)

        @block.vector
        def _(dve):
            n = 0

            def link(ins):
                nonlocal n
                n += 1
                ins.then_inc(dlink, 1)
                dve.wait_ge(dlink, n)

            def stage(name):
                assert ENGINE[name] == "dve"
                begin(dve, name)

            def pieces(name):
                assert ENGINE[name] == "dve"
                return by_piece(dve, name)

            def tiled(x):
                return x.rearrange("p (t f) -> p t f", f=D)

            def per_row(name, n):
                return W[name][:, None, :].to_broadcast([P, n, D])

            def row_stats(p, ts, x):
                for t in ts:
                    ins = dve.bn_stats(halves[:, t, :], x[:, t * D:(t + 1) * D])
                link(ins)
                for t in ts:
                    ins = dve.bn_aggr(st[:, t, :], halves[:, t, :])
                ins.then_inc(piece[p], 1)

            def norm_out(name, dst, x):
                for p, _, ts in pieces(name):
                    link(dve.reciprocal(rstd[:, ts.start:ts.stop], root[:, ts.start:ts.stop]))
                    for t in ts:
                        ins = dve.tensor_scalar(dst[:, t * D:(t + 1) * D], x[:, t * D:(t + 1) * D], st[:, t, 0:1],
                                                rstd[:, t:t + 1], ALU.subtract, ALU.mult)
                    ins.then_inc(piece[p], 1)

            def one_hot(s, u, S):
                dve.tensor_tensor(OH[u][:, :].rearrange("p (c d) -> p c d", d=P),
                                  dloc[:, bass.ds(s * CH, CH)][:, :, None].to_broadcast([P, CH, P]),
                                  iota_d[:, None, :].to_broadcast([P, CH, P]), ALU.is_equal).then_inc(S["onehot"], 1)

            def finish(S):
                if "landed" in S:
                    dve.wait_ge(S["landed"], GROUPS * (1 + S["passes before"]))
                for q in range(RING):
                    if "landed" not in S:
                        dve.wait_ge(S["gathered"][q], landed(NSG - RING + q, q, S, "gathered"))
                    if "rows" in S:
                        dve.wait_ge(S["edge_data"][q], landed(NSG - RING + q, q, S, "rows"))
                dve.wait_ge(S["added"], STEPS)
                dve.sem_inc(turn, 1)

            stage("step tables 1")
            dve.wait_ge(lists_in, 16 * n_lists)
            link(dve.tensor_copy(ends[0:TILES - 1, :], endi[:, :]))
            link(dve.tensor_scalar(pcol[:, 2:3], pcol[:, 0:1], float(P - 1), None, ALU.is_equal))
            link(dve.tensor_scalar(ends[0:TILES - 1, :], ends[0:TILES - 1, :], pcol[0:TILES - 1, 1:2], None, ALU.is_lt))
            link(dve.tensor_reduce(gl[0:TILES - 1, :], ends[0:TILES - 1, :], AX.X, ALU.add))
            link(dve.tensor_scalar(past_g[0:TILES - 1, :], iota_s[0:TILES - 1, 0:GROUPS], gl[0:TILES - 1, 0:1], None,
                                   ALU.is_ge))
            link(dve.tensor_tensor(gl[0:TILES - 1, :], gl[0:TILES - 1, :], pcol[0:TILES - 1, 0:1], ALU.add))
            dve.tensor_scalar(past[0:TILES - 1, :], iota_s[0:TILES - 1, :], gl[0:TILES - 1, 0:1], None,
                              ALU.is_gt).then_inc(turn, 1)
            stage("step tables 2")
            link(dve.tensor_copy(tstep[:, :], bank(0, NSP)))
            link(dve.tensor_tensor(gstep[:, :], iota_s[:, :], tstep[:, :], ALU.subtract))
            link(dve.tensor_scalar(gstep[:, :], gstep[:, :], float(GROUPS - 1), None, ALU.min))
            link(dve.tensor_copy(tile_i[0:1, :], tstep[0:1, :]))
            link(dve.tensor_copy(group_i[0:1, :], gstep[0:1, :]))
            link(dve.tensor_scalar(gstep[0:1, :], gstep[0:1, :], 1.0, None, ALU.add))
            link(dve.tensor_copy(need_i[0:1, :], gstep[0:1, :]))
            link(dve.tensor_scalar(slot_i[0:1, :], group_i[0:1, :], RING - 1, (CH * D).bit_length() - 1,
                                   ALU.bitwise_and, ALU.logical_shift_left))
            link(dve.tensor_tensor(taken_g[:, :], bank(1, GROUPS, 1), iota_s[0:1, 0:GROUPS], ALU.add))
            link(dve.tensor_scalar(taken_i[:, :], taken_g[:, :], 1.0, None, ALU.add))
            pk = packed.rearrange("p (g f c) -> p f g c", f=4, c=CH)

            def chunks(x):
                return x.rearrange("p (g c) -> p g c", c=CH)

            dve.tensor_copy(pk[:, 0], chunks(src_g[:, 0:CHUNKS]))
            dve.tensor_copy(pk[:, 1], chunks(idx_in[:, 0, :]))
            dve.tensor_copy(pk[:, 3], chunks(idx_in[:, 2, :]))
            link(dve.tensor_copy(pk[:, 2], chunks(idx_in[:, 1, :])))
            link(dve.tensor_tensor(pk[:, 2], pk[:, 2], pk[:, 1], ALU.not_equal))
            link(dve.tensor_scalar(pk[:, 2], pk[:, 2], pcol[:, 2:3], None, ALU.max))
            dve.tensor_scalar(pk[:, 3], pk[:, 3], 0.0, float(TYPES - 1), ALU.max, ALU.min).then_inc(turn, 1)
            dve.wait_ge(turn, TURNS["step order"])

            def order_fields(s):
                g = dve.value_load(group_i[0:1, bass.ds(s, 1)], min_val=0, max_val=GROUPS - 1)
                dve.tensor_copy(fields[:, bass.ds(s * 16, 16)], packed[:, bass.ds(g * 16, 16)]).then_inc(fcopy, 1)

            with dve.Fori(0, DVE_SHARE // 8) as j:
                for k in range(8):
                    order_fields(j * 8 + k)
            link(dve.memset(cnt[:, :], 0.0))
            dve.wait_ge(fcopy, NSP)

            def stepped(x):
                return x[:, :].rearrange("p (s c) -> p s c", c=CH)

            dve.tensor_copy(stepped(src_i), fview[:, :, 0])
            dve.tensor_copy(stepped(last), fview[:, :, 2])
            dve.tensor_copy(stepped(etype), fview[:, :, 3])
            link(dve.tensor_scalar(tstep[:, :], tstep[:, :], float(P), None, ALU.mult))
            link(dve.tensor_tensor(stepped(dloc), fview[:, :, 1], tstep[:, :, None].to_broadcast([P, NSP, CH]),
                                   ALU.subtract))
            rv, pv = rows_f.rearrange("p (k e) -> p k e", e=P), pen.rearrange("p (k e) -> p k e", e=P)
            link(dve.tensor_copy(rows_f, rows_i[:, :]))
            link(dve.memset(pv[:, :, 0:1], -BIG))
            link(dve.tensor_tensor(pv[:, :, 1:P], rv[:, :, 1:P], rv[:, :, 0:P - 1], ALU.is_equal))
            link(dve.tensor_scalar(pv[:, :, 1:P], pv[:, :, 1:P], 1.0, BIG, ALU.subtract, ALU.mult))
            dve.wait_ge(loaded, 16 * n_loads)
            V = {k[7:]: W["col_" + k] for k in VEC_COLS if k[:2] == "L2"}
            V_gru = [W["col_L1_gnn_b_ih"], W["col_L1_gnn_b_hh"]]
            for l in range(3):
                link(dve.tensor_scalar(bnv[:, 2 * l:2 * l + 1], V["bn_gamma"][:, l:l + 1], INV, None, ALU.mult))
                link(dve.tensor_tensor(bnv[:, 2 * l + 1:2 * l + 2], V["conv_b2"][:, l:l + 1], bnv[:, 2 * l:2 * l + 1],
                                       ALU.mult))
                link(dve.tensor_tensor(bnv[:, 2 * l + 1:2 * l + 2], bnv[:, 2 * l + 1:2 * l + 2],
                                       V["bn_beta"][:, l:l + 1], ALU.add))
            for scale, bias, g, b, be in ((vs1, vb1, "vn_g1", "vn_b1", "vn_be1"), (vs2, vb2, "vn_g2", "vn_b2", "vn_be2")):
                link(dve.tensor_scalar(scale[:, :], V[g][:, :], INV, None, ALU.mult))
                link(dve.tensor_tensor(bias[:, :], V[b][:, :], scale[:, :], ALU.mult))
                link(dve.tensor_tensor(bias[:, :], bias[:, :], V[be][:, :], ALU.add))
            link(dve.tensor_tensor(gbias[:, :], V_gru[0][:, 0:2], V_gru[1][:, 0:2], ALU.add))
            dve.tensor_copy(identb[:, :], ident[:, :])
            dve.tensor_copy(vn[:, :], V["vn_emb"][:, :]).then_inc(turn, 1)

            def sum_pass(S, first=False):
                link(dve.memset(agg[:, 0:NP], 0.0))

                def one_hot_all(s, u):
                    if first:
                        dve.tensor_tensor(TOH[u % 2][:, :, 0:TYPES],
                                          etype[:, bass.ds(s * CH, CH)][:, :, None].to_broadcast([P, CH, TYPES]),
                                          iota_t[:, None, :].to_broadcast([P, CH, TYPES]), ALU.is_equal)
                    one_hot(s, u, S)

                one_hot_all(0, 0)

                def body(s, u):
                    one_hot_all(s + 1, (u + 1) % RING)
                    add_sums(s, u, S, first)

                walk(dve, body)
                finish(S)

            def add_sums(s, u, S, first=False):
                t = dve.value_load(tile_i[0:1, bass.ds(s, 1)], min_val=0, max_val=TILES - 1)
                if not (isinstance(s, int) and s < 1):
                    dve.wait_ge(S["added"], s)
                dve.wait_ge(S["scattered"], s + 1)
                w = agg[:, bass.ds(t * P, P)]
                if first:
                    cw = cnt[:, bass.ds(t * P, P)]
                    dve.tensor_tensor(cw, cw, bank(2 + u % 2, P, TYPES + 1), ALU.add)
                dve.tensor_tensor(w, w, bank(u % 2, P), ALU.add).then_inc(S["added"], 1)

            for l in (1, 2):
                stage(f"sage {l} edges")
                sum_pass(SUM[f"sage {l} edges"], first=(l == 1))
                if l == 1:
                    stage("one over degree")
                    link(dve.tensor_scalar(rdeg[:, :], ps[:, 0:TILES], 1.0, None, ALU.max))
                    dve.reciprocal(rdeg[:, :], rdeg[:, :]).then_inc(turn, 1)
                for p, _, ts in pieces(f"sage {l} mean"):
                    for t in ts:
                        cs = slice(t * D, (t + 1) * D)
                        ins = dve.scalar_tensor_tensor(out=w1[:, cs], in0=ps[:, cs], scalar=rdeg[:, t:t + 1],
                                                       in1=W[f"L0_gnn_bl{l}"][:, :], op0=ALU.mult, op1=ALU.add)
                    ins.then_inc(piece[p], 1)
                for p, cs, _ in pieces(f"sage {l} add"):
                    dve.tensor_tensor(w1[:, cs], w1[:, cs], ps[:, cs], ALU.add).then_inc(piece[p], 1)
            for p, cs, ts in pieces("sage norm stats"):
                link(dve.tensor_tensor(w1[:, cs], hr[:, cs], res[:, cs], ALU.add))
                row_stats(p, ts, w1)
            norm_out("sage norm out", res, w1)

            stage("gru edges")
            sum_pass(SUM["gru edges"])
            for p, cs, _ in pieces("gru hn gated"):
                dve.scalar_tensor_tensor(out=w1[:, cs], in0=ps[:, cs], scalar=V_gru[1][:, 2:3], in1=w1[:, cs],
                                         op0=ALU.add, op1=ALU.mult).then_inc(piece[p], 1)
            for p, cs, _ in pieces("gru in add"):
                dve.tensor_tensor(w1[:, cs], w1[:, cs], ps[:, cs], ALU.add).then_inc(piece[p], 1)
            for p, cs, _ in pieces("gru state"):
                link(dve.tensor_tensor(hr[:, cs], ht[:, cs], w1[:, cs], ALU.subtract))
                link(dve.tensor_tensor(hr[:, cs], hr[:, cs], w2[:, cs], ALU.mult))
                dve.tensor_tensor(hr[:, cs], hr[:, cs], w1[:, cs], ALU.add).then_inc(piece[p], 1)
            for p, cs, ts in pieces("gru norm stats"):
                link(dve.tensor_tensor(w1[:, cs], ps[:, cs], res[:, cs], ALU.add))
                row_stats(p, ts, w1)
            norm_out("gru norm out", res, w1)
            for l in range(3):
                S = GIN[l]
                stage(f"gin {l} edges")
                link(dve.memset(agg[:, 0:NP], 0.0))
                if l < 2:
                    link(dve.tensor_reduce(vsum[:, :], ht[:, 0:N], AX.X, ALU.add))
                    link(dve.tensor_tensor(vsum[:, :], vsum[:, :], vn[:, :], ALU.add))

                def add_term(s, u, S=S):
                    need = dve.value_load(need_i[0:1, bass.ds(s, 1)], min_val=1, max_val=GROUPS)
                    at = dve.value_load(slot_i[0:1, bass.ds(s, 1)], min_val=0, max_val=(RING - 1) * CH * D)
                    dve.wait_ge(S["landed"], need + S["passes before"] * GROUPS)
                    dve.wait_ge(S["projected"], s + 1)
                    dve.tensor_tensor(rows[u], Gall[:, bass.ds(at, CH * D)], bank(2 + u % 2),
                                      ALU.add).then_inc(S["summed"], 1)

                one_hot(0, 0, S)
                add_term(0, 0)

                def body(s, u, S=S, add_term=add_term):
                    one_hot(s + 1, (u + 1) % RING, S)
                    add_term(s + 1, (u + 1) % RING)
                    add_sums(s, u, S)

                walk(dve, body)
                dve.wait_ge(S["rectified"], STEPS + 1)
                dve.wait_ge(S["added"], STEPS)
                finish(S)
                if l < 2:
                    stage(f"gin {l} virtual node")
                    dve.tensor_tensor(vn[:, :], vn[:, :], vt[:, :], ALU.add).then_inc(turn, 1)
                for p, cs, _ in pieces(f"gin {l} add"):
                    dve.tensor_tensor(w1[:, cs], agg[:, cs], ht[:, cs], ALU.add).then_inc(piece[p], 1)
                for p, cs, _ in pieces(f"gin {l} residual"):
                    if l < 2:
                        dve.scalar_tensor_tensor(out=ht[:, cs], in0=w1[:, cs], scalar=vn[:, 0:1], in1=ht[:, cs],
                                                 op0=ALU.add, op1=ALU.add).then_inc(piece[p], 1)
                    else:
                        dve.tensor_tensor(w1[:, cs], w1[:, cs], ht[:, cs], ALU.add).then_inc(piece[p], 1)
            for p, cs, ts in pieces("gin norm stats"):
                link(dve.tensor_tensor(w1[:, cs], ps[:, cs], res[:, cs], ALU.add))
                row_stats(p, ts, w1)
            norm_out("gin norm out", res, w1)

            for l in range(3):
                H = HEADS[l]
                C = D // H
                KH = CH * H
                HC = H * (C + 1)
                S = GAT[l]
                for p, cs, ts in pieces(f"gat {l} left out"):
                    dve.tensor_tensor(tiled(hr[:, cs]), tiled(ps[:, cs]), per_row(f"L3_gnn_bl{l}", len(ts)),
                                      ALU.add).then_inc(piece[p], 1)
                for p, cs, ts in pieces(f"gat {l} right out"):
                    dve.tensor_tensor(tiled(w1[:, cs]), tiled(ps[:, cs]), per_row(f"L3_gnn_br{l}", len(ts)),
                                      ALU.add).then_inc(piece[p], 1)
                for k in (1, 2):
                    for p, cs, ts in pieces(f"gat {l} right rest {k}"):
                        dve.tensor_tensor(tiled(w1[:, cs]), tiled(w1[:, cs]),
                                          right_parts[:, k - 1, ts.start:ts.stop], ALU.subtract).then_inc(piece[p], 1)
                stage(f"gat {l} edges")
                link(dve.memset(agg[:, 0:TILES * HC], 0.0))
                link(dve.memset(mx[:, :], -BIG))
                link(dve.memset(scanned[:, :], 2 * BIG))
                term = [bank(1), bank(2)]
                score_t, scan_back, seg_max = bank(3, P, KH), bank(4, KH + CH), bank(5, CH * (H + 1))
                max_of_edge, sums = bank(6, KH), bank(7, HC)
                att = W[f"L3_gnn_att{l}"]

                tiles = {}

                def load_tile(s, u):
                    tiles[u] = dve.value_load(tile_i[0:1, bass.ds(s, 1)], min_val=0, max_val=TILES - 1)

                def by_chunk(x, heads_first=False):
                    return x.rearrange("p (h c) -> p c h" if heads_first else "p (c h) -> p c h", c=CH)

                def chunk_max(s, u):
                    so = by_chunk(segout[u % 2][:, 0:CH * (H + 1)])
                    dve.wait_ge(S["seg_out"], s + 1)
                    dve.scalar_tensor_tensor(out=by_chunk(sval[:, 0:KH]), in0=so[:, :, H:H + 1].to_broadcast([P, CH, H]),
                                             scalar=-BIG, in1=so[:, :, 0:H], op0=ALU.add,
                                             op1=ALU.min).then_inc(S["chunk_max"], 1)

                def step_max(s, u):
                    dve.wait_ge(S["chunk_max"], s + 1)
                    dve.tensor_reduce(smx[:, 0:H], sval[:, 0:KH].rearrange("p (c h) -> p h c", c=CH), AX.X,
                                      ALU.max).then_inc(S["step_max"], 1)

                tile_max = {}

                def new_max(s, u):
                    tile_max[0] = mt = mx[:, bass.ds(tiles[u] * 4, H)]
                    held(dve, S["kept"], s)
                    dve.wait_ge(S["step_max"], s + 1)
                    dve.tensor_tensor(mnew[:, 0:H], smx[:, 0:H], mt, ALU.max).then_inc(S["new_max"], 1)

                def max_drop(s, u):
                    dve.wait_ge(S["new_max"], s + 1)
                    dve.tensor_tensor(mdif[u % 2][:, 0:H], tile_max[0], mnew[:, 0:H],
                                      ALU.subtract).then_inc(S["max_drop"], 1)

                def keep_max(s, u):
                    dve.wait_ge(S["max_drop"], s + 1)
                    dve.tensor_scalar(tile_max[0], mnew[:, 0:H], 1.0, None, ALU.mult).then_inc(S["kept"], 1)

                def add_terms(s, u):
                    dve.wait_ge(S["gathered"][u], landed(s, u, S, "gathered"))
                    dve.wait_ge(S["projected"], s + 1)
                    dve.tensor_tensor(msg[u % 2], G[u][:, :], term[u % 2], ALU.add).then_inc(S["summed"], 1)

                def scan(s, u):
                    dve.wait_ge(S["score_t"], s + 1)
                    dve.tensor_tensor_scan(out=scanned[0:KH, :], data0=pn[u][0:KH, :], data1=score_t, initial=-BIG,
                                           op0=ALU.add, op1=ALU.max).then_inc(S["scanned"], 1)

                def leak(s, u):
                    dve.wait_ge(S["summed"], s + 1)
                    dve.scalar_tensor_tensor(out=lk[u % 2], in0=msg[u % 2], scalar=0.2, in1=msg[u % 2], op0=ALU.mult,
                                             op1=ALU.max).then_inc(S["leaky"], 1)

                def attend(s, u):
                    dve.wait_ge(S["leaky"], s + 1)
                    x = lk[u % 2].rearrange("p (c f) -> p c f", f=D)
                    dve.tensor_tensor(x, x, att[:, None, :].to_broadcast([P, CH, D]), ALU.mult).then_inc(S["attended"], 1)

                def sum_scores(s, u):
                    dve.wait_ge(S["attended"], s + 1)
                    dve.tensor_reduce(by_chunk(score[u % 4][:, 0:KH], True),
                                      lk[u % 2].rearrange("p (c h k) -> p c h k", c=CH, h=H), AX.X,
                                      ALU.add).then_inc(S["score"], 1)

                def below_max(s, u):
                    dve.wait_ge(S["max_of_edge"], s + 1)
                    dve.tensor_tensor(by_chunk(delta[:, 0:KH]), by_chunk(score[u % 4][:, 0:KH], True),
                                      by_chunk(max_of_edge), ALU.subtract).then_inc(S["delta"], 1)

                def seg_rhs(s, u):
                    lst = last[:, bass.ds(s * CH, CH)]
                    dve.wait_ge(S["scan_back"], s + 1)
                    dve.tensor_tensor(by_chunk(segrhs[:, 0:CH * (H + 1)]), by_chunk(scan_back, True),
                                      lst[:, :, None].to_broadcast([P, CH, H + 1]), ALU.mult).then_inc(S["seg_rhs"], 1)

                def rescale(s, u):
                    if u not in tiles:
                        load_tile(s, u)
                    tile_sums[0] = w = agg[:, bass.ds(tiles[u] * HC, HC)]
                    held(dve, S["added"], s)
                    dve.wait_ge(S["scale"], s + 1)
                    wh = w.rearrange("p (h c) -> p h c", h=H)
                    dve.tensor_tensor(wh, wh, scl[u % 2][:, 0:H, None].to_broadcast([P, H, C + 1]),
                                      ALU.mult).then_inc(S["rescaled"], 1)

                tile_sums = {}

                def take_sums(s, u):
                    dve.wait_ge(S["rescaled"], s + 1)
                    dve.wait_ge(S["scattered"], s + 1)
                    dve.tensor_tensor(tile_sums[0], tile_sums[0], sums, ALU.add).then_inc(S["added"], 1)

                def weigh(s, u):
                    dve.wait_ge(S["weight"], s + 1)
                    wt = WT[u % 2][:, 0:KH * (C + 1)].rearrange("p (k c) -> p k c", c=C + 1)
                    dve.tensor_tensor(wt[:, :, 0:C], G[u][:, :].rearrange("p (k c) -> p k c", c=C),
                                      wt[:, :, C:C + 1].to_broadcast([P, KH, C]), ALU.mult).then_inc(S["weighted"], 1)

                plan = [(load_tile, 0), (new_max, 0), (add_terms, 3), (max_drop, 0), (scan, 2), (rescale, -1), (leak, 3), (keep_max, 0),
                        (below_max, 0), (attend, 3), (chunk_max, 1), (seg_rhs, 2), (step_max, 1), (sum_scores, 3),
                        (take_sums, -1), (weigh, 0)]

                def body(s, u):
                    for work, k in plan:
                        if on(s + k):
                            work(s + k, (u + k) % RING)

                walk(dve, body, AHEAD, rounds=2, each_turn=tiles.clear)
                tiles.clear()
                rescale(STEPS - 1, (STEPS - 1) % RING)
                take_sums(STEPS - 1, (STEPS - 1) % RING)
                for k, more in (("projected", 4), ("turned", 5), ("onehot_t", 5), ("onehot", AHEAD), ("seg_out", 2),
                                ("score_t", 3), ("scan_back", 2)):
                    dve.wait_ge(S[k], STEPS + more)
                finish(S)

                av = agg[:, 0:TILES * HC].rearrange("p (t h c) -> p t h c", h=H, c=C + 1)
                for p, cs, ts in pieces(f"gat {l} norm stats"):
                    at = slice(ts.start, ts.stop)
                    rd = rden[:, at, 0:H]
                    link(dve.tensor_scalar(rd, av[:, at, :, C], 1e-30, None, ALU.max))
                    link(dve.reciprocal(rd, rd))
                    for h in range(H):
                        ins = dve.tensor_tensor(tiled(w1[:, cs])[:, :, h * C:(h + 1) * C], av[:, at, h, 0:C],
                                                rden[:, at, h:h + 1].to_broadcast([P, len(ts), C]), ALU.mult)
                    link(ins)
                    link(dve.tensor_tensor(tiled(w1[:, cs]), tiled(w1[:, cs]), per_row(f"L3_gnn_b{l}", len(ts)), ALU.add))
                    row_stats(p, ts, w1)
                norm_out(f"gat {l} norm out", w1, w1)
            for p, cs, ts in pieces("gat 2 affine"):
                link(dve.tensor_tensor(tiled(w1[:, cs]), tiled(w1[:, cs]), per_row("L3_gnn_g2", len(ts)), ALU.mult))
                dve.tensor_tensor(tiled(w1[:, cs]), tiled(w1[:, cs]), per_row("L3_gnn_be2", len(ts)),
                                  ALU.add).then_inc(piece[p], 1)
            for p, cs, ts in pieces("last norm stats"):
                link(dve.tensor_tensor(w1[:, cs], w1[:, cs], res[:, cs], ALU.add))
                row_stats(p, ts, w1)
            norm_out("last norm out", res, w1)


def kernel(**inputs):
    import numpy as np
    import concourse.bacc as bacc
    from concourse.bass_utils import run_bass_kernel_spmd

    inp = {k: np.asarray(v) for k, v in inputs.items()}
    host = {}

    def pad(v, n, fill):
        return np.concatenate([v, np.full((n - len(v),) + v.shape[1:], fill, v.dtype)])

    def columns(v):
        return v.reshape(CHUNKS, P).T

    dst = pad(inp["dst"], EP + 1, 1 << 20)
    host["x"] = pad(inp["x"], NP, 0)
    host["src_cols"] = columns(pad(inp["src"], EP, 0))
    host["dst_cols"] = columns(dst[:EP])
    host["next_cols"] = columns(dst[1:])
    host["type_cols"] = columns(pad(inp["edge_type_9"], EP, 0))
    host["dst_rows"] = dst[:EP].reshape(CHUNKS, P)
    host["dst_ends"] = dst[GE - 1:EP:GE].reshape(1, GROUPS)
    host["ea16"] = pad(inp["edge_attr_16"], EP, 0).reshape(CHUNKS, P, 16).transpose(0, 2, 1).reshape(CHUNKS * 16, P)
    host["ea32"] = pad(inp["edge_attr_32"], EP, 0).reshape(CHUNKS, P, 32).transpose(0, 2, 1).reshape(CHUNKS * 32, P)
    for k in ("L0_gnn_Wl1", "L0_gnn_Wr1", "L0_gnn_Wl2", "L0_gnn_Wr2",
              *[f"L3_gnn_{v}{l}" for l in range(3) for v in ("Wl", "Wr")]):
        host[k] = inp[k]

    def blocks(w):
        b = np.zeros((CH, w.shape[0], CH, D), w.dtype)
        for c in range(CH):
            b[c, :, c] = w
        return b.reshape(-1, CH * D)

    for l in range(3):
        host[f"L3_gnn_We{l}"] = blocks(inp[f"L3_gnn_We{l}"])
    for k in ("L1_gnn_W_msg", "L1_gnn_W_ih", "L1_gnn_W_hh"):
        host[k] = inp[k].T
    host["L1_aug"] = np.concatenate([inp["L1_gnn_edge_embed"], inp["L1_gnn_b_msg"][None]])
    host["L2_conv_edge"] = np.concatenate([np.concatenate([blocks(inp["L2_gnn_conv_edge_w"][l]),
                                                           np.tile(inp["L2_gnn_conv_edge_b"][l], CH)[None]])
                                           for l in range(3)], 1)
    for k in ("L2_gnn_conv_w1", "L2_gnn_vn_w1"):
        host[k] = inp[k].transpose(1, 0, 2).reshape(D, -1)
    for k in ("L2_gnn_conv_w2", "L2_gnn_vn_w2"):
        host[k] = inp[k].reshape(-1, 2, D, D).transpose(2, 0, 1, 3).reshape(D, -1)
    for k in VEC_COLS:
        host["col_" + k] = inp[k].reshape(-1, D).T
    for k in VEC_ROWS:
        host[k] = inp[k].reshape(1, -1)

    nc = bacc.Bacc("TRN2", target_bir_lowering=False, num_devices=1)
    arrays, args = {}, {}
    for name, v in host.items():
        v = np.ascontiguousarray(v)
        arrays[f"in_{name}"] = v
        args[name] = nc.dram_tensor(f"in_{name}", v.shape, mybir.dt.from_np(v.dtype), kind="ExternalInput").ap()
    out = nc.dram_tensor("out", (N, D), F32, kind="ExternalOutput").ap()
    build(nc, args, out)
    r = run_bass_kernel_spmd(nc, [arrays], core_ids=[0])
    return r.results[0]["out"]
```
